# Optimizing a Trainium2 kernel written in Bass

```python
import numpy as np
import jax
import jax.numpy as jnp

def _softmax(x, axis=-1):
    return jax.nn.softmax(x, axis=axis)

def _gelu(x):
    return jax.nn.gelu(x, approximate=True)

def _silu(x):
    return jax.nn.silu(x)

def _sigmoid(x):
    return jax.nn.sigmoid(x)

def _layernorm(x, axis=-1, eps=1e-05):
    m = jnp.mean(x, axis=axis, keepdims=True)
    v = jnp.var(x, axis=axis, keepdims=True)
    return (x - m) / jnp.sqrt(v + eps)

def _scatter_add(tgt, idx, src, axis=0):
    return tgt.at[idx].add(src)

def _segment_sum(src, seg, n):
    return jax.ops.segment_sum(src, seg, n)
kernel_name = 'mk_vit_tower_d2_tok_img1024_r4_daf3ff'

def setup_inputs(seed: int=0):
    np.random.seed(seed)
    _w = jnp.asarray

    def _rec_inputs():
        import jax
        import jax.numpy as jnp
        _rk = jax.random.key(seed)
        x = -0.00016672 + 0.999947 * jax.random.normal(jax.random.fold_in(_rk, 1), (32, 3, 96, 96), jnp.float32)
        return x
    x = _rec_inputs()

    def _L0_tok_setup():
        import jax, jax.numpy as jnp
        import numpy as np
        B, C, H, W = (64, 3, 96, 96)
        P = 16
        NP = H // P * (W // P)
        PD = C * P * P
        ED = 256
        NCLS = 1

        def _layernorm(x, g, b, eps=1e-05):
            mu = jnp.mean(x, axis=-1, keepdims=True)
            var = jnp.mean(jnp.square(x - mu), axis=-1, keepdims=True)
            return (x - mu) * jax.lax.rsqrt(var + eps) * g + b
        key = jax.random.key(seed)
        ks = jax.random.split(key, 8)
        x = jax.random.normal(ks[0], (B, C, H, W), dtype=jnp.float32)
        ln1_g = jnp.ones((PD,), jnp.float32)
        ln1_b = jnp.zeros((PD,), jnp.float32)
        W_proj = jax.random.normal(ks[1], (PD, ED), jnp.float32) / np.sqrt(PD)
        b_proj = jnp.zeros((ED,), jnp.float32)
        ln2_g = jnp.ones((ED,), jnp.float32)
        ln2_b = jnp.zeros((ED,), jnp.float32)
        cls_token = jax.random.normal(ks[2], (1, NCLS, ED), jnp.float32)
        pos_emb = jax.random.normal(ks[3], (1, NP + NCLS, ED), jnp.float32)
        return {'x': x, 'ln1_g': ln1_g, 'ln1_b': ln1_b, 'W_proj': W_proj, 'b_proj': b_proj, 'ln2_g': ln2_g, 'ln2_b': ln2_b, 'cls_token': cls_token, 'pos_emb': pos_emb}
    _L0_tok_all = _L0_tok_setup()
    _L0_tok_in = {k: v for k, v in _L0_tok_all.items() if k in ('ln1_g', 'ln1_b', 'W_proj', 'b_proj', 'ln2_g', 'ln2_b', 'cls_token', 'pos_emb')}
    del _L0_tok_all

    def _L0_attn_setup():
        import jax, jax.numpy as jnp
        import numpy as np
        NUM_HEADS = 16
        DEPTH = 0

        def rotate_half(x):
            x1, x2 = jnp.split(x, 2, axis=-1)
            return jnp.concatenate((-x2, x1), axis=-1)

        def rotary_tables(seq_len, rot_dim, dtype):
            inv_freq = 1.0 / 10000.0 ** (jnp.arange(0, rot_dim, 2, dtype=jnp.float32) / rot_dim)
            freqs = jnp.arange(seq_len, dtype=jnp.float32)[:, None] * inv_freq[None, :]
            emb = jnp.concatenate((freqs, freqs), axis=-1)
            return (emb.astype(dtype), jnp.cos(emb).astype(dtype), jnp.sin(emb).astype(dtype))
        key = jax.random.key(seed)
        ks = jax.random.split(key, 7)
        B, N, C = (1, 512, 256)
        hd = C // NUM_HEADS
        std_qkv = (1.0 / C) ** 0.5
        std_proj = (1.0 / (2 * C)) ** 0.5
        return {'x': jax.random.normal(ks[0], (B, N, C), dtype=jnp.float32), 'W_qkv': jax.random.normal(ks[1], (6 * C, C), dtype=jnp.float32) * std_qkv, 'W_proj': jax.random.normal(ks[2], (C, 2 * C), dtype=jnp.float32) * std_proj, 'lambda_q1': jax.random.normal(ks[3], (hd,), dtype=jnp.float32) * 0.1, 'lambda_q2': jax.random.normal(ks[4], (hd,), dtype=jnp.float32) * 0.1, 'lambda_k1': jax.random.normal(ks[5], (hd,), dtype=jnp.float32) * 0.1, 'lambda_k2': jax.random.normal(ks[6], (hd,), dtype=jnp.float32) * 0.1}
    _L0_attn_all = _L0_attn_setup()
    _L0_attn_in = {k: v for k, v in _L0_attn_all.items() if k in ('W_qkv', 'W_proj', 'lambda_q1', 'lambda_q2', 'lambda_k1', 'lambda_k2')}
    del _L0_attn_all

    def _L0_ffn_setup():
        import jax, jax.numpy as jnp
        import numpy as np
        BLOCK = 32
        W_BITS = 4
        ACT_BITS = 16

        def act_qdq(x):
            qmax = 2.0 ** (ACT_BITS - 1) - 1.0
            scale = jnp.maximum(jnp.max(jnp.abs(x)) / qmax, 1e-12)
            return jnp.clip(jnp.round(x / scale), -qmax - 1.0, qmax) * scale

        def fixed_qdq_u16(x):
            scale = 1.0 / 65536.0
            return jnp.clip(jnp.round(x / scale), 0.0, 65535.0) * scale

        def lpbq_dequant(w):
            O, I = w.shape
            qmax = 2.0 ** (W_BITS - 1) - 1.0
            wb = w.reshape(O, I // BLOCK, BLOCK)
            s = jnp.maximum(jnp.max(jnp.abs(wb), axis=-1, keepdims=True) / qmax, 1e-12)
            wq = jnp.clip(jnp.round(wb / s), -qmax - 1.0, qmax) * s
            return wq.reshape(O, I)
        key = jax.random.key(seed)
        k1, k2, k3, k4 = jax.random.split(key, 4)
        B, S, H, I = (2, 1024, 256, 768)
        x = jax.random.normal(k1, (B, S, H), jnp.float32)
        w_gate = jax.random.normal(k2, (I, H), jnp.float32) * 0.02
        w_up = jax.random.normal(k3, (I, H), jnp.float32) * 0.02
        w_down = jax.random.normal(k4, (H, I), jnp.float32) * 0.02
        return {'x': x, 'w_gate': w_gate, 'w_up': w_up, 'w_down': w_down}
    _L0_ffn_all = _L0_ffn_setup()
    _L0_ffn_in = {k: v for k, v in _L0_ffn_all.items() if k in ('w_gate', 'w_up', 'w_down')}
    del _L0_ffn_all

    def _L1_attn_setup():
        import jax, jax.numpy as jnp
        import numpy as np
        NUM_HEADS = 16
        EPS = 1e-12

        def _l2norm(t):
            n = jnp.sqrt(jnp.sum(t * t, axis=-1, keepdims=True))
            return t / jnp.maximum(n, EPS)
        key = jax.random.key(seed)
        kx, kq, kk, kv = jax.random.split(key, 4)
        B, S, E = (2, 512, 256)
        head_dim = E // NUM_HEADS
        bound = 1.0 / np.sqrt(E)
        x = jax.random.normal(kx, (B, S, E), dtype=jnp.float32)
        Wq = jax.random.uniform(kq, (E, E), dtype=jnp.float32, minval=-bound, maxval=bound)
        Wk = jax.random.uniform(kk, (E, E), dtype=jnp.float32, minval=-bound, maxval=bound)
        Wv = jax.random.uniform(kv, (E, E), dtype=jnp.float32, minval=-bound, maxval=bound)
        g_scale = jnp.asarray(np.sqrt(head_dim), dtype=jnp.float32)
        return {'x': x, 'Wq': Wq, 'Wk': Wk, 'Wv': Wv, 'g_scale': g_scale}
    _L1_attn_all = _L1_attn_setup()
    _L1_attn_in = {k: v for k, v in _L1_attn_all.items() if k in ('Wq', 'Wk', 'Wv', 'g_scale')}
    del _L1_attn_all

    def _L1_ffn_setup():
        import jax, jax.numpy as jnp
        import numpy as np
        D_MODEL = 256
        DEPTH = 8
        M = 2 ** DEPTH
        N_INTERNAL = M - 1
        B, T = (8, 1024)

        def _leaf_probs(gate):
            BT = gate.shape[0]
            lp = jnp.ones((BT, M), dtype=gate.dtype)
            for level in range(DEPTH):
                n = 2 ** level
                half = M // (2 * n)
                g = gate[:, n - 1:2 * n - 1]
                f = jnp.stack([1.0 - g, g], axis=-1)
                f = jnp.broadcast_to(f[..., None], (BT, n, 2, half))
                lp = lp * f.reshape(BT, M)
            return lp
        key = jax.random.key(seed)
        ks = jax.random.split(key, 7)
        x = jax.random.normal(ks[0], (B, T, D_MODEL), dtype=jnp.float32)
        Wq = jax.random.normal(ks[1], (D_MODEL, D_MODEL), dtype=jnp.float32) * 0.02
        routers = jax.random.normal(ks[2], (N_INTERNAL, D_MODEL), dtype=jnp.float32) * 0.02
        leaf_keys = jax.random.normal(ks[3], (M, D_MODEL), dtype=jnp.float32) * 0.02
        leaf_values = jax.random.normal(ks[4], (M, D_MODEL), dtype=jnp.float32) * 0.02
        Wout_w = jax.random.normal(ks[5], (D_MODEL, D_MODEL), dtype=jnp.float32) * 0.02
        Wout_b = jax.random.normal(ks[6], (D_MODEL,), dtype=jnp.float32) * 0.02
        return {'x': x, 'Wq': Wq, 'routers': routers, 'leaf_keys': leaf_keys, 'leaf_values': leaf_values, 'Wout_w': Wout_w, 'Wout_b': Wout_b}
    _L1_ffn_all = _L1_ffn_setup()
    _L1_ffn_in = {k: v for k, v in _L1_ffn_all.items() if k in ('Wq', 'routers', 'leaf_keys', 'leaf_values', 'Wout_w', 'Wout_b')}
    del _L1_ffn_all
    return {'x': x, 'L0_tok_ln1_g': _L0_tok_in['ln1_g'], 'L0_tok_ln1_b': _L0_tok_in['ln1_b'], 'L0_tok_W_proj': _L0_tok_in['W_proj'], 'L0_tok_b_proj': _L0_tok_in['b_proj'], 'L0_tok_ln2_g': _L0_tok_in['ln2_g'], 'L0_tok_ln2_b': _L0_tok_in['ln2_b'], 'L0_tok_cls_token': _L0_tok_in['cls_token'], 'L0_tok_pos_emb': _L0_tok_in['pos_emb'], 'L0_attn_W_qkv': _L0_attn_in['W_qkv'], 'L0_attn_W_proj': _L0_attn_in['W_proj'], 'L0_attn_lambda_q1': _L0_attn_in['lambda_q1'], 'L0_attn_lambda_q2': _L0_attn_in['lambda_q2'], 'L0_attn_lambda_k1': _L0_attn_in['lambda_k1'], 'L0_attn_lambda_k2': _L0_attn_in['lambda_k2'], 'L0_ffn_w_gate': _L0_ffn_in['w_gate'], 'L0_ffn_w_up': _L0_ffn_in['w_up'], 'L0_ffn_w_down': _L0_ffn_in['w_down'], 'L1_attn_Wq': _L1_attn_in['Wq'], 'L1_attn_Wk': _L1_attn_in['Wk'], 'L1_attn_Wv': _L1_attn_in['Wv'], 'L1_attn_g_scale': _L1_attn_in['g_scale'], 'L1_ffn_Wq': _L1_ffn_in['Wq'], 'L1_ffn_routers': _L1_ffn_in['routers'], 'L1_ffn_leaf_keys': _L1_ffn_in['leaf_keys'], 'L1_ffn_leaf_values': _L1_ffn_in['leaf_values'], 'L1_ffn_Wout_w': _L1_ffn_in['Wout_w'], 'L1_ffn_Wout_b': _L1_ffn_in['Wout_b']}

def reference(x, L0_tok_ln1_g, L0_tok_ln1_b, L0_tok_W_proj, L0_tok_b_proj, L0_tok_ln2_g, L0_tok_ln2_b, L0_tok_cls_token, L0_tok_pos_emb, L0_attn_W_qkv, L0_attn_W_proj, L0_attn_lambda_q1, L0_attn_lambda_q2, L0_attn_lambda_k1, L0_attn_lambda_k2, L0_ffn_w_gate, L0_ffn_w_up, L0_ffn_w_down, L1_attn_Wq, L1_attn_Wk, L1_attn_Wv, L1_attn_g_scale, L1_ffn_Wq, L1_ffn_routers, L1_ffn_leaf_keys, L1_ffn_leaf_values, L1_ffn_Wout_w, L1_ffn_Wout_b):
    import jax
    import jax.numpy as jnp

    def _L0_tok_ref(x, ln1_g, ln1_b, W_proj, b_proj, ln2_g, ln2_b, cls_token, pos_emb):
        import jax, jax.numpy as jnp
        import numpy as np
        B, C, H, W = (64, 3, 96, 96)
        P = 16
        NP = H // P * (W // P)
        PD = C * P * P
        ED = 256
        NCLS = 1

        def _layernorm(x, g, b, eps=1e-05):
            mu = jnp.mean(x, axis=-1, keepdims=True)
            var = jnp.mean(jnp.square(x - mu), axis=-1, keepdims=True)
            return (x - mu) * jax.lax.rsqrt(var + eps) * g + b
        b = x.shape[0]
        h, w = (H // P, W // P)
        patches = x.reshape(b, C, h, P, w, P)
        patches = patches.transpose(0, 2, 4, 3, 5, 1).reshape(b, h * w, P * P * C)
        z = _layernorm(patches, ln1_g, ln1_b)
        z = jnp.einsum('bnp,pe->bne', z, W_proj) + b_proj
        z = _layernorm(z, ln2_g, ln2_b)
        cls = jnp.broadcast_to(cls_token, (b, NCLS, ED))
        z = jnp.concatenate([cls, z], axis=1)
        z = z + pos_emb
        return z

    def _L0_attn_ref(x, W_qkv, W_proj, lambda_q1, lambda_q2, lambda_k1, lambda_k2):
        import jax, jax.numpy as jnp
        import numpy as np
        NUM_HEADS = 16
        DEPTH = 0

        def rotate_half(x):
            x1, x2 = jnp.split(x, 2, axis=-1)
            return jnp.concatenate((-x2, x1), axis=-1)

        def rotary_tables(seq_len, rot_dim, dtype):
            inv_freq = 1.0 / 10000.0 ** (jnp.arange(0, rot_dim, 2, dtype=jnp.float32) / rot_dim)
            freqs = jnp.arange(seq_len, dtype=jnp.float32)[:, None] * inv_freq[None, :]
            emb = jnp.concatenate((freqs, freqs), axis=-1)
            return (emb.astype(dtype), jnp.cos(emb).astype(dtype), jnp.sin(emb).astype(dtype))
        B, N, C = x.shape
        H = NUM_HEADS
        hd = C // H
        scale = hd ** (-0.5)
        lambda_init = 0.8 - 0.6 * np.exp(-0.3 * DEPTH)
        qkv = jnp.einsum('bnc,dc->bnd', x, W_qkv)
        qkv = qkv.reshape(B, N, 6, H, hd).transpose(2, 0, 3, 1, 4)
        q = jnp.concatenate((qkv[0], qkv[1]), axis=-1)
        k = jnp.concatenate((qkv[2], qkv[3]), axis=-1)
        v = jnp.concatenate((qkv[4], qkv[5]), axis=-1)
        _, cos, sin = rotary_tables(N, 2 * hd, x.dtype)
        q = q * cos + rotate_half(q) * sin
        k = k * cos + rotate_half(k) * sin
        q1, q2 = jnp.split(q, 2, axis=-1)
        k1, k2 = jnp.split(k, 2, axis=-1)
        attn1 = jnp.einsum('bhid,bhjd->bhij', q1, k1) * scale
        attn2 = jnp.einsum('bhid,bhjd->bhij', q2, k2) * scale
        lam1 = jnp.exp(jnp.sum(lambda_q1 * lambda_k1))
        lam2 = jnp.exp(jnp.sum(lambda_q2 * lambda_k2))
        lam = (lam1 - lam2 + lambda_init).astype(x.dtype)
        probs = jax.nn.softmax(attn1, axis=-1) - lam * jax.nn.softmax(attn2, axis=-1)
        out = jnp.einsum('bhij,bhjd->bhid', probs, v)
        out = out.transpose(0, 2, 1, 3).reshape(B, N, 2 * C)
        out = jnp.einsum('bnd,cd->bnc', out, W_proj)
        return out

    def _L0_ffn_ref(x, w_gate, w_up, w_down):
        import jax, jax.numpy as jnp
        import numpy as np
        BLOCK = 32
        W_BITS = 4
        ACT_BITS = 16

        def act_qdq(x):
            qmax = 2.0 ** (ACT_BITS - 1) - 1.0
            scale = jnp.maximum(jnp.max(jnp.abs(x)) / qmax, 1e-12)
            return jnp.clip(jnp.round(x / scale), -qmax - 1.0, qmax) * scale

        def fixed_qdq_u16(x):
            scale = 1.0 / 65536.0
            return jnp.clip(jnp.round(x / scale), 0.0, 65535.0) * scale

        def lpbq_dequant(w):
            O, I = w.shape
            qmax = 2.0 ** (W_BITS - 1) - 1.0
            wb = w.reshape(O, I // BLOCK, BLOCK)
            s = jnp.maximum(jnp.max(jnp.abs(wb), axis=-1, keepdims=True) / qmax, 1e-12)
            wq = jnp.clip(jnp.round(wb / s), -qmax - 1.0, qmax) * s
            return wq.reshape(O, I)
        x = act_qdq(x)
        up = act_qdq(x @ lpbq_dequant(w_up).T)
        gate = act_qdq(x @ lpbq_dequant(w_gate).T)
        sig = fixed_qdq_u16(jax.nn.sigmoid(gate))
        gate = act_qdq(gate * sig)
        o = act_qdq(gate * up)
        return o @ lpbq_dequant(w_down).T

    def _L1_attn_ref(x, Wq, Wk, Wv, g_scale):
        import jax, jax.numpy as jnp
        import numpy as np
        NUM_HEADS = 16
        EPS = 1e-12

        def _l2norm(t):
            n = jnp.sqrt(jnp.sum(t * t, axis=-1, keepdims=True))
            return t / jnp.maximum(n, EPS)
        B, S, E = x.shape
        H = NUM_HEADS
        D = E // H
        q = (x @ Wq.T).reshape(B, S, H, D).transpose(0, 2, 1, 3)
        k = (x @ Wk.T).reshape(B, S, H, D).transpose(0, 2, 1, 3)
        v = (x @ Wv.T).reshape(B, S, H, D).transpose(0, 2, 1, 3)
        q = _l2norm(q)
        k = _l2norm(k)
        scores = g_scale * jnp.einsum('bhqd,bhkd->bhqk', q, k)
        attn = jax.nn.softmax(scores, axis=-1)
        out = jnp.einsum('bhqk,bhkd->bhqd', attn, v)
        out = out.transpose(0, 2, 1, 3).reshape(B, S, E)
        return out

    def _L1_ffn_ref(x, Wq, routers, leaf_keys, leaf_values, Wout_w, Wout_b):
        import jax, jax.numpy as jnp
        import numpy as np
        D_MODEL = 256
        DEPTH = 8
        M = 2 ** DEPTH
        N_INTERNAL = M - 1
        B, T = (8, 1024)

        def _leaf_probs(gate):
            BT = gate.shape[0]
            lp = jnp.ones((BT, M), dtype=gate.dtype)
            for level in range(DEPTH):
                n = 2 ** level
                half = M // (2 * n)
                g = gate[:, n - 1:2 * n - 1]
                f = jnp.stack([1.0 - g, g], axis=-1)
                f = jnp.broadcast_to(f[..., None], (BT, n, 2, half))
                lp = lp * f.reshape(BT, M)
            return lp
        Bv, Tv, d = x.shape
        q = jnp.einsum('btd,ed->bte', x, Wq)
        q_flat = q.reshape(Bv * Tv, d)
        gate = jax.nn.sigmoid(q_flat @ routers.T)
        leaf_prob = _leaf_probs(gate)
        ret = (leaf_prob @ leaf_values).reshape(Bv, Tv, d)
        return jnp.einsum('btd,ed->bte', ret, Wout_w) + Wout_b
    h = _L0_tok_ref(x, L0_tok_ln1_g, L0_tok_ln1_b, L0_tok_W_proj, L0_tok_b_proj, L0_tok_ln2_g, L0_tok_ln2_b, L0_tok_cls_token, L0_tok_pos_emb)
    h = h + _L0_attn_ref(_layernorm(h, axis=-1), L0_attn_W_qkv, L0_attn_W_proj, L0_attn_lambda_q1, L0_attn_lambda_q2, L0_attn_lambda_k1, L0_attn_lambda_k2)
    h = h + _L0_ffn_ref(_layernorm(h, axis=-1), L0_ffn_w_gate, L0_ffn_w_up, L0_ffn_w_down)
    h = h + _L1_attn_ref(_layernorm(h, axis=-1), L1_attn_Wq, L1_attn_Wk, L1_attn_Wv, L1_attn_g_scale)
    h = h + _L1_ffn_ref(_layernorm(h, axis=-1), L1_ffn_Wq, L1_ffn_routers, L1_ffn_leaf_keys, L1_ffn_leaf_values, L1_ffn_Wout_w, L1_ffn_Wout_b)
    return h

_drawn_inputs = setup_inputs


def setup_inputs(seed=0):
    import zlib

    import numpy as np

    out = dict(_drawn_inputs(seed))
    spreads = {'L0_tok_ln1_g': (1.0, 0.2),
     'L0_tok_ln1_b': (0.0, 0.1),
     'L0_tok_b_proj': (0.0, 0.1),
     'L0_tok_ln2_g': (1.0, 0.2),
     'L0_tok_ln2_b': (0.0, 0.1)}
    factors = {'L0_attn_lambda_q1': 8.0,
     'L0_attn_lambda_q2': 4.691,
     'L0_attn_lambda_k1': 3.548,
     'L0_attn_lambda_k2': 3.538,
     'L0_ffn_w_gate': 2.7,
     'L1_ffn_Wq': 8.0,
     'L1_ffn_routers': 8.0,
     'L1_ffn_leaf_values': 8.0,
     'L1_ffn_Wout_w': 8.0,
     'L1_ffn_Wout_b': 4.033}
    for name, (base, spread) in spreads.items():
        noise = np.random.default_rng([zlib.crc32(name.encode()), seed]).standard_normal(out[name].shape)
        drawn = base * np.exp(spread * noise) if base else spread * noise
        out[name] = jnp.asarray(drawn.astype(out[name].dtype))
    for name, factor in factors.items():
        out[name] = (out[name] * factor).astype(out[name].dtype)
    return out
```

```python
from contextlib import ExitStack
import math

import numpy as np

import concourse.bass as bass
from concourse import mybir

F32 = mybir.dt.float32
I16 = mybir.dt.int16
U16 = mybir.dt.uint16
ALU = mybir.AluOpType
ACT = mybir.ActivationFunctionType
AX = mybir.AxisListType

P = 128
IMGS = 32
PATCH = 36
TOK = PATCH + 1
NT = IMGS * TOK
CH = 4
CI = IMGS // CH
CT = CI * TOK
CP = CI * PATCH
PAIRS = CI // 2
ED = 256
ET = ED // P
PD = 768
PT6 = PD // P
HEADS = 16
HD = 16
HT = 8
IF = 768
IT = IF // P
GAP = 64
PW = GAP + TOK
BLK = 32
LEAVES = 256
DEPTH = 8
EPS = 1e-5
L2_SCALE = 2.0 ** 16

C_ID, C_BD, C_MASK, C_COS, C_SIN, C_END = 0, 128, 256, 264, 301, 338
V_G1, V_B1, V_BP, V_G2, V_B2, V_CLS, V_WB, V_POS, V_END = 0, 6, 12, 14, 16, 18, 20, 22, 22 + 2 * TOK


def bc(ap, shape):
    return ap.to_broadcast(shape)


def program(nc, xT, wtok, vecs, lams, gsc, cst, wqkT, wvT, wprojT, w_up, w_gate, w_down,
            w1qkT, w1vT, wq1, routT, leafT, woutT, outT):
    with ExitStack() as top:
        def sb(name, shape, dt=F32):
            return top.enter_context(nc.sbuf_tensor(name, shape, dt))

        K = {}
        K["h"] = sb("h", [P, ET, NT])
        K["xn"] = sb("xn", [P, ET, NT])
        K["cst"] = sb("cst_sb", [P, C_END])
        K["vec"] = sb("vec_sb", [P, V_END])
        K["wqk"] = sb("wqk_sb", [P, ET, 4 * ED])
        K["wv"] = sb("wv_sb", [P, ET, 2 * ED])
        K["wp"] = sb("wp_sb", [P, 4, ED])
        K["w1qk"] = sb("w1qk_sb", [P, ET, 2 * ED])
        K["w1v"] = sb("w1v_sb", [P, ET, ED])
        K["wup"] = sb("wup_sb", [P, ET, IF])
        K["wgate"] = sb("wgate_sb", [P, ET, IF])
        K["wdown"] = sb("wdown_sb", [P, IT, ED])
        K["mask0"] = sb("mask0", [P, HT])
        K["mask1"] = sb("mask1", [P, HT])
        K["neglam"] = sb("neglam", [P, 2])
        K["eps"] = sb("eps", [P, 2])
        K["mean256"] = sb("mean256", [P, P])
        K["loaded"] = top.enter_context(nc.semaphore("weights_loaded"))
        K["ident"] = K["cst"][:, C_ID:C_ID + P]

        tokenizer(nc, K, xT, wtok, vecs, lams, gsc, cst, wqkT, wvT, wprojT, w_up, w_gate, w_down, w1qkT, w1vT)
        layernorm(nc, K, "ln_a")
        diff_attention(nc, K)
        layernorm(nc, K, "ln_f")
        quantised_ffn(nc, K)
        layernorm(nc, K, "ln_b")
        cosine_attention(nc, K)
        layernorm(nc, K, "ln_g")
        tree_ffn(nc, K, wq1, routT, leafT, woutT, outT)


def tokenizer(nc, K, xT, wtok, vecs, lams, gsc, cst, wqkT, wvT, wprojT, w_up, w_gate, w_down, w1qkT, w1vT):
    h, cs, vec, ident = K["h"], K["cst"], K["vec"], K["ident"]
    with ExitStack() as st:
        def sb(name, shape, dt=F32):
            return st.enter_context(nc.sbuf_tensor(name, shape, dt))

        def ps(name, shape):
            return st.enter_context(nc.psum_tensor(name, shape, F32))

        def sem(name):
            return st.enter_context(nc.semaphore(name))

        x = sb("x_sb", [P, CH, PT6, CP])
        w = sb("wtok_sb", [P, PT6, ED])
        wg = sb("wtok_g", [P, PT6, ED])
        mean768 = sb("mean768", [P, P])
        xc = sb("t_xc", [P, 2, PT6, CP])
        sq = sb("t_sq", [P, PT6, CP])
        ln1 = sb("t_ln1", [P, CP])
        rstd1 = sb("t_rstd1", [P, CP])
        zr = sb("t_zr", [P, ET, CP])
        zs = sb("t_zs", [P, ET, CP])
        xc2 = sb("t_xc2", [P, ET, CP])
        sq2 = sb("t_sq2", [P, ET, CP])
        ln2 = sb("t_ln2", [P, CP])
        rstd2 = sb("t_rstd2", [P, CP])
        z3 = sb("t_z3", [P, ET, CP])
        c0 = sb("t_c0", [P, ET])
        posb = sb("t_posb", [P, ET, TOK])
        raw = sb("raw_w", [P, 3, IT * ED])
        wint = sb("int_w", [P, IT * ED], I16)
        wdq = sb("deq_w", [P, 3, IT * ED])
        wmax = sb("wmax", [P, 3, 48])
        wsc = sb("wsc", [P, 3, 48])
        wrs = sb("wrs", [P, 3, 48])
        row = sb("row", [1, 80])
        onesr = sb("onesr", [1, P])

        p_mean = ps("p_mean", [P, 2, 512])
        p_var = ps("p_var", [P, 512])
        p_z = ps("p_z", [P, 2, 512])
        p_mu2 = ps("p_mu2", [P, 512])
        p_var2 = ps("p_var2", [P, 512])
        p_misc = ps("p_misc", [P, 512])

        small_in = sem("small_in")
        wtok_in = sem("wtok_in")
        x_in = [sem(f"x_in{c}") for c in range(CH)]
        ffw_in = sem("ffw_in")
        consts = sem("consts")
        wg_ready = sem("wg_ready")
        c0_psum = sem("c0_psum")
        row_step = sem("row_step")
        row_exp = sem("row_exp")
        row_bc = sem("row_bc")
        mean_ready = sem("mean_ready")
        xc_ready = sem("xc_ready")
        sq_ready = sem("sq_ready")
        var_ready = sem("var_ready")
        ln1_done = sem("ln1_done")
        rstd1_ready = sem("rstd1_ready")
        z_ready = sem("z_ready")
        zr_ready = sem("zr_ready")
        zs_ready = sem("zs_ready")
        mu2_ready = sem("mu2_ready")
        xc2_ready = sem("xc2_ready")
        sq2_ready = sem("sq2_ready")
        var2_ready = sem("var2_ready")
        ln2_done = sem("ln2_done")
        rstd2_ready = sem("rstd2_ready")
        z3_ready = sem("z3_ready")
        h_ready = sem("h_ready")
        deq = sem("deq")
        wt_psum = sem("wt_psum")
        wt_out = sem("wt_out")

        with nc.Block() as block:
            @block.sync
            def _(sp):
                sp.dma_start(cs[:], cst).then_inc(small_in, 16)
                sp.dma_start(vec[:], vecs).then_inc(small_in, 16)
                sp.dma_start(row[0:1, 0:64], lams).then_inc(small_in, 16)
                sp.dma_start(row[0:1, 79:80], gsc).then_inc(small_in, 16)
                sp.dma_start(x[:, 0], xT[0]).then_inc(x_in[0], 16)
                sp.dma_start(w[:], wtok).then_inc(wtok_in, 16)
                for c in range(1, CH):
                    sp.dma_start(x[:, c], xT[c]).then_inc(x_in[c], 16)
                sp.dma_start(K["wqk"][:], wqkT).then_inc(K["loaded"], 16)
                sp.dma_start(K["wv"][:], wvT).then_inc(K["loaded"], 16)
                for n, src in enumerate((w_up, w_gate, w_down)):
                    sp.dma_start(raw[:, n, :], src).then_inc(ffw_in, 16)
                sp.dma_start(K["wp"][:], wprojT).then_inc(K["loaded"], 16)
                sp.dma_start(K["w1qk"][:], w1qkT).then_inc(K["loaded"], 16)
                sp.dma_start(K["w1v"][:], w1vT).then_inc(K["loaded"], 16)

            @block.gpsimd
            def _(pool):
                nc.gpsimd.memset(mean768[:], 1.0 / PD).then_inc(consts, 1)
                nc.gpsimd.memset(K["mean256"][:], 1.0 / ED).then_inc(consts, 1)
                nc.gpsimd.memset(onesr[:], 1.0).then_inc(consts, 1)
                nc.gpsimd.memset(K["eps"][:, 0:1], EPS).then_inc(consts, 1)
                nc.gpsimd.memset(K["eps"][:, 1:2], 0.5 * math.log(L2_SCALE)).then_inc(consts, 1)

            @block.tensor
            def _(pe):
                pe.wait_ge(consts, 5)
                pe.wait_ge(small_in, 64)

                def mean(c):
                    pe.wait_ge(x_in[c], 16)
                    if c >= 2:
                        pe.wait_ge(xc_ready, c - 1)
                    for k in range(PT6):
                        last = nc.tensor.matmul(p_mean[:, c % 2, 0:CP], mean768[:], x[:, c, k, :],
                                                start=(k == 0), stop=(k == PT6 - 1))
                    last.then_inc(mean_ready, 1)

                mean(0)
                pe.wait_ge(wtok_in, 16)
                for t in range(ET):
                    for k in range(PT6):
                        last = nc.tensor.matmul(p_misc[:, t:t + 1], w[:, k, t * P:(t + 1) * P],
                                                vec[:, V_B1 + k:V_B1 + k + 1], start=(k == 0), stop=(k == PT6 - 1))
                last.then_inc(c0_psum, 1)
                pe.wait_ge(wg_ready, PT6)
                for c in range(CH + 1):
                    if c < CH:
                        pe.wait_ge(xc_ready, c + 1)
                        if c >= 1:
                            pe.wait_ge(zr_ready, c)
                        for t in range(ET):
                            for k in range(PT6):
                                last = nc.tensor.matmul(p_z[:, t, 0:CP], wg[:, k, t * P:(t + 1) * P],
                                                        xc[:, c % 2, k, :], start=(k == 0), stop=(k == PT6 - 1))
                        last.then_inc(z_ready, 1)
                    if c + 1 < CH:
                        mean(c + 1)
                    if c < CH:
                        pe.wait_ge(sq_ready, c + 1)
                        if c >= 1:
                            pe.wait_ge(ln1_done, c)
                        for k in range(PT6):
                            last = nc.tensor.matmul(p_var[:, 0:CP], mean768[:], sq[:, k, :],
                                                    start=(k == 0), stop=(k == PT6 - 1))
                        last.then_inc(var_ready, 1)
                    if c >= 1:
                        pe.wait_ge(zs_ready, 2 * c)
                        if c >= 2:
                            pe.wait_ge(xc2_ready, c - 1)
                        for k in range(ET):
                            last = nc.tensor.matmul(p_mu2[:, 0:CP], K["mean256"][:], zs[:, k, :],
                                                    start=(k == 0), stop=(k == ET - 1))
                        last.then_inc(mu2_ready, 1)
                        pe.wait_ge(sq2_ready, c)
                        if c >= 2:
                            pe.wait_ge(ln2_done, c - 1)
                        for k in range(ET):
                            last = nc.tensor.matmul(p_var2[:, 0:CP], K["mean256"][:], sq2[:, k, :],
                                                    start=(k == 0), stop=(k == ET - 1))
                        last.then_inc(var2_ready, 1)
                pe.wait_ge(row_step, 5)
                pe.wait_ge(row_step, 6)
                nc.tensor.matmul(p_mean[:, 0, 0:2], onesr[0:1, :], row[0:1, 78:80], start=True, stop=True).then_inc(row_bc, 1)
                n = 0
                for m in range(3):
                    pe.wait_ge(deq, 3 * (m + 1))
                    for q in range(3):
                        if n >= 2:
                            pe.wait_ge(wt_out, n - 1)
                        for b in range(4):
                            s = 4 * q + b
                            src = wdq[:, m, s * P:(s + 1) * P]
                            last = nc.tensor.transpose(p_z[:, n % 2, b * P:(b + 1) * P], src, ident)
                        last.then_inc(wt_psum, 1)
                        n += 1

            @block.scalar
            def _(act):
                act.wait_ge(consts, 5)
                act.wait_ge(row_step, 2)
                nc.scalar.activation(row[0:1, 70:72], row[0:1, 68:70], ACT.Exp).then_inc(row_exp, 1)

                def square(c):
                    act.wait_ge(xc_ready, c + 1)
                    nc.scalar.activation(sq[:], xc[:, c % 2], ACT.Square).then_inc(sq_ready, 1)

                square(0)
                for c in range(CH):
                    if c < CH:
                        act.wait_ge(var_ready, c + 1)
                        nc.scalar.activation(ln1[:], p_var[:, 0:CP], ACT.Ln, bias=K["eps"][:, 0:1]).then_inc(ln1_done, 1)
                        act.wait_ge(ln1_done, c + 1)
                        if c >= 1:
                            act.wait_ge(zr_ready, c)
                        nc.scalar.activation(rstd1[:], ln1[:], ACT.Exp, scale=-0.5).then_inc(rstd1_ready, 1)
                        act.wait_ge(zr_ready, c + 1)
                        if c >= 1:
                            act.wait_ge(xc2_ready, c)
                        for t in range(ET):
                            nc.scalar.activation(zs[:, t], zr[:, t], ACT.Identity, bias=c0[:, t:t + 1]).then_inc(zs_ready, 1)
                        if c + 1 < CH:
                            square(c + 1)
                        act.wait_ge(xc2_ready, c + 1)
                        nc.scalar.activation(sq2[:], xc2[:], ACT.Square).then_inc(sq2_ready, 1)
                        act.wait_ge(var2_ready, c + 1)
                        nc.scalar.activation(ln2[:], p_var2[:, 0:CP], ACT.Ln, bias=K["eps"][:, 0:1]).then_inc(ln2_done, 1)
                        act.wait_ge(ln2_done, c + 1)
                        if c >= 1:
                            act.wait_ge(z3_ready, c)
                        nc.scalar.activation(rstd2[:], ln2[:], ACT.Exp, scale=-0.5).then_inc(rstd2_ready, 1)
                dst = [K["wup"], K["wgate"], K["wdown"]]
                n = 0
                for m in range(3):
                    for q in range(3):
                        act.wait_ge(wt_psum, n + 1)
                        for b in range(4):
                            s = 4 * q + b
                            if m < 2:
                                o, i = s // ET, s % ET
                                out = dst[m][:, i, o * P:(o + 1) * P]
                            else:
                                o, i = s // IT, s % IT
                                out = dst[m][:, i, o * P:(o + 1) * P]
                            last = nc.scalar.copy(out, p_z[:, n % 2, b * P:(b + 1) * P])
                        last.then_inc(wt_out, 1)
                        n += 1

            @block.vector
            def _(dve):
                dve.wait_ge(small_in, 64)
                nc.vector.tensor_tensor(row[0:1, 0:32], row[0:1, 0:32], row[0:1, 32:64], ALU.mult).then_inc(row_step, 1)
                dve.wait_ge(row_step, 1)
                nc.vector.tensor_reduce(row[0:1, 68:70], row[0:1, 0:32].rearrange("p (a b) -> p a b", a=2),
                                        AX.X, ALU.add).then_inc(row_step, 1)
                nc.vector.tensor_tensor(posb[:], vec[:, V_POS:V_END].rearrange("p (t n) -> p t n", t=ET),
                                        bc(vec[:, V_B2:V_B2 + ET].unsqueeze(2), [P, ET, TOK]), ALU.add).then_inc(row_step, 1)
                dve.wait_ge(wtok_in, 16)
                for k in range(PT6):
                    nc.vector.tensor_scalar(wg[:, k], w[:, k], vec[:, V_G1 + k:V_G1 + k + 1], None, ALU.mult).then_inc(wg_ready, 1)
                dve.wait_ge(c0_psum, 1)
                nc.vector.tensor_tensor(c0[:], p_misc[:, 0:ET], vec[:, V_BP:V_BP + ET], ALU.add).then_inc(row_step, 1)
                hv = h[:].rearrange("p t (i n) -> p t i n", n=TOK)
                nc.vector.tensor_tensor(hv[:, :, :, 0],
                                        bc(vec[:, V_CLS:V_CLS + ET].unsqueeze(2), [P, ET, IMGS]),
                                        bc(vec[:, V_POS:V_END].rearrange("p (t n) -> p t n", t=ET)[:, :, 0:1],
                                           [P, ET, IMGS]), ALU.add).then_inc(h_ready, 1)

                def centre(c):
                    dve.wait_ge(mean_ready, c + 1)
                    if c >= 2:
                        dve.wait_ge(var_ready, c - 1)
                    nc.vector.tensor_tensor(xc[:, c % 2], x[:, c],
                                            bc(p_mean[:, c % 2, 0:CP].unsqueeze(1), [P, PT6, CP]),
                                            ALU.subtract).then_inc(xc_ready, 1)

                centre(0)
                for c in range(CH):
                    if c + 1 < CH:
                        centre(c + 1)
                    dve.wait_ge(z_ready, c + 1)
                    dve.wait_ge(rstd1_ready, c + 1)
                    if c >= 1:
                        dve.wait_ge(zs_ready, 2 * c)
                    nc.vector.tensor_tensor(zr[:], p_z[:, :, 0:CP], bc(rstd1[:].unsqueeze(1), [P, ET, CP]),
                                            ALU.mult).then_inc(zr_ready, 1)
                    dve.wait_ge(mu2_ready, c + 1)
                    if c >= 1:
                        dve.wait_ge(sq2_ready, c)
                    nc.vector.tensor_tensor(xc2[:], zs[:], bc(p_mu2[:, 0:CP].unsqueeze(1), [P, ET, CP]),
                                            ALU.subtract).then_inc(xc2_ready, 1)
                    dve.wait_ge(rstd2_ready, c + 1)
                    if c >= 1:
                        dve.wait_ge(h_ready, 2 * c + 1)
                    nc.vector.tensor_tensor(z3[:], xc2[:], bc(rstd2[:].unsqueeze(1), [P, ET, CP]),
                                            ALU.mult).then_inc(z3_ready, 1)
                    dve.wait_ge(z3_ready, c + 1)
                    for t in range(ET):
                        nc.vector.scalar_tensor_tensor(
                            out=hv[:, t, c * CI:(c + 1) * CI, 1:TOK],
                            in0=z3[:, t].rearrange("p (i n) -> p i n", n=PATCH),
                            scalar=vec[:, V_G2 + t:V_G2 + t + 1],
                            in1=bc(posb[:, t, 1:TOK].unsqueeze(1), [P, CI, PATCH]),
                            op0=ALU.mult, op1=ALU.add).then_inc(h_ready, 1)
                dve.wait_ge(row_exp, 1)
                nc.vector.tensor_tensor(row[0:1, 72:73], row[0:1, 71:72], row[0:1, 70:71], ALU.subtract).then_inc(row_step, 1)
                dve.wait_ge(row_step, 5)
                nc.vector.tensor_scalar(row[0:1, 78:79], row[0:1, 72:73], -(0.8 - 0.6 * math.exp(0.0)), None,
                                        ALU.add).then_inc(row_step, 1)
                dve.wait_ge(row_bc, 1)
                nc.vector.tensor_copy(K["neglam"][:], p_mean[:, 0, 0:2]).then_inc(row_step, 1)
                dve.wait_ge(row_step, 7)
                nc.vector.tensor_scalar(K["mask0"][:], cs[:, C_MASK:C_MASK + HT], float(HD) ** -0.5, None,
                                        ALU.mult).then_inc(row_step, 1)
                nc.vector.tensor_scalar(K["mask1"][:], cs[:, C_MASK:C_MASK + HT], K["neglam"][:, 1:2], None,
                                        ALU.mult).then_inc(row_step, 1)
                dve.wait_ge(ffw_in, 48)
                for m in range(3):
                    blocks = raw[:, m].rearrange("p (b n) -> p b n", n=BLK)
                    nc.vector.tensor_reduce(wmax[:, m], blocks, AX.X, ALU.max, apply_absolute_value=True).then_inc(wg_ready, 1)
                dve.wait_ge(wg_ready, PT6 + 3)
                nc.vector.tensor_scalar(wsc[:], wmax[:], 1.0 / 7.0, 1e-12, ALU.mult, ALU.max).then_inc(wg_ready, 1)
                dve.wait_ge(wg_ready, PT6 + 4)
                nc.vector.reciprocal(wrs[:], wsc[:]).then_inc(wg_ready, 1)
                dve.wait_ge(wg_ready, PT6 + 5)
                for m in range(3):
                    blocks = raw[:, m].rearrange("p (b n) -> p b n", n=BLK)
                    ints = wint[:].rearrange("p (b n) -> p b n", n=BLK)
                    if m:
                        dve.wait_ge(deq, 3 * m)
                    nc.vector.tensor_tensor(ints, blocks, bc(wrs[:, m].unsqueeze(2), [P, 48, BLK]), ALU.mult).then_inc(deq, 2)
                    dve.wait_ge(deq, 3 * m + 2)
                    nc.vector.tensor_tensor(wdq[:, m].rearrange("p (b n) -> p b n", n=BLK), ints,
                                            bc(wsc[:, m].unsqueeze(2), [P, 48, BLK]), ALU.mult).then_inc(deq, 1)


def layernorm(nc, K, name):
    h, xn = K["h"], K["xn"]
    with ExitStack() as st:
        def sb(n, shape, dt=F32):
            return st.enter_context(nc.sbuf_tensor(f"{name}_{n}", shape, dt))

        def sem(n):
            return st.enter_context(nc.semaphore(f"{name}_{n}"))

        xc = sb("xc", [P, CH, ET, CT])
        sq = sb("sq", [P, CH, ET, CT])
        lnv = sb("lnv", [P, CH, CT])
        rstd = sb("rstd", [P, CH, CT])
        p_mu = st.enter_context(nc.psum_tensor(f"{name}_mu", [P, CH, 512], F32))
        p_var = st.enter_context(nc.psum_tensor(f"{name}_var", [P, CH, 512], F32))
        mean_ready, centred, squared = sem("mean_ready"), sem("centred"), sem("squared")
        var_ready, logged, rstd_ready = sem("var_ready"), sem("logged"), sem("rstd_ready")
        xn_ready = sem("xn_ready")

        def cols(c):
            return slice(c * CT, (c + 1) * CT)

        with nc.Block() as block:
            @block.tensor
            def _(pe):
                for c in range(CH):
                    for k in range(ET):
                        last = nc.tensor.matmul(p_mu[:, c, 0:CT], K["mean256"][:], h[:, k, cols(c)],
                                                start=(k == 0), stop=(k == ET - 1))
                    last.then_inc(mean_ready, 1)
                for c in range(CH):
                    pe.wait_ge(squared, c + 1)
                    for k in range(ET):
                        last = nc.tensor.matmul(p_var[:, c, 0:CT], K["mean256"][:], sq[:, c, k, :],
                                                start=(k == 0), stop=(k == ET - 1))
                    last.then_inc(var_ready, 1)

            @block.vector
            def _(dve):
                for c in range(CH):
                    dve.wait_ge(mean_ready, c + 1)
                    nc.vector.tensor_tensor(xc[:, c], h[:, :, cols(c)], bc(p_mu[:, c, 0:CT].unsqueeze(1), [P, ET, CT]),
                                            ALU.subtract).then_inc(centred, 1)
                for c in range(CH):
                    dve.wait_ge(rstd_ready, c + 1)
                    nc.vector.tensor_tensor(xn[:, :, cols(c)], xc[:, c], bc(rstd[:, c].unsqueeze(1), [P, ET, CT]),
                                            ALU.mult).then_inc(xn_ready, 1)

            @block.scalar
            def _(act):
                for c in range(CH):
                    act.wait_ge(centred, c + 1)
                    nc.scalar.activation(sq[:, c], xc[:, c], ACT.Square).then_inc(squared, 1)
                for c in range(CH):
                    act.wait_ge(var_ready, c + 1)
                    nc.scalar.activation(lnv[:, c], p_var[:, c, 0:CT], ACT.Ln, bias=K["eps"][:, 0:1]).then_inc(logged, 1)
                    act.wait_ge(logged, c + 1)
                    nc.scalar.activation(rstd[:, c], lnv[:, c], ACT.Exp, scale=-0.5).then_inc(rstd_ready, 1)


def diff_attention(nc, K):
    h, xn, cs, ident = K["h"], K["xn"], K["cst"], K["ident"]
    NU = ET * PAIRS
    BW = HT * TOK
    with ExitStack() as st:
        def sb(n, shape, dt=F32):
            return st.enter_context(nc.sbuf_tensor(f"da_{n}", shape, dt))

        def ps(n, shape):
            return st.enter_context(nc.psum_tensor(f"da_{n}", shape, F32))

        def sem(n):
            return st.enter_context(nc.semaphore(f"da_{n}"))

        xg = sb("xg", [P, ET, CI, GAP])
        cos_t = sb("cost", [P, 2, 2, CT])
        sin_t = sb("sint", [P, 2, 2, CT])
        qr = sb("qr", [P, ET, 2, CT])
        kr = sb("kr", [P, ET, 2, CT])
        kx = sb("kx", [P, ET, 2, CI, HT, TOK])
        vt = sb("vt", [P, PAIRS, 512])
        vx = sb("vx", [P, CI, 2, HT * 32])
        ex = sb("ex", [P, 4, 2 * HT, TOK])
        pr = sb("pr", [P, 2, HT, GAP])
        pts = sb("pts", [P, 2, 4 * PW])
        ot = sb("ot", [P, 4, CT])
        mx = sb("mx", [P, 2, 2 * HT])
        sm = sb("sm", [P, 2, 2 * HT])
        rc = sb("rc", [P, 4, 2 * HT])

        p_s = ps("p_s", [P, 2, 2, 512])
        p_t = ps("p_t", [P, 512])
        p_o = ps("p_o", [P, 512])
        p_v = ps("p_v", [P, 2, 512])

        init = sem("init")
        xg_ready = sem("xg_ready")
        qk_ready = sem("qk_ready")
        rot_ready = sem("rot_ready")
        rot_used = sem("rot_used")
        kx_dve = sem("kx_dve")
        kx_act = sem("kx_act")
        v_ready = sem("v_ready")
        vt_ready = sem("vt_ready")
        vx_ready = sem("vx_ready")
        s_ready = sem("s_ready")
        max_ready = sem("max_ready")
        sub_ready = sem("sub_ready")
        exp_ready = sem("exp_ready")
        sum_ready = sem("sum_ready")
        inv_ready = sem("inv_ready")
        rc_ready = sem("rc_ready")
        norm_ready = sem("norm_ready")
        p_ready = sem("p_ready")
        pt_ready = sem("pt_ready")
        pts_ready = sem("pts_ready")
        pv_ready = sem("pv_ready")
        ot_ready = sem("ot_ready")
        y_ready = sem("y_ready")
        h_done = sem("h_done")

        JOBS = [("k", 0), ("q", 0), ("k", 1), ("q", 1)]

        with nc.Block() as block:
            @block.gpsimd
            def _(pool):
                for s in (sub_ready, rot_used, v_ready, vx_ready, pv_ready, h_done, pts_ready, ot_ready, pt_ready, p_ready, y_ready):
                    pool.sem_inc(s, 1)
                nc.gpsimd.memset(vx[:], 0.0).then_inc(init, 1)
                nc.gpsimd.memset(pr[:], 0.0).then_inc(init, 1)
                nc.gpsimd.memset(xg[:], 0.0).then_inc(init, 1)
                pool.wait_ge(init, 3)
                with pool.Fori(0, CH) as i:
                    for j, (which, t) in enumerate(JOBS):
                        dst = kr if which == "k" else qr
                        pool.wait_ge(rot_ready, i * 8 + 2 * j + 2)
                        nc.gpsimd.tensor_tensor(dst[:, t, 0], cos_t[:, j % 2, 0], sin_t[:, j % 2, 1],
                                                ALU.subtract).then_inc(rot_used, 1)
                        nc.gpsimd.tensor_tensor(dst[:, t, 1], cos_t[:, j % 2, 1], sin_t[:, j % 2, 0],
                                                ALU.add).then_inc(rot_used, 1)
                    for u in range(NU):
                        e = ex[0:PW, u % 4]
                        pool.wait_ge(rc_ready, i * NU + u + 1)
                        nc.gpsimd.tensor_tensor(e, e, bc(rc[0:PW, u % 4].unsqueeze(2), [PW, 2 * HT, TOK]),
                                                ALU.mult).then_inc(norm_ready, 1)
                        pool.wait_ge(norm_ready, i * NU + u + 1)
                        pool.wait_ge(pt_ready, i * NU + u + 1)
                        nc.gpsimd.tensor_tensor(pr[0:PW, u % 2, :, 0:TOK], e[:, 0:HT], e[:, HT:2 * HT],
                                                ALU.add).then_inc(p_ready, 1)

            @block.sync
            def _(sp):
                sp.wait_ge(init, 3)
                with sp.Fori(0, CH) as i:
                    for p in range(PAIRS):
                        sp.wait_ge(vt_ready, i * PAIRS + p + 1)
                        for m in range(2):
                            for par in range(2):
                                sp.dma_start(vx[GAP * par:GAP * par + TOK, 2 * p + m, par, :],
                                             vt[GAP * m:GAP * m + TOK, p, par * 256:(par + 1) * 256]).then_inc(vx_ready, 16)

            @block.tensor
            def _(pe):
                pe.wait_ge(K["loaded"], 80)
                pe.wait_ge(init, 3)
                with pe.Fori(0, CH) as i:
                    tok = bass.ds(i * CT, CT)
                    for j, (which, t) in enumerate(JOBS):
                        if j < 2:
                            pe.wait_ge(sub_ready, i * NU + 1)
                        else:
                            pe.wait_ge(rot_ready, i * 8 + 2 * (j - 2) + 2)
                        for half in range(2):
                            o = (2 * ED if which == "k" else 0) + half * ED + t * P
                            for k in range(ET):
                                last = nc.tensor.matmul(p_s[:, j % 2, half, 0:CT], K["wqk"][:, k, o:o + P],
                                                        xn[:, k, tok], start=(k == 0), stop=(k == ET - 1))
                        last.then_inc(qk_ready, 1)
                    pe.wait_ge(xg_ready, i + 1)
                    pe.wait_ge(h_done, i + 1)
                    for p in range(PAIRS):
                        if p >= 2:
                            pe.wait_ge(vt_ready, i * PAIRS + p - 1)
                        for k in range(ET):
                            both = xg[:, k, 2 * p:2 * p + 2, :].rearrange("p a b -> p (a b)")
                            last = nc.tensor.matmul(p_v[0:PW, p % 2, :], both[:, 0:PW], K["wv"][:, k, :],
                                                    start=(k == 0), stop=(k == ET - 1))
                        last.then_inc(v_ready, 1)
                    for s in range(NU + 2):
                        if s < NU:
                            t, p = s // PAIRS, s % PAIRS
                            if s < 2:
                                pe.wait_ge(rot_ready, i * 8 + 2 * (s + 2) + 2)
                            else:
                                pe.wait_ge(sub_ready, i * NU + s - 1 + 1)
                            if p == 0:
                                pe.wait_ge(kx_dve, i * ET + t + 1)
                                pe.wait_ge(kx_act, i * ET + t + 1)
                                pe.wait_ge(rot_used, i * 8 + 4 * t + 4 + 1)
                            for m in range(2):
                                img = 2 * p + m
                                for half in range(2):
                                    last = nc.tensor.matmul(
                                        p_s[GAP * m:GAP * m + TOK, s % 2, half, 0:BW],
                                        qr[:, t, half, img * TOK:(img + 1) * TOK],
                                        kx[:, t, half, img].rearrange("p a b -> p (a b)"), start=True, stop=True)
                            last.then_inc(s_ready, 1)
                        if 1 <= s <= NU:
                            u = s - 1
                            pe.wait_ge(p_ready, i * NU + u + 2)
                            pe.wait_ge(pts_ready, i * NU + u + 1)
                            for hp in range(4):
                                src = pr[0:PW, u % 2, 2 * hp:2 * hp + 2, :].rearrange("p a b -> p (a b)")
                                last = nc.tensor.transpose(p_t[0:PW, hp * PW:(hp + 1) * PW], src[:, 0:PW],
                                                           ident[0:PW, 0:PW])
                            last.then_inc(pt_ready, 1)
                        if s >= 2:
                            u = s - 2
                            t, p = u // PAIRS, u % PAIRS
                            if u == 0:
                                pe.wait_ge(vx_ready, (i + 1) * (PAIRS * 4 * 16) + 1)
                            pe.wait_ge(pts_ready, i * NU + u + 2)
                            pe.wait_ge(ot_ready, i * NU + u + 1)
                            for m in range(2):
                                for hl in range(HT):
                                    hg = t * HT + hl
                                    last = nc.tensor.matmul(
                                        p_o[32 * (hl % 4):32 * (hl % 4) + 32,
                                            (hl // 4) * 2 * TOK + m * TOK:(hl // 4) * 2 * TOK + (m + 1) * TOK],
                                        vx[0:PW, 2 * p + m, hl % 2, (hg // 2) * 32:(hg // 2 + 1) * 32],
                                        pts[0:PW, u % 2, (hl // 2) * PW + GAP * m:(hl // 2) * PW + GAP * m + TOK],
                                        start=True, stop=True)
                            last.then_inc(pv_ready, 1)
                    pe.wait_ge(ot_ready, i * NU + NU + 1)
                    for t in range(ET):
                        for k in range(4):
                            last = nc.tensor.matmul(p_v[:, t, 0:CT], K["wp"][:, k, t * P:(t + 1) * P],
                                                    ot[:, k, :], start=(k == 0), stop=(k == 3))
                    last.then_inc(y_ready, 1)

            @block.scalar
            def _(act):
                act.wait_ge(init, 3)
                with act.Fori(0, CH) as i:
                    act.wait_ge(v_ready, i * PAIRS + 1)
                    nc.scalar.copy(xg[:, :, :, 0:TOK],
                                   xn[:, :, bass.ds(i * CT, CT)].rearrange("p t (a b) -> p t a b", b=TOK)).then_inc(xg_ready, 1)

                    def expand(t):
                        act.wait_ge(rot_used, i * 8 + 4 * t + 2 + 1)
                        for half in range(2):
                            for hh in range(4, HT):
                                last = nc.scalar.activation(
                                    kx[:, t, half, :, hh, :], kr[:, t, half].rearrange("p (a b) -> p a b", b=TOK),
                                    ACT.Copy, scale=K["mask0"][:, hh:hh + 1])
                        last.then_inc(kx_act, 1)

                    expand(0)
                    expand(1)
                    act.wait_ge(vx_ready, i * (PAIRS * 4 * 16) + 1)
                    act.wait_ge(pv_ready, i * NU + 1)
                    for p in range(PAIRS):
                        act.wait_ge(v_ready, i * PAIRS + p + 2)
                        nc.scalar.copy(vt[0:PW, p, :], p_v[0:PW, p % 2, :]).then_inc(vt_ready, 1)
                    for s in range(NU + 2):
                        if s < NU:
                            act.wait_ge(sub_ready, i * NU + s + 2)
                            nc.scalar.activation(ex[0:PW, s % 4], ex[0:PW, s % 4], ACT.Exp).then_inc(exp_ready, 1)
                        if 1 <= s <= NU:
                            u = s - 1
                            act.wait_ge(pt_ready, i * NU + u + 2)
                            nc.scalar.copy(pts[0:PW, u % 2], p_t[0:PW, 0:4 * PW]).then_inc(pts_ready, 1)
                        if s >= 2:
                            u = s - 2
                            t, p = u // PAIRS, u % PAIRS
                            act.wait_ge(pv_ready, i * NU + u + 2)
                            act.wait_ge(y_ready, i + 1)
                            nc.scalar.copy(ot[:, 2 * t:2 * t + 2, p * 2 * TOK:(p + 1) * 2 * TOK],
                                           p_o[:, 0:4 * TOK].rearrange("p (a b) -> p a b", a=2)).then_inc(ot_ready, 1)

            @block.vector
            def _(dve):
                with dve.Fori(0, CH) as i:
                    def rotate(j):
                        dve.wait_ge(qk_ready, i * 4 + j + 1)
                        dve.wait_ge(rot_used, i * 8 + (2 * j - 2 if j >= 2 else 0) + 1)
                        for n, (dst, col) in enumerate(((cos_t, C_COS), (sin_t, C_SIN))):
                            table = cs[:, col:col + TOK].unsqueeze(1)
                            for half in range(2):
                                last = nc.vector.tensor_tensor(
                                    dst[:, j % 2, half].rearrange("p (a b) -> p a b", b=TOK),
                                    p_s[:, j % 2, half, 0:CT].rearrange("p (a b) -> p a b", b=TOK),
                                    bc(table, [P, CI, TOK]), ALU.mult)
                            last.then_inc(rot_ready, 1)

                    def expand(t):
                        dve.wait_ge(rot_used, i * 8 + 4 * t + 2 + 1)
                        for half in range(2):
                            for hh in range(4):
                                last = nc.vector.tensor_scalar(
                                    kx[:, t, half, :, hh, :], kr[:, t, half].rearrange("p (a b) -> p a b", b=TOK),
                                    K["mask0"][:, hh:hh + 1], None, ALU.mult)
                        last.then_inc(kx_dve, 1)

                    rotate(0)
                    rotate(1)
                    expand(0)
                    rotate(2)
                    rotate(3)
                    expand(1)
                    for s in range(NU + 1):
                        if s < NU:
                            dve.wait_ge(s_ready, i * NU + s + 1)
                            sc = p_s[0:PW, s % 2, :, 0:BW].rearrange("p a (b c) -> p a b c", c=TOK)
                            nc.vector.tensor_reduce(mx[0:PW, s % 2].rearrange("p (a b) -> p a b", a=2), sc,
                                                    AX.X, ALU.max).then_inc(max_ready, 1)
                            dve.wait_ge(max_ready, i * NU + s + 1)
                            dve.wait_ge(p_ready, i * NU + max(s - 3, 0) + 1)
                            nc.vector.tensor_tensor(
                                ex[0:PW, s % 4].rearrange("p (a b) c -> p a b c", a=2), sc,
                                bc(mx[0:PW, s % 2].rearrange("p (a b) -> p a b", a=2).unsqueeze(3), [PW, 2, HT, TOK]),
                                ALU.subtract).then_inc(sub_ready, 1)
                        if s >= 1:
                            u = s - 1
                            dve.wait_ge(exp_ready, i * NU + u + 1)
                            nc.vector.tensor_reduce(sm[0:PW, u % 2], ex[0:PW, u % 4], AX.X, ALU.add).then_inc(sum_ready, 1)
                            dve.wait_ge(sum_ready, i * NU + u + 1)
                            nc.vector.reciprocal(rc[0:PW, u % 4], sm[0:PW, u % 2]).then_inc(inv_ready, 1)
                            dve.wait_ge(inv_ready, i * NU + u + 1)
                            nc.vector.tensor_scalar(rc[0:PW, u % 4, HT:2 * HT], rc[0:PW, u % 4, HT:2 * HT],
                                                    K["neglam"][0:PW, 0:1], None, ALU.mult).then_inc(rc_ready, 1)
                    dve.wait_ge(y_ready, i + 2)
                    tok = bass.ds(i * CT, CT)
                    nc.vector.tensor_tensor(h[:, :, tok], h[:, :, tok], p_v[:, :, 0:CT], ALU.add).then_inc(h_done, 1)


def quantised_ffn(nc, K):
    h, xn, ident = K["h"], K["xn"], K["ident"]
    with ExitStack() as st:
        def sb(n, shape, dt=F32):
            return st.enter_context(nc.sbuf_tensor(f"ff_{n}", shape, dt))

        def sem(n):
            return st.enter_context(nc.semaphore(f"ff_{n}"))

        gate = sb("gate", [P, IT, NT])
        up = sb("up", [P, IT, NT])
        gq = sb("gq", [P, IT, NT], I16)
        uq = sb("uq", [P, IT, NT], I16)
        sg = sb("sg", [P, 2, NT])
        sq = sb("sq", [P, 2, NT], U16)
        xq = sb("xq", [P, ET, NT], I16)
        oq = sb("oq", [P, 2, IT, CT], I16)
        of = sb("of", [P, 2, IT, CT])
        part = sb("part", [P, 2, IT * CH])
        pmax = sb("pmax", [P, 8])
        grow = sb("grow", [1, 8])
        gmax = sb("gmax", [P, 8])
        sc = sb("sc", [P, 32])
        onesr = sb("onesr", [1, P])

        p_t = st.enter_context(nc.psum_tensor("ff_t", [P, 512], F32))
        p_b = st.enter_context(nc.psum_tensor("ff_b", [P, 512], F32))
        p_g = st.enter_context(nc.psum_tensor("ff_g", [P, 2, 2, 512], F32))

        ones_ready = sem("ones_ready")
        xmax = sem("xmax")
        pm_ready = sem("pm_ready")
        turned = sem("turned")
        row_ready = sem("row_ready")
        spread = sem("spread")
        scale = sem("scale")
        xq_int = sem("xq_int")
        x_ready = sem("x_ready")
        gu_ready = sem("gu_ready")
        gu_copied = sem("gu_copied")
        gu_max = sem("gu_max")
        gq_ready = sem("gq_ready")
        uq_ready = sem("uq_ready")
        sg_ready = sem("sg_ready")
        sq_ready = sem("sq_ready")
        act_ready = sem("act_ready")
        act_max = sem("act_max")
        aq_ready = sem("aq_ready")
        o_ready = sem("o_ready")
        o_max = sem("o_max")
        oq_ready = sem("oq_ready")
        of_ready = sem("of_ready")
        y_ready = sem("y_ready")
        h_done = sem("h_done")

        QM = 1.0 / 32767.0

        def spread_max(pe, n):
            pe.wait_ge(pm_ready, n + 1)
            w = 2 if n == 1 else 1
            c = PMC[n]
            for j in range(w):
                last = nc.tensor.transpose(p_t[0:1, j * P:(j + 1) * P], pmax[:, c + j:c + j + 1], ident)
            last.then_inc(turned, 1)
            pe.wait_ge(row_ready, n + 1)
            nc.tensor.matmul(p_b[:, c:c + w], onesr[0:1, :], grow[0:1, c:c + w], start=True, stop=True).then_inc(spread, 1)

        PMC = [0, 1, 3, 4]

        def cols(c):
            return slice(c * CT, (c + 1) * CT)

        with nc.Block() as block:
            @block.tensor
            def _(pe):
                pe.wait_ge(ones_ready, 1)
                spread_max(pe, 0)
                for c in range(CH):
                    pe.wait_ge(x_ready, c + 1)
                    for o in range(IT):
                        n = c * IT + o
                        if n >= 2:
                            pe.wait_ge(gu_copied, n - 1)
                            pe.wait_ge(gu_max, n - 1)
                        for m, wt in enumerate((K["wgate"], K["wup"])):
                            for k in range(ET):
                                last = nc.tensor.matmul(p_g[:, n % 2, m, 0:CT], wt[:, k, o * P:(o + 1) * P],
                                                        xn[:, k, cols(c)], start=(k == 0), stop=(k == ET - 1))
                        last.then_inc(gu_ready, 1)
                spread_max(pe, 1)
                spread_max(pe, 2)
                spread_max(pe, 3)
                for c in range(CH):
                    pe.wait_ge(of_ready, c + 1)
                    if c >= 2:
                        pe.wait_ge(h_done, c - 1)
                    for t in range(ET):
                        for k in range(IT):
                            last = nc.tensor.matmul(p_g[:, c % 2, t, 0:CT], K["wdown"][:, k, t * P:(t + 1) * P],
                                                    of[:, c % 2, k], start=(k == 0), stop=(k == IT - 1))
                    last.then_inc(y_ready, 1)

            @block.scalar
            def _(act):
                for n in range(CH * IT):
                    c, o = n // IT, n % IT
                    act.wait_ge(gu_ready, n + 1)
                    act.wait_ge(gu_max, n + 1)
                    nc.scalar.copy(gate[:, o, cols(c)], p_g[:, n % 2, 0, 0:CT])
                    nc.scalar.copy(up[:, o, cols(c)], p_g[:, n % 2, 1, 0:CT]).then_inc(gu_copied, 1)
                act.wait_ge(scale, 10)
                for o in range(IT):
                    act.wait_ge(gq_ready, o + 1)
                    if o >= 2:
                        act.wait_ge(sq_ready, o - 1)
                    nc.scalar.activation(sg[:, o % 2], gq[:, o], ACT.Sigmoid, scale=sc[:, 6:7]).then_inc(sg_ready, 1)
                act.wait_ge(gu_copied, CH * IT)
                for o in range(IT):
                    nc.scalar.activation(uq[:, o], up[:, o], ACT.Copy, scale=sc[:, 9:10]).then_inc(uq_ready, 1)

            @block.vector
            def _(dve):
                nc.vector.memset(onesr[:], 1.0).then_inc(ones_ready, 1)
                steps = [0]

                def link(ins):
                    steps[0] += 1
                    ins.then_inc(scale, 1)
                    dve.wait_ge(scale, steps[0])

                def global_max(n):
                    w, c = (2 if n == 1 else 1), PMC[n]
                    dve.wait_ge(turned, n + 1)
                    nc.vector.tensor_reduce(grow[0:1, c:c + w], p_t[0:1, 0:w * P].rearrange("p (a b) -> p a b", a=w),
                                            AX.X, ALU.max).then_inc(row_ready, 1)
                    dve.wait_ge(spread, n + 1)
                    return p_b[:, c:c + w]

                nc.vector.tensor_reduce(pmax[:, 0:1], xn[:].rearrange("p t n -> p (t n)"), AX.X, ALU.max,
                                        apply_absolute_value=True).then_inc(pm_ready, 1)
                g = global_max(0)
                link(nc.vector.tensor_scalar(sc[:, 0:1], g, QM, 1e-12, ALU.mult, ALU.max))
                link(nc.vector.reciprocal(sc[:, 1:2], sc[:, 0:1]))
                for c in range(CH):
                    nc.vector.tensor_scalar(xq[:, :, cols(c)], xn[:, :, cols(c)], sc[:, 1:2], None,
                                            ALU.mult).then_inc(xq_int, 1)
                    dve.wait_ge(xq_int, c + 1)
                    nc.vector.tensor_copy(xn[:, :, cols(c)], xq[:, :, cols(c)]).then_inc(x_ready, 1)
                for n in range(CH * IT):
                    dve.wait_ge(gu_ready, n + 1)
                    nc.vector.tensor_reduce(part[:, :, n], p_g[:, n % 2, :, 0:CT], AX.X, ALU.max,
                                            apply_absolute_value=True).then_inc(gu_max, 1)
                dve.wait_ge(gu_max, CH * IT)
                nc.vector.tensor_reduce(pmax[:, 1:3], part[:], AX.X, ALU.max).then_inc(pm_ready, 1)
                g = global_max(1)
                link(nc.vector.tensor_scalar(sc[:, 2:4], g, sc[:, 0:1], None, ALU.mult))
                link(nc.vector.tensor_scalar(sc[:, 6:8], sc[:, 2:4], QM, 1e-12, ALU.mult, ALU.max))
                link(nc.vector.reciprocal(sc[:, 4:6], sc[:, 6:8]))
                link(nc.vector.tensor_scalar(sc[:, 8:10], sc[:, 4:6], sc[:, 0:1], None, ALU.mult))
                dve.wait_ge(gu_copied, CH * IT)
                link(nc.vector.tensor_scalar(sc[:, 10:11], sc[:, 6:7], 1.0 / 65536.0, None, ALU.mult))
                link(nc.vector.memset(sc[:, 11:12], 0.0))
                link(nc.vector.memset(sc[:, 12:13], 0.0))
                link(nc.vector.memset(sc[:, 13:14], 0.0))
                for o in range(IT + 2):
                    if o < IT:
                        nc.vector.tensor_scalar(gq[:, o], gate[:, o], sc[:, 8:9], None, ALU.mult).then_inc(gq_ready, 1)
                    if 1 <= o <= IT:
                        dve.wait_ge(sg_ready, o)
                        if o >= 3:
                            dve.wait_ge(act_ready, o - 2)
                        nc.vector.tensor_scalar(sq[:, (o - 1) % 2], sg[:, (o - 1) % 2], 65536.0, None,
                                                ALU.mult).then_inc(sq_ready, 1)
                    if o >= 2:
                        dve.wait_ge(sq_ready, o - 1)
                        dve.wait_ge(gq_ready, o - 1)
                        nc.vector.tensor_tensor(gate[:, o - 2], gq[:, o - 2], sq[:, (o - 2) % 2],
                                                ALU.mult).then_inc(act_ready, 1)
                        dve.wait_ge(act_ready, o - 1)
                        nc.vector.tensor_reduce(part[:, 0, o - 2:o - 1], gate[:, o - 2], AX.X, ALU.max,
                                                apply_absolute_value=True).then_inc(act_max, 1)
                dve.wait_ge(act_max, IT)
                nc.vector.tensor_reduce(pmax[:, 3:4], part[:, 0, 0:IT], AX.X, ALU.max).then_inc(pm_ready, 1)
                g = global_max(2)
                link(nc.vector.tensor_scalar(sc[:, 14:15], g, sc[:, 10:11], None, ALU.mult))
                link(nc.vector.tensor_scalar(sc[:, 15:16], sc[:, 14:15], QM, 1e-12, ALU.mult, ALU.max))
                link(nc.vector.reciprocal(sc[:, 16:17], sc[:, 15:16]))
                link(nc.vector.tensor_scalar(sc[:, 17:18], sc[:, 16:17], sc[:, 10:11], None, ALU.mult))
                link(nc.vector.tensor_tensor(sc[:, 18:19], sc[:, 15:16], sc[:, 7:8], ALU.mult))
                for o in range(IT):
                    dve.wait_ge(sg_ready, IT)
                    nc.vector.tensor_scalar(gq[:, o], gate[:, o], sc[:, 17:18], None, ALU.mult).then_inc(aq_ready, 1)
                    dve.wait_ge(aq_ready, o + 1)
                    dve.wait_ge(uq_ready, o + 1)
                    nc.vector.tensor_tensor(up[:, o], gq[:, o], uq[:, o], ALU.mult).then_inc(o_ready, 1)
                    dve.wait_ge(o_ready, o + 1)
                    nc.vector.tensor_reduce(part[:, 1, o:o + 1], up[:, o], AX.X, ALU.max,
                                            apply_absolute_value=True).then_inc(o_max, 1)
                dve.wait_ge(o_max, IT)
                nc.vector.tensor_reduce(pmax[:, 4:5], part[:, 1, 0:IT], AX.X, ALU.max).then_inc(pm_ready, 1)
                g = global_max(3)
                link(nc.vector.tensor_scalar(sc[:, 19:20], g, sc[:, 18:19], None, ALU.mult))
                link(nc.vector.tensor_scalar(sc[:, 20:21], sc[:, 19:20], QM, 1e-12, ALU.mult, ALU.max))
                link(nc.vector.reciprocal(sc[:, 21:22], sc[:, 20:21]))
                link(nc.vector.tensor_scalar(sc[:, 22:23], sc[:, 21:22], sc[:, 18:19], None, ALU.mult))
                for c in range(CH + 1):
                    if c < CH:
                        nc.vector.tensor_scalar(oq[:, c % 2], up[:, :, cols(c)], sc[:, 22:23], None,
                                                ALU.mult).then_inc(oq_ready, 1)
                        dve.wait_ge(oq_ready, c + 1)
                        if c >= 2:
                            dve.wait_ge(y_ready, c - 1)
                        nc.vector.tensor_copy(of[:, c % 2], oq[:, c % 2]).then_inc(of_ready, 1)
                    if c >= 1:
                        dve.wait_ge(y_ready, c)
                        if c < CH:
                            dve.wait_ge(of_ready, c + 1)
                        nc.vector.scalar_tensor_tensor(out=h[:, :, cols(c - 1)], in0=p_g[:, (c - 1) % 2, :, 0:CT],
                                                       scalar=sc[:, 20:21], in1=h[:, :, cols(c - 1)],
                                                       op0=ALU.mult, op1=ALU.add).then_inc(h_done, 1)


def cosine_attention(nc, K):
    h, xn, cs, ident = K["h"], K["xn"], K["cst"], K["ident"]
    NU = PAIRS
    BW = HT * TOK
    with ExitStack() as st:
        def sb(n, shape, dt=F32):
            return st.enter_context(nc.sbuf_tensor(f"ca_{n}", shape, dt))

        def ps(n, shape):
            return st.enter_context(nc.psum_tensor(f"ca_{n}", shape, F32))

        def sem(n):
            return st.enter_context(nc.semaphore(f"ca_{n}"))

        xg = sb("xg", [P, ET, CI, GAP])
        sq = sb("sq", [P, 2, ET, CT])
        ss = sb("ss", [P, ET, CT])
        ls = sb("ls", [P, ET, CT])
        inv = sb("inv", [P, 2, ET, CT])
        qn = sb("qn", [P, ET, CT])
        kn = sb("kn", [P, ET, CT])
        kx = sb("kx", [P, ET, CI, HT, TOK])
        vx = sb("vx", [P, CI, HT, 2, HD])
        vs = sb("vs", [P, PAIRS, HT, 2, HD])
        ex = sb("ex", [P, 4, HEADS, TOK])
        pr = sb("pr", [P, 2, HEADS, GAP])
        pts = sb("pts", [P, 2, 2, 4 * PW])
        mx = sb("mx", [P, 2, HEADS])
        sm = sb("sm", [P, 2, HEADS])
        rc = sb("rc", [P, 4, HEADS])

        p_s = ps("p_s", [P, 2, 2, 512])
        p_t = ps("p_t", [P, 2, 512])
        p_o = ps("p_o", [P, 512])
        p_v = ps("p_v", [P, 512])

        init = sem("init")
        xg_ready = sem("xg_ready")
        qk_ready = sem("qk_ready")
        sq_ready = sem("sq_ready")
        ss_ready = sem("ss_ready")
        ss_kept = sem("ss_kept")
        log_ready = sem("log_ready")
        inv_ready = sem("inv_ready")
        qk_normed = sem("qk_normed")
        kx_dve = sem("kx_dve")
        kx_act = sem("kx_act")
        v_ready = sem("v_ready")
        vs_ready = sem("vs_ready")
        vx_ready = sem("vx_ready")
        s_ready = sem("s_ready")
        max_ready = sem("max_ready")
        sub_ready = sem("sub_ready")
        exp_ready = sem("exp_ready")
        sum_ready = sem("sum_ready")
        rc_ready = sem("rc_ready")
        p_ready = sem("p_ready")
        pt_ready = sem("pt_ready")
        pts_ready = sem("pts_ready")
        pv_ready = sem("pv_ready")
        h_done = sem("h_done")

        with nc.Block() as block:
            @block.gpsimd
            def _(pool):
                for s in (sub_ready, v_ready, vx_ready, pv_ready, h_done, pts_ready, pt_ready, p_ready, vs_ready, log_ready):
                    pool.sem_inc(s, 1)
                nc.gpsimd.memset(vx[:], 0.0).then_inc(init, 1)
                nc.gpsimd.memset(vs[:], 0.0).then_inc(init, 1)
                nc.gpsimd.memset(pr[:], 0.0).then_inc(init, 1)
                nc.gpsimd.memset(xg[:], 0.0).then_inc(init, 1)
                pool.wait_ge(init, 4)
                with pool.Fori(0, CH) as i:
                    for u in range(NU):
                        pool.wait_ge(rc_ready, i * NU + u + 1)
                        pool.wait_ge(pt_ready, i * NU + u + 1)
                        nc.gpsimd.tensor_tensor(pr[0:PW, u % 2, :, 0:TOK], ex[0:PW, u % 4],
                                                bc(rc[0:PW, u % 4].unsqueeze(2), [PW, HEADS, TOK]),
                                                ALU.mult).then_inc(p_ready, 1)

            @block.sync
            def _(sp):
                sp.wait_ge(init, 4)
                with sp.Fori(0, CH) as i:
                    for p in range(PAIRS):
                        sp.wait_ge(vs_ready, i * PAIRS + p + 2)
                        sp.dma_start(vx[GAP:GAP + TOK, 2 * p], vs[0:TOK, p]).then_inc(vx_ready, 16)
                        sp.dma_start(vx[0:TOK, 2 * p + 1], vs[GAP:GAP + TOK, p]).then_inc(vx_ready, 16)

            @block.tensor
            def _(pe):
                pe.wait_ge(init, 4)
                with pe.Fori(0, CH) as i:
                    tok = bass.ds(i * CT, CT)
                    for j in range(2):
                        pe.wait_ge(sub_ready, i * NU + 1)
                        for t in range(ET):
                            o = (1 - j) * ED + t * P
                            for k in range(ET):
                                last = nc.tensor.matmul(p_s[:, j, t, 0:CT], K["w1qk"][:, k, o:o + P],
                                                        xn[:, k, tok], start=(k == 0), stop=(k == ET - 1))
                        last.then_inc(qk_ready, 1)
                    pe.wait_ge(xg_ready, i + 1)
                    for p in range(PAIRS):
                        if p == 0:
                            pe.wait_ge(vs_ready, i * PAIRS + 1)
                        else:
                            pe.wait_ge(vs_ready, i * PAIRS + p + 1)
                        for k in range(ET):
                            both = xg[:, k, 2 * p:2 * p + 2, :].rearrange("p a b -> p (a b)")
                            last = nc.tensor.matmul(p_v[0:PW, 0:ED], both[:, 0:PW], K["w1v"][:, k, :],
                                                    start=(k == 0), stop=(k == ET - 1))
                        last.then_inc(v_ready, 1)
                        if p < 2:
                            pe.wait_ge(sq_ready, i * 2 + p + 1)
                            if p == 0:
                                pe.wait_ge(pts_ready, i * 2 * NU + 1)
                            else:
                                pe.wait_ge(ss_kept, i * 2 + p)
                            for t in range(ET):
                                last = nc.tensor.matmul(p_t[:, t, 0:CT], cs[:, C_BD:C_BD + P], sq[:, p, t],
                                                        start=True, stop=True)
                            last.then_inc(ss_ready, 1)
                    for s in range(NU + 2):
                        if s < NU:
                            if s < 2:
                                pe.wait_ge(qk_normed, i * 2 + 2)
                            else:
                                pe.wait_ge(sub_ready, i * NU + s - 1 + 1)
                            if s == 0:
                                pe.wait_ge(kx_dve, i + 1)
                                pe.wait_ge(kx_act, i + 1)
                            for m in range(2):
                                img = 2 * s + m
                                for t in range(ET):
                                    last = nc.tensor.matmul(
                                        p_s[GAP * m:GAP * m + TOK, s % 2, t, 0:BW],
                                        qn[:, t, img * TOK:(img + 1) * TOK],
                                        kx[:, t, img].rearrange("p a b -> p (a b)"), start=True, stop=True)
                            last.then_inc(s_ready, 1)
                        if 1 <= s <= NU:
                            u = s - 1
                            pe.wait_ge(p_ready, i * NU + u + 2)
                            pe.wait_ge(ss_kept, i * 2 + 2)
                            pe.wait_ge(pts_ready, i * 2 * NU + 2 * u + 1)
                            for hp in range(HT):
                                src = pr[0:PW, u % 2, 2 * hp:2 * hp + 2, :].rearrange("p a b -> p (a b)")
                                last = nc.tensor.transpose(p_t[0:PW, hp // 4, (hp % 4) * PW:(hp % 4 + 1) * PW],
                                                           src[:, 0:PW], ident[0:PW, 0:PW])
                            last.then_inc(pt_ready, 1)
                        if s >= 2:
                            u = s - 2
                            if u == 0:
                                pe.wait_ge(vx_ready, (i + 1) * (PAIRS * 2 * 16) + 1)
                            pe.wait_ge(pts_ready, i * 2 * NU + 2 * u + 2 + 1)
                            pe.wait_ge(h_done, i * NU + u + 1)
                            for m in range(2):
                                for hp in range(HT):
                                    c = (hp // 4) * 2 * TOK + m * TOK
                                    last = nc.tensor.matmul(
                                        p_o[32 * (hp % 4):32 * (hp % 4) + 32, c:c + TOK],
                                        vx[0:PW, 2 * u + m, hp].rearrange("p a b -> p (a b)"),
                                        pts[0:PW, u % 2, hp // 4,
                                            (hp % 4) * PW + GAP * m:(hp % 4) * PW + GAP * m + TOK],
                                        start=True, stop=True)
                            last.then_inc(pv_ready, 1)

            @block.scalar
            def _(act):
                act.wait_ge(init, 4)
                with act.Fori(0, CH) as i:
                    act.wait_ge(v_ready, i * PAIRS + 1)
                    nc.scalar.copy(xg[:, :, :, 0:TOK],
                                   xn[:, :, bass.ds(i * CT, CT)].rearrange("p t (a b) -> p t a b", b=TOK)).then_inc(xg_ready, 1)
                    for j in range(2):
                        act.wait_ge(qk_ready, i * 2 + j + 1)
                        nc.scalar.activation(sq[:, j], p_s[:, j, :, 0:CT], ACT.Square).then_inc(sq_ready, 1)
                    act.wait_ge(vx_ready, i * (PAIRS * 2 * 16) + 1)
                    act.wait_ge(pv_ready, i * NU + 1)

                    def values(p):
                        act.wait_ge(v_ready, i * PAIRS + p + 2)
                        v = p_v[:, 0:ED].rearrange("p (a b c) -> p a b c", a=2, c=HD)
                        nc.scalar.copy(vx[0:TOK, 2 * p, :, 0, :], v[0:TOK, 0])
                        nc.scalar.copy(vs[0:TOK, p, :, 1, :], v[0:TOK, 1])
                        nc.scalar.copy(vx[GAP:PW, 2 * p + 1, :, 1, :], v[GAP:PW, 1])
                        nc.scalar.copy(vs[GAP:PW, p, :, 0, :], v[GAP:PW, 0]).then_inc(vs_ready, 1)

                    def inverse(j):
                        act.wait_ge(ss_kept, i * 2 + j + 1)
                        nc.scalar.activation(ls[:], ss[:], ACT.Ln, scale=L2_SCALE).then_inc(log_ready, 1)
                        act.wait_ge(log_ready, i * 2 + j + 2)
                        nc.scalar.activation(inv[:, j], ls[:], ACT.Exp, scale=-0.5,
                                             bias=K["eps"][:, 1:2]).then_inc(inv_ready, 1)

                    values(0)
                    inverse(0)
                    values(1)
                    inverse(1)
                    act.wait_ge(qk_normed, i * 2 + 1)
                    for t in range(ET):
                        for hh in range(4, HT):
                            last = nc.scalar.activation(kx[:, t, :, hh, :], kn[:, t].rearrange("p (a b) -> p a b", b=TOK),
                                                        ACT.Copy, scale=K["mask1"][:, hh:hh + 1])
                    last.then_inc(kx_act, 1)
                    values(2)
                    values(3)
                    for s in range(NU + 1):
                        if s < NU:
                            act.wait_ge(sub_ready, i * NU + s + 2)
                            nc.scalar.activation(ex[0:PW, s % 4], ex[0:PW, s % 4], ACT.Exp).then_inc(exp_ready, 1)
                        if s >= 1:
                            u = s - 1
                            act.wait_ge(pt_ready, i * NU + u + 2)
                            for b in range(2):
                                nc.scalar.copy(pts[0:PW, u % 2, b], p_t[0:PW, b, 0:4 * PW]).then_inc(pts_ready, 1)

            @block.vector
            def _(dve):
                with dve.Fori(0, CH) as i:
                    for j in range(2):
                        dve.wait_ge(ss_ready, i * 2 + j + 1)
                        dve.wait_ge(log_ready, i * 2 + j + 1)
                        nc.vector.tensor_scalar(ss[:], p_t[:, :, 0:CT], 1e-24, None, ALU.max).then_inc(ss_kept, 1)
                        dve.wait_ge(inv_ready, i * 2 + j + 1)
                        nc.vector.tensor_tensor((kn, qn)[j][:], p_s[:, j, :, 0:CT], inv[:, j], ALU.mult).then_inc(qk_normed, 1)
                        if j == 0:
                            dve.wait_ge(qk_normed, i * 2 + 1)
                            for t in range(ET):
                                for hh in range(4):
                                    last = nc.vector.tensor_scalar(
                                        kx[:, t, :, hh, :], kn[:, t].rearrange("p (a b) -> p a b", b=TOK),
                                        K["mask1"][:, hh:hh + 1], None, ALU.mult)
                            last.then_inc(kx_dve, 1)
                    for s in range(NU + 3):
                        if s < NU:
                            dve.wait_ge(s_ready, i * NU + s + 1)
                            sc = p_s[0:PW, s % 2, :, 0:BW].rearrange("p a (b c) -> p a b c", c=TOK)
                            nc.vector.tensor_reduce(mx[0:PW, s % 2].rearrange("p (a b) -> p a b", a=2), sc,
                                                    AX.X, ALU.max).then_inc(max_ready, 1)
                            dve.wait_ge(max_ready, i * NU + s + 1)
                            dve.wait_ge(p_ready, i * NU + 1)
                            nc.vector.tensor_tensor(
                                ex[0:PW, s % 4].rearrange("p (a b) c -> p a b c", a=2), sc,
                                bc(mx[0:PW, s % 2].rearrange("p (a b) -> p a b", a=2).unsqueeze(3), [PW, 2, HT, TOK]),
                                ALU.subtract).then_inc(sub_ready, 1)
                        if 1 <= s <= NU:
                            u = s - 1
                            dve.wait_ge(exp_ready, i * NU + u + 1)
                            nc.vector.tensor_reduce(sm[0:PW, u % 2], ex[0:PW, u % 4], AX.X, ALU.add).then_inc(sum_ready, 1)
                            dve.wait_ge(sum_ready, i * NU + u + 1)
                            nc.vector.reciprocal(rc[0:PW, u % 4], sm[0:PW, u % 2]).then_inc(rc_ready, 1)
                        if s >= 3:
                            u = s - 3
                            dve.wait_ge(pv_ready, i * NU + u + 2)
                            pair = bass.ds(i * CT + u * 2 * TOK, 2 * TOK)
                            nc.vector.tensor_tensor(h[:, :, pair], h[:, :, pair],
                                                    p_o[:, 0:4 * TOK].rearrange("p (a b) -> p a b", a=2),
                                                    ALU.add).then_inc(h_done, 1)


def tree_ffn(nc, K, wq1, routT, leafT, woutT, outT):
    h, xn, vec, ident = K["h"], K["xn"], K["vec"], K["ident"]
    NTT = (NT + P - 1) // P
    NN = LEAVES - 1
    with ExitStack() as st:
        def sb(n, shape, dt=F32):
            return st.enter_context(nc.sbuf_tensor(f"tr_{n}", shape, dt))

        def ps(n, shape):
            return st.enter_context(nc.psum_tensor(f"tr_{n}", shape, F32))

        def sem(n):
            return st.enter_context(nc.semaphore(f"tr_{n}"))

        wq = sb("wq", [P, ET, ED])
        wr = sb("wr", [P, ET, NN])
        lf = sb("lf", [P, ET, LEAVES])
        wo = sb("wo", [P, ET, ED])
        route = sb("route", [P, ET, NN])
        leafo = sb("leafo", [P, ET, ED])
        sig = sb("sig", [P, NTT, LEAVES])
        lpa = sb("lpa", [P, NTT, LEAVES])
        lpb = sb("lpb", [P, NTT, LEAVES])
        lpT = sb("lpT", [P, ET, NT])
        y = sb("y", [P, ET, NT])

        p_w = ps("p_w", [P, 2, 512])
        p_l = ps("p_l", [P, 2, 512])
        p_t = ps("p_t", [P, 2, 512])
        p_y = ps("p_y", [P, 2, 512])

        w_in = sem("w_in")
        fold_ready = sem("fold_ready")
        fold_kept = sem("fold_kept")
        logit_ready = sem("logit_ready")
        sig_ready = sem("sig_ready")
        sig_zero = sem("sig_zero")
        level = sem("level")
        lpT_psum = sem("lpT_psum")
        lpT_ready = sem("lpT_ready")
        y_psum = sem("y_psum")
        y_ready = sem("y_ready")
        stored = sem("stored")

        def rows(n):
            return min(P, NT - n * P)

        HALF = [(0, NTT // 2), (NTT // 2, NTT)]

        with nc.Block() as block:
            @block.sync
            def _(sp):
                sp.dma_start(wq[:], wq1).then_inc(w_in, 16)
                sp.dma_start(wr[:], routT).then_inc(w_in, 16)
                sp.dma_start(lf[:], leafT).then_inc(w_in, 16)
                sp.dma_start(wo[:], woutT).then_inc(w_in, 16)
                for c in range(CH):
                    sp.wait_ge(y_ready, c + 1)
                    sp.dma_start(outT[:, :, c * CT:(c + 1) * CT], y[:, :, c * CT:(c + 1) * CT]).then_inc(stored, 16)
                sp.wait_ge(stored, CH * 16)

            @block.gpsimd
            def _(pool):
                nc.gpsimd.memset(sig[:], 0.5).then_inc(sig_zero, 1)

            @block.tensor
            def _(pe):
                pe.wait_ge(w_in, 64)
                for t in range(ET):
                    for k in range(ET):
                        last = nc.tensor.matmul(p_w[:, 0, t * 256:t * 256 + NN], wq[:, k, t * P:(t + 1) * P], wr[:, k, :],
                                                start=(k == 0), stop=(k == ET - 1))
                last.then_inc(fold_ready, 1)
                for t in range(ET):
                    for k in range(ET):
                        last = nc.tensor.matmul(p_w[:, 1, t * 256:t * 256 + ED], lf[:, k, t * P:(t + 1) * P], wo[:, k, :],
                                                start=(k == 0), stop=(k == ET - 1))
                last.then_inc(fold_ready, 1)
                pe.wait_ge(fold_kept, 1)
                for n in range(NTT):
                    if n >= 2:
                        pe.wait_ge(sig_ready, n - 1)
                    r = rows(n)
                    for k in range(ET):
                        last = nc.tensor.matmul(p_l[0:r, n % 2, 0:NN], xn[:, k, n * P:n * P + r], route[:, k, :],
                                                start=(k == 0), stop=(k == ET - 1))
                    last.then_inc(logit_ready, 1)
                for n in range(NTT):
                    if n in (0, NTT // 2):
                        pe.wait_ge(level, 16 if n == 0 else 32)
                    if n >= 2:
                        pe.wait_ge(lpT_ready, n - 1)
                    r = rows(n)
                    for t in range(ET):
                        last = nc.tensor.transpose(p_t[:, n % 2, t * P:t * P + r], lpa[0:r, n, t * P:(t + 1) * P],
                                                   ident[0:r, 0:r])
                    last.then_inc(lpT_psum, 1)
                pe.wait_ge(fold_kept, 2)
                for c in range(CH):
                    pe.wait_ge(lpT_ready, min(NTT, -(-(c + 1) * CT // P)))
                    if c >= 1:
                        pe.wait_ge(y_ready, c)
                    for t in range(ET):
                        for k in range(ET):
                            last = nc.tensor.matmul(p_y[:, t, 0:CT], leafo[:, k, t * P:(t + 1) * P],
                                                    lpT[:, k, c * CT:(c + 1) * CT], start=(k == 0), stop=(k == ET - 1))
                    last.then_inc(y_psum, 1)

            @block.scalar
            def _(act):
                act.wait_ge(sig_zero, 1)
                act.wait_ge(fold_ready, 2)
                nc.scalar.copy(route[:], p_w[:, 0].rearrange("p (a b) -> p a b", a=2)[:, :, 0:NN]).then_inc(fold_kept, 1)
                nc.scalar.copy(leafo[:], p_w[:, 1].rearrange("p (a b) -> p a b", a=2)).then_inc(fold_kept, 1)
                for n in range(NTT):
                    r = rows(n)
                    act.wait_ge(logit_ready, n + 1)
                    nc.scalar.activation(sig[0:r, n, 0:NN], p_l[0:r, n % 2, 0:NN], ACT.Sigmoid).then_inc(sig_ready, 1)
                for n in range(NTT):
                    r = rows(n)
                    act.wait_ge(lpT_psum, n + 1)
                    nc.scalar.copy(lpT[:, :, n * P:n * P + r],
                                   p_t[:, n % 2, 0:2 * P].rearrange("p (a b) -> p a b", a=2)[:, :, 0:r]).then_inc(lpT_ready, 1)

            @block.vector
            def _(dve):
                done = 0
                for a, b in HALF:
                    dve.wait_ge(sig_ready, b)
                    n = b - a
                    for lv in range(DEPTH):
                        w = 2 ** lv
                        src, dst = (lpb, lpa) if lv % 2 else (lpa, lpb)
                        pair = dst[:, a:b, 0:2 * w].rearrange("p n (c s) -> p n c s", s=2)
                        g = sig[:, a:b, w - 1:2 * w - 1]
                        if lv == 0:
                            nc.vector.tensor_copy(pair[:, :, :, 1], g).then_inc(level, 1)
                            nc.vector.tensor_scalar(pair[:, :, :, 0], g, -1.0, 1.0, ALU.mult, ALU.add).then_inc(level, 1)
                        else:
                            nc.vector.tensor_tensor(pair[:, :, :, 1], src[:, a:b, 0:w], g, ALU.mult).then_inc(level, 1)
                            dve.wait_ge(level, done + 1)
                            nc.vector.tensor_tensor(pair[:, :, :, 0], src[:, a:b, 0:w], pair[:, :, :, 1],
                                                    ALU.subtract).then_inc(level, 1)
                        done += 2
                        dve.wait_ge(level, done)
                for c in range(CH):
                    dve.wait_ge(y_psum, c + 1)
                    cols = slice(c * CT, (c + 1) * CT)
                    for t in range(ET):
                        last = nc.vector.scalar_tensor_tensor(out=y[:, t, cols], in0=p_y[:, t, 0:CT],
                                                              scalar=vec[:, V_WB + t:V_WB + t + 1], in1=h[:, t, cols],
                                                              op0=ALU.add, op1=ALU.add)
                    last.then_inc(y_ready, 1)


def tiles(a, k):
    return np.ascontiguousarray(a.reshape(k, P, -1).transpose(1, 0, 2))


def constants():
    c = np.zeros((P, C_END), np.float32)
    c[:, C_ID:C_ID + P] = np.eye(P)
    row = np.arange(P)
    c[:, C_BD:C_BD + P] = (row[:, None] // HD) == (row[None, :] // HD)
    c[:, C_MASK:C_MASK + HT] = (row[:, None] // HD) == np.arange(HT)[None, :]
    inv = (np.float32(1.0) / np.float32(10000.0) ** (np.arange(0, 2 * HD, 2, dtype=np.float32) / np.float32(2 * HD)))
    ang = np.arange(TOK, dtype=np.float32)[None, :] * inv.astype(np.float32)[row % HD][:, None]
    c[:, C_COS:C_COS + TOK] = np.cos(ang)
    c[:, C_SIN:C_SIN + TOK] = np.sin(ang)
    return c


def kernel(**inp):
    import concourse.bacc as bacc
    from concourse.bass_utils import run_bass_kernel_spmd

    a = {k: np.asarray(v) for k, v in inp.items()}
    x = a["x"].reshape(IMGS, 3, 6, 16, 6, 16).transpose(0, 2, 4, 3, 5, 1).reshape(IMGS * PATCH, PD)
    xT = x.T.reshape(PT6, P, CH, CP).transpose(2, 1, 0, 3)

    def vec(v):
        return v.reshape(-1, P).T

    pos = a["L0_tok_pos_emb"][0].T.reshape(ET, P, TOK).transpose(1, 0, 2).reshape(P, ET * TOK)
    vecs = np.concatenate([vec(a["L0_tok_ln1_g"]), vec(a["L0_tok_ln1_b"]), vec(a["L0_tok_b_proj"]),
                           vec(a["L0_tok_ln2_g"]), vec(a["L0_tok_ln2_b"]), vec(a["L0_tok_cls_token"].reshape(-1)),
                           vec(a["L1_ffn_Wout_b"]), pos], axis=1)
    lams = np.concatenate([a["L0_attn_lambda_q1"], a["L0_attn_lambda_q2"],
                           a["L0_attn_lambda_k1"], a["L0_attn_lambda_k2"]]).reshape(1, 64)
    wqkv = a["L0_attn_W_qkv"]
    wv = wqkv[4 * ED:].reshape(2, HT, 2, HD, ED).transpose(2, 1, 0, 3, 4).reshape(2 * ED, ED)
    w1v = a["L1_attn_Wv"].reshape(HT, 2, HD, ED).transpose(1, 0, 2, 3).reshape(ED, ED)
    arrays = {
        "xT": xT, "wtok": tiles(a["L0_tok_W_proj"], PT6), "vecs": vecs, "lams": lams,
        "gsc": a["L1_attn_g_scale"].reshape(1, 1), "cst": constants(),
        "wqkT": tiles(wqkv[:4 * ED].T, ET), "wvT": tiles(wv.T, ET),
        "wprojT": tiles(a["L0_attn_W_proj"].T, 4),
        "w_up": tiles(a["L0_ffn_w_up"], IT).reshape(P, -1), "w_gate": tiles(a["L0_ffn_w_gate"], IT).reshape(P, -1),
        "w_down": tiles(a["L0_ffn_w_down"], ET).reshape(P, -1),
        "w1qkT": tiles(np.concatenate([a["L1_attn_Wq"], a["L1_attn_Wk"]]).T, ET),
        "w1vT": tiles(w1v.T, ET),
        "wq1": tiles(a["L1_ffn_Wq"], ET), "routT": tiles(a["L1_ffn_routers"].T, ET),
        "leafT": tiles(a["L1_ffn_leaf_values"].T, ET), "woutT": tiles(a["L1_ffn_Wout_w"].T, ET),
    }
    arrays = {k: np.ascontiguousarray(v) for k, v in arrays.items()}
    nc = bacc.Bacc("TRN2", target_bir_lowering=False, num_devices=1)
    args = [nc.dram_tensor(k, v.shape, mybir.dt.from_np(v.dtype), kind="ExternalInput").ap() for k, v in arrays.items()]
    out = nc.dram_tensor("outT", (P, ET, NT), F32, kind="ExternalOutput").ap()
    program(nc, *args, out)
    got = run_bass_kernel_spmd(nc, [arrays], core_ids=[0]).results[0]["outT"]
    return np.ascontiguousarray(got.transpose(2, 1, 0).reshape(IMGS, TOK, ED))
```

```python
from contextlib import ExitStack
import math

import numpy as np

import concourse.bass as bass
from concourse import mybir

F32 = mybir.dt.float32
I16 = mybir.dt.int16
U16 = mybir.dt.uint16
ALU = mybir.AluOpType
ACT = mybir.ActivationFunctionType
AX = mybir.AxisListType

P = 128
IMGS = 32
PATCH = 36
TOK = PATCH + 1
NT = IMGS * TOK
CH = 4
CI = IMGS // CH
CT = CI * TOK
CP = CI * PATCH
PAIRS = CI // 2
ED = 256
ET = ED // P
PD = 768
PT6 = PD // P
HEADS = 16
HD = 16
HT = 8
IF = 768
IT = IF // P
GAP = 64
PW = GAP + TOK
BLK = 32
LEAVES = 256
DEPTH = 8
EPS = 1e-5
L2_SCALE = 2.0 ** 16

C_ID, C_BD, C_MASK, C_COS, C_SIN, C_END = 0, 128, 256, 264, 301, 338
V_G1, V_B1, V_BP, V_G2, V_B2, V_CLS, V_WB, V_POS, V_END = 0, 6, 12, 14, 16, 18, 20, 22, 22 + 2 * TOK


def bc(ap, shape):
    return ap.to_broadcast(shape)


def program(nc, xT, wtok, vecs, lams, gsc, cst, wqkT, wvT, wprojT, w_up, w_gate, w_down,
            w1qkT, w1vT, wq1, routT, leafT, woutT, outT):
    with ExitStack() as top:
        def sb(name, shape, dt=F32):
            return top.enter_context(nc.sbuf_tensor(name, shape, dt))

        K = {}
        K["h"] = sb("h", [P, ET, NT])
        K["xn"] = sb("xn", [P, ET, NT])
        K["cst"] = sb("cst_sb", [P, C_END])
        K["vec"] = sb("vec_sb", [P, V_END])
        K["wqk"] = sb("wqk_sb", [P, ET, 4 * ED])
        K["wv"] = sb("wv_sb", [P, ET, 2 * ED])
        K["wp"] = sb("wp_sb", [P, 4, ED])
        K["w1qk"] = sb("w1qk_sb", [P, ET, 2 * ED])
        K["w1v"] = sb("w1v_sb", [P, ET, ED])
        K["wup"] = sb("wup_sb", [P, ET, IF])
        K["wgate"] = sb("wgate_sb", [P, ET, IF])
        K["wdown"] = sb("wdown_sb", [P, IT, ED])
        K["mask0"] = sb("mask0", [P, HT])
        K["mask1"] = sb("mask1", [P, HT])
        K["neglam"] = sb("neglam", [P, 2])
        K["eps"] = sb("eps", [P, 2])
        K["mean256"] = sb("mean256", [P, P])
        K["xg"] = sb("xg", [P, ET, CI, GAP])
        K["pr"] = sb("pr", [P, 4 * HT * GAP])
        K["vx"] = sb("vx", [P, CI, 2, HT * 32])
        K["loaded"] = top.enter_context(nc.semaphore("weights_loaded"))
        K["ident"] = K["cst"][:, C_ID:C_ID + P]

        tokenizer(nc, K, xT, wtok, vecs, lams, gsc, cst, wqkT, wvT, wprojT, w_up, w_gate, w_down, w1qkT, w1vT)
        layernorm(nc, K, "ln_a")
        diff_attention(nc, K)
        layernorm(nc, K, "ln_f")
        quantised_ffn(nc, K)
        layernorm(nc, K, "ln_b")
        cosine_attention(nc, K)
        layernorm(nc, K, "ln_g")
        tree_ffn(nc, K, wq1, routT, leafT, woutT, outT)


def tokenizer(nc, K, xT, wtok, vecs, lams, gsc, cst, wqkT, wvT, wprojT, w_up, w_gate, w_down, w1qkT, w1vT):
    h, cs, vec, ident = K["h"], K["cst"], K["vec"], K["ident"]
    with ExitStack() as st:
        def sb(name, shape, dt=F32):
            return st.enter_context(nc.sbuf_tensor(name, shape, dt))

        def ps(name, shape):
            return st.enter_context(nc.psum_tensor(name, shape, F32))

        def sem(name):
            return st.enter_context(nc.semaphore(name))

        x = sb("x_sb", [P, CH, PT6, CP])
        w = sb("wtok_sb", [P, PT6, ED])
        wg = sb("wtok_g", [P, PT6, ED])
        mean768 = sb("mean768", [P, P])
        xc = sb("t_xc", [P, 2, PT6, CP])
        sq = sb("t_sq", [P, PT6, CP])
        ln1 = sb("t_ln1", [P, CP])
        rstd1 = sb("t_rstd1", [P, CP])
        zr = sb("t_zr", [P, ET, CP])
        zs = sb("t_zs", [P, ET, CP])
        xc2 = sb("t_xc2", [P, ET, CP])
        sq2 = sb("t_sq2", [P, ET, CP])
        ln2 = sb("t_ln2", [P, CP])
        rstd2 = sb("t_rstd2", [P, CP])
        z3 = sb("t_z3", [P, ET, CP])
        c0 = sb("t_c0", [P, ET])
        posb = sb("t_posb", [P, ET, TOK])
        raw = sb("raw_w", [P, 3, IT * ED])
        wint = sb("int_w", [P, IT * ED], I16)
        wdq = sb("deq_w", [P, 3, IT * ED])
        wmax = sb("wmax", [P, 3, 48])
        wsc = sb("wsc", [P, 3, 48])
        wrs = sb("wrs", [P, 3, 48])
        row = sb("row", [1, 80])
        onesr = sb("onesr", [1, P])

        p_mean = ps("p_mean", [P, 2, 512])
        p_var = ps("p_var", [P, 512])
        p_z = ps("p_z", [P, 2, 512])
        p_mu2 = ps("p_mu2", [P, 512])
        p_var2 = ps("p_var2", [P, 512])
        p_misc = ps("p_misc", [P, 512])

        small_in = sem("small_in")
        wtok_in = sem("wtok_in")
        x_in = [sem(f"x_in{c}") for c in range(CH)]
        ffw_in = sem("ffw_in")
        consts = sem("consts")
        wg_ready = sem("wg_ready")
        c0_psum = sem("c0_psum")
        row_step = sem("row_step")
        row_exp = sem("row_exp")
        row_bc = sem("row_bc")
        mean_ready = sem("mean_ready")
        xc_ready = sem("xc_ready")
        sq_ready = sem("sq_ready")
        var_ready = sem("var_ready")
        ln1_done = sem("ln1_done")
        rstd1_ready = sem("rstd1_ready")
        z_ready = sem("z_ready")
        zr_ready = sem("zr_ready")
        zs_ready = sem("zs_ready")
        mu2_ready = sem("mu2_ready")
        xc2_ready = sem("xc2_ready")
        sq2_ready = sem("sq2_ready")
        var2_ready = sem("var2_ready")
        ln2_done = sem("ln2_done")
        rstd2_ready = sem("rstd2_ready")
        z3_ready = sem("z3_ready")
        h_ready = sem("h_ready")
        deq = sem("deq")
        wt_psum = sem("wt_psum")
        wt_out = sem("wt_out")

        with nc.Block() as block:
            @block.sync
            def _(sp):
                sp.dma_start(cs[:], cst).then_inc(small_in, 16)
                sp.dma_start(vec[:], vecs).then_inc(small_in, 16)
                sp.dma_start(row[0:1, 0:64], lams).then_inc(small_in, 16)
                sp.dma_start(row[0:1, 79:80], gsc).then_inc(small_in, 16)
                sp.dma_start(x[:, 0], xT[0]).then_inc(x_in[0], 16)
                sp.dma_start(w[:], wtok).then_inc(wtok_in, 16)
                for c in range(1, CH):
                    sp.dma_start(x[:, c], xT[c]).then_inc(x_in[c], 16)
                sp.dma_start(K["wqk"][:], wqkT).then_inc(K["loaded"], 16)
                sp.dma_start(K["wv"][:], wvT).then_inc(K["loaded"], 16)
                for n, src in enumerate((w_up, w_gate, w_down)):
                    sp.dma_start(raw[:, n, :], src).then_inc(ffw_in, 16)
                sp.dma_start(K["wp"][:], wprojT).then_inc(K["loaded"], 16)
                sp.dma_start(K["w1qk"][:], w1qkT).then_inc(K["loaded"], 16)
                sp.dma_start(K["w1v"][:], w1vT).then_inc(K["loaded"], 16)

            @block.gpsimd
            def _(pool):
                nc.gpsimd.memset(mean768[:], 1.0 / PD).then_inc(consts, 1)
                nc.gpsimd.memset(K["mean256"][:], 1.0 / ED).then_inc(consts, 1)
                nc.gpsimd.memset(onesr[:], 1.0).then_inc(consts, 1)
                nc.gpsimd.memset(K["eps"][:, 0:1], EPS).then_inc(consts, 1)
                nc.gpsimd.memset(K["eps"][:, 1:2], 0.5 * math.log(L2_SCALE)).then_inc(consts, 1)
                nc.gpsimd.memset(K["xg"][:], 0.0)
                nc.gpsimd.memset(K["pr"][:], 0.0)
                nc.gpsimd.memset(K["vx"][:], 0.0)

            @block.tensor
            def _(pe):
                pe.wait_ge(consts, 5)
                pe.wait_ge(small_in, 64)

                def mean(c):
                    pe.wait_ge(x_in[c], 16)
                    if c >= 2:
                        pe.wait_ge(xc_ready, c - 1)
                    for k in range(PT6):
                        last = nc.tensor.matmul(p_mean[:, c % 2, 0:CP], mean768[:], x[:, c, k, :],
                                                start=(k == 0), stop=(k == PT6 - 1))
                    last.then_inc(mean_ready, 1)

                mean(0)
                pe.wait_ge(wtok_in, 16)
                for t in range(ET):
                    for k in range(PT6):
                        last = nc.tensor.matmul(p_misc[:, t:t + 1], w[:, k, t * P:(t + 1) * P],
                                                vec[:, V_B1 + k:V_B1 + k + 1], start=(k == 0), stop=(k == PT6 - 1))
                last.then_inc(c0_psum, 1)
                pe.wait_ge(wg_ready, PT6)
                for c in range(CH + 1):
                    if c < CH:
                        pe.wait_ge(xc_ready, c + 1)
                        if c >= 1:
                            pe.wait_ge(zr_ready, c)
                        for t in range(ET):
                            for k in range(PT6):
                                last = nc.tensor.matmul(p_z[:, t, 0:CP], wg[:, k, t * P:(t + 1) * P],
                                                        xc[:, c % 2, k, :], start=(k == 0), stop=(k == PT6 - 1))
                        last.then_inc(z_ready, 1)
                    if c + 1 < CH:
                        mean(c + 1)
                    if c < CH:
                        pe.wait_ge(sq_ready, c + 1)
                        if c >= 1:
                            pe.wait_ge(ln1_done, c)
                        for k in range(PT6):
                            last = nc.tensor.matmul(p_var[:, 0:CP], mean768[:], sq[:, k, :],
                                                    start=(k == 0), stop=(k == PT6 - 1))
                        last.then_inc(var_ready, 1)
                    if c >= 1:
                        pe.wait_ge(zs_ready, 2 * c)
                        if c >= 2:
                            pe.wait_ge(xc2_ready, c - 1)
                        for k in range(ET):
                            last = nc.tensor.matmul(p_mu2[:, 0:CP], K["mean256"][:], zs[:, k, :],
                                                    start=(k == 0), stop=(k == ET - 1))
                        last.then_inc(mu2_ready, 1)
                        pe.wait_ge(sq2_ready, c)
                        if c >= 2:
                            pe.wait_ge(ln2_done, c - 1)
                        for k in range(ET):
                            last = nc.tensor.matmul(p_var2[:, 0:CP], K["mean256"][:], sq2[:, k, :],
                                                    start=(k == 0), stop=(k == ET - 1))
                        last.then_inc(var2_ready, 1)
                pe.wait_ge(row_step, 5)
                pe.wait_ge(row_step, 6)
                nc.tensor.matmul(p_mean[:, 0, 0:2], onesr[0:1, :], row[0:1, 78:80], start=True, stop=True).then_inc(row_bc, 1)
                n = 0
                for m in range(3):
                    pe.wait_ge(deq, 3 * (m + 1))
                    for q in range(3):
                        if n >= 2:
                            pe.wait_ge(wt_out, n - 1)
                        for b in range(4):
                            s = 4 * q + b
                            src = wdq[:, m, s * P:(s + 1) * P]
                            last = nc.tensor.transpose(p_z[:, n % 2, b * P:(b + 1) * P], src, ident)
                        last.then_inc(wt_psum, 1)
                        n += 1

            @block.scalar
            def _(act):
                nc.scalar.preload_act_table_set("natural_log_exp_and_others")
                act.wait_ge(consts, 5)
                act.wait_ge(row_step, 2)
                nc.scalar.activation(row[0:1, 70:72], row[0:1, 68:70], ACT.Exp).then_inc(row_exp, 1)

                def square(c):
                    act.wait_ge(xc_ready, c + 1)
                    nc.scalar.activation(sq[:], xc[:, c % 2], ACT.Square).then_inc(sq_ready, 1)

                square(0)
                for c in range(CH):
                    if c < CH:
                        act.wait_ge(var_ready, c + 1)
                        nc.scalar.activation(ln1[:], p_var[:, 0:CP], ACT.Ln, bias=K["eps"][:, 0:1]).then_inc(ln1_done, 1)
                        act.wait_ge(ln1_done, c + 1)
                        if c >= 1:
                            act.wait_ge(zr_ready, c)
                        nc.scalar.activation(rstd1[:], ln1[:], ACT.Exp, scale=-0.5).then_inc(rstd1_ready, 1)
                        act.wait_ge(zr_ready, c + 1)
                        if c >= 1:
                            act.wait_ge(xc2_ready, c)
                        for t in range(ET):
                            nc.scalar.activation(zs[:, t], zr[:, t], ACT.Identity, bias=c0[:, t:t + 1]).then_inc(zs_ready, 1)
                        if c + 1 < CH:
                            square(c + 1)
                        act.wait_ge(xc2_ready, c + 1)
                        nc.scalar.activation(sq2[:], xc2[:], ACT.Square).then_inc(sq2_ready, 1)
                        act.wait_ge(var2_ready, c + 1)
                        nc.scalar.activation(ln2[:], p_var2[:, 0:CP], ACT.Ln, bias=K["eps"][:, 0:1]).then_inc(ln2_done, 1)
                        act.wait_ge(ln2_done, c + 1)
                        if c >= 1:
                            act.wait_ge(z3_ready, c)
                        nc.scalar.activation(rstd2[:], ln2[:], ACT.Exp, scale=-0.5).then_inc(rstd2_ready, 1)
                dst = [K["wup"], K["wgate"], K["wdown"]]
                n = 0
                for m in range(3):
                    for q in range(3):
                        act.wait_ge(wt_psum, n + 1)
                        for b in range(4):
                            s = 4 * q + b
                            if m < 2:
                                o, i = s // ET, s % ET
                                out = dst[m][:, i, o * P:(o + 1) * P]
                            else:
                                o, i = s // IT, s % IT
                                out = dst[m][:, i, o * P:(o + 1) * P]
                            last = nc.scalar.copy(out, p_z[:, n % 2, b * P:(b + 1) * P])
                        last.then_inc(wt_out, 1)
                        n += 1

            @block.vector
            def _(dve):
                dve.wait_ge(small_in, 64)
                nc.vector.tensor_tensor(row[0:1, 0:32], row[0:1, 0:32], row[0:1, 32:64], ALU.mult).then_inc(row_step, 1)
                dve.wait_ge(row_step, 1)
                nc.vector.tensor_reduce(row[0:1, 68:70], row[0:1, 0:32].rearrange("p (a b) -> p a b", a=2),
                                        AX.X, ALU.add).then_inc(row_step, 1)
                nc.vector.tensor_tensor(posb[:], vec[:, V_POS:V_END].rearrange("p (t n) -> p t n", t=ET),
                                        bc(vec[:, V_B2:V_B2 + ET].unsqueeze(2), [P, ET, TOK]), ALU.add).then_inc(row_step, 1)
                dve.wait_ge(wtok_in, 16)
                for k in range(PT6):
                    nc.vector.tensor_scalar(wg[:, k], w[:, k], vec[:, V_G1 + k:V_G1 + k + 1], None, ALU.mult).then_inc(wg_ready, 1)
                dve.wait_ge(c0_psum, 1)
                nc.vector.tensor_tensor(c0[:], p_misc[:, 0:ET], vec[:, V_BP:V_BP + ET], ALU.add).then_inc(row_step, 1)
                hv = h[:].rearrange("p t (i n) -> p t i n", n=TOK)
                nc.vector.tensor_tensor(hv[:, :, :, 0],
                                        bc(vec[:, V_CLS:V_CLS + ET].unsqueeze(2), [P, ET, IMGS]),
                                        bc(vec[:, V_POS:V_END].rearrange("p (t n) -> p t n", t=ET)[:, :, 0:1],
                                           [P, ET, IMGS]), ALU.add).then_inc(h_ready, 1)

                def centre(c):
                    dve.wait_ge(mean_ready, c + 1)
                    if c >= 2:
                        dve.wait_ge(var_ready, c - 1)
                    nc.vector.tensor_tensor(xc[:, c % 2], x[:, c],
                                            bc(p_mean[:, c % 2, 0:CP].unsqueeze(1), [P, PT6, CP]),
                                            ALU.subtract).then_inc(xc_ready, 1)

                centre(0)
                for c in range(CH):
                    if c + 1 < CH:
                        centre(c + 1)
                    dve.wait_ge(z_ready, c + 1)
                    dve.wait_ge(rstd1_ready, c + 1)
                    if c >= 1:
                        dve.wait_ge(zs_ready, 2 * c)
                    nc.vector.tensor_tensor(zr[:], p_z[:, :, 0:CP], bc(rstd1[:].unsqueeze(1), [P, ET, CP]),
                                            ALU.mult).then_inc(zr_ready, 1)
                    dve.wait_ge(mu2_ready, c + 1)
                    if c >= 1:
                        dve.wait_ge(sq2_ready, c)
                    nc.vector.tensor_tensor(xc2[:], zs[:], bc(p_mu2[:, 0:CP].unsqueeze(1), [P, ET, CP]),
                                            ALU.subtract).then_inc(xc2_ready, 1)
                    dve.wait_ge(rstd2_ready, c + 1)
                    if c >= 1:
                        dve.wait_ge(h_ready, 2 * c + 1)
                    nc.vector.tensor_tensor(z3[:], xc2[:], bc(rstd2[:].unsqueeze(1), [P, ET, CP]),
                                            ALU.mult).then_inc(z3_ready, 1)
                    dve.wait_ge(z3_ready, c + 1)
                    for t in range(ET):
                        nc.vector.scalar_tensor_tensor(
                            out=hv[:, t, c * CI:(c + 1) * CI, 1:TOK],
                            in0=z3[:, t].rearrange("p (i n) -> p i n", n=PATCH),
                            scalar=vec[:, V_G2 + t:V_G2 + t + 1],
                            in1=bc(posb[:, t, 1:TOK].unsqueeze(1), [P, CI, PATCH]),
                            op0=ALU.mult, op1=ALU.add).then_inc(h_ready, 1)
                dve.wait_ge(row_exp, 1)
                nc.vector.tensor_tensor(row[0:1, 72:73], row[0:1, 71:72], row[0:1, 70:71], ALU.subtract).then_inc(row_step, 1)
                dve.wait_ge(row_step, 5)
                nc.vector.tensor_scalar(row[0:1, 78:79], row[0:1, 72:73], -(0.8 - 0.6 * math.exp(0.0)), None,
                                        ALU.add).then_inc(row_step, 1)
                dve.wait_ge(row_bc, 1)
                nc.vector.tensor_copy(K["neglam"][:], p_mean[:, 0, 0:2]).then_inc(row_step, 1)
                dve.wait_ge(row_step, 7)
                nc.vector.tensor_scalar(K["mask0"][:], cs[:, C_MASK:C_MASK + HT], float(HD) ** -0.5, None,
                                        ALU.mult).then_inc(row_step, 1)
                nc.vector.tensor_scalar(K["mask1"][:], cs[:, C_MASK:C_MASK + HT], K["neglam"][:, 1:2], None,
                                        ALU.mult).then_inc(row_step, 1)
                dve.wait_ge(ffw_in, 48)
                for m in range(3):
                    blocks = raw[:, m].rearrange("p (b n) -> p b n", n=BLK)
                    nc.vector.tensor_reduce(wmax[:, m], blocks, AX.X, ALU.max, apply_absolute_value=True).then_inc(wg_ready, 1)
                dve.wait_ge(wg_ready, PT6 + 3)
                nc.vector.tensor_scalar(wsc[:], wmax[:], 1.0 / 7.0, 1e-12, ALU.mult, ALU.max).then_inc(wg_ready, 1)
                dve.wait_ge(wg_ready, PT6 + 4)
                nc.vector.reciprocal(wrs[:], wsc[:]).then_inc(wg_ready, 1)
                dve.wait_ge(wg_ready, PT6 + 5)
                for m in range(3):
                    blocks = raw[:, m].rearrange("p (b n) -> p b n", n=BLK)
                    ints = wint[:].rearrange("p (b n) -> p b n", n=BLK)
                    if m:
                        dve.wait_ge(deq, 3 * m)
                    nc.vector.tensor_tensor(ints, blocks, bc(wrs[:, m].unsqueeze(2), [P, 48, BLK]), ALU.mult).then_inc(deq, 2)
                    dve.wait_ge(deq, 3 * m + 2)
                    nc.vector.tensor_tensor(wdq[:, m].rearrange("p (b n) -> p b n", n=BLK), ints,
                                            bc(wsc[:, m].unsqueeze(2), [P, 48, BLK]), ALU.mult).then_inc(deq, 1)


def layernorm(nc, K, name):
    h, xn = K["h"], K["xn"]
    with ExitStack() as st:
        def sb(n, shape, dt=F32):
            return st.enter_context(nc.sbuf_tensor(f"{name}_{n}", shape, dt))

        def sem(n):
            return st.enter_context(nc.semaphore(f"{name}_{n}"))

        xc = sb("xc", [P, CH, ET, CT])
        sq = sb("sq", [P, CH, ET, CT])
        lnv = sb("lnv", [P, CH, CT])
        rstd = sb("rstd", [P, CH, CT])
        p_mu = st.enter_context(nc.psum_tensor(f"{name}_mu", [P, CH, 512], F32))
        p_var = st.enter_context(nc.psum_tensor(f"{name}_var", [P, CH, 512], F32))
        mean_ready, centred, squared = sem("mean_ready"), sem("centred"), sem("squared")
        var_ready, logged, rstd_ready = sem("var_ready"), sem("logged"), sem("rstd_ready")
        xn_ready = sem("xn_ready")

        def cols(c):
            return slice(c * CT, (c + 1) * CT)

        with nc.Block() as block:
            @block.tensor
            def _(pe):
                for c in range(CH):
                    for k in range(ET):
                        last = nc.tensor.matmul(p_mu[:, c, 0:CT], K["mean256"][:], h[:, k, cols(c)],
                                                start=(k == 0), stop=(k == ET - 1))
                    last.then_inc(mean_ready, 1)
                for c in range(CH):
                    pe.wait_ge(squared, c + 1)
                    for k in range(ET):
                        last = nc.tensor.matmul(p_var[:, c, 0:CT], K["mean256"][:], sq[:, c, k, :],
                                                start=(k == 0), stop=(k == ET - 1))
                    last.then_inc(var_ready, 1)

            @block.vector
            def _(dve):
                for c in range(CH):
                    dve.wait_ge(mean_ready, c + 1)
                    nc.vector.tensor_tensor(xc[:, c], h[:, :, cols(c)], bc(p_mu[:, c, 0:CT].unsqueeze(1), [P, ET, CT]),
                                            ALU.subtract).then_inc(centred, 1)
                for c in range(CH):
                    dve.wait_ge(rstd_ready, c + 1)
                    nc.vector.tensor_tensor(xn[:, :, cols(c)], xc[:, c], bc(rstd[:, c].unsqueeze(1), [P, ET, CT]),
                                            ALU.mult).then_inc(xn_ready, 1)

            @block.scalar
            def _(act):
                for c in range(CH):
                    act.wait_ge(centred, c + 1)
                    nc.scalar.activation(sq[:, c], xc[:, c], ACT.Square).then_inc(squared, 1)
                for c in range(CH):
                    act.wait_ge(var_ready, c + 1)
                    nc.scalar.activation(lnv[:, c], p_var[:, c, 0:CT], ACT.Ln, bias=K["eps"][:, 0:1]).then_inc(logged, 1)
                    act.wait_ge(logged, c + 1)
                    nc.scalar.activation(rstd[:, c], lnv[:, c], ACT.Exp, scale=-0.5).then_inc(rstd_ready, 1)


def diff_attention(nc, K):
    h, xn, cs, ident = K["h"], K["xn"], K["cst"], K["ident"]
    NU = ET * PAIRS
    BW = HT * TOK
    with ExitStack() as st:
        def sb(n, shape, dt=F32):
            return st.enter_context(nc.sbuf_tensor(f"da_{n}", shape, dt))

        def ps(n, shape):
            return st.enter_context(nc.psum_tensor(f"da_{n}", shape, F32))

        def sem(n):
            return st.enter_context(nc.semaphore(f"da_{n}"))

        xg, vx = K["xg"], K["vx"]
        pr = K["pr"][:].rearrange("p (s a b) -> p s a b", s=4, b=GAP)
        cos_t = sb("cost", [P, 2, 2, CT])
        sin_t = sb("sint", [P, 2, 2, CT])
        qr = sb("qr", [P, ET, 2, CT])
        kr = sb("kr", [P, ET, 2, CT])
        kx = sb("kx", [P, ET, 2, CI, HT, TOK])
        vt = sb("vt", [P, PAIRS, 512])
        ex = sb("ex", [P, 4, 2 * HT, TOK])
        pts = sb("pts", [P, 2, 4 * PW])
        ot = sb("ot", [P, 4, CT])
        mx = sb("mx", [P, 2, 2 * HT])
        sm = sb("sm", [P, 2, 2 * HT])
        rc = sb("rc", [P, 4, 2 * HT])

        p_s = ps("p_s", [P, 2, 2, 512])
        p_t = ps("p_t", [P, 512])
        p_o = ps("p_o", [P, 512])
        p_v = ps("p_v", [P, 2, 512])

        xg_ready = sem("xg_ready")
        qk_ready = sem("qk_ready")
        rot_ready = sem("rot_ready")
        rot_used = sem("rot_used")
        kx_dve = sem("kx_dve")
        kx_act = sem("kx_act")
        v_ready = sem("v_ready")
        vt_ready = sem("vt_ready")
        vx_ready = sem("vx_ready")
        s_ready = sem("s_ready")
        max_ready = sem("max_ready")
        sub_ready = sem("sub_ready")
        exp_ready = sem("exp_ready")
        sum_ready = sem("sum_ready")
        inv_ready = sem("inv_ready")
        rc_ready = sem("rc_ready")
        norm_ready = sem("norm_ready")
        p_ready = sem("p_ready")
        pt_ready = sem("pt_ready")
        pts_ready = sem("pts_ready")
        pv_ready = sem("pv_ready")
        ot_ready = sem("ot_ready")
        y_ready = sem("y_ready")
        h_done = sem("h_done")

        JOBS = [("k", 0), ("q", 0), ("k", 1), ("q", 1)]

        def span(c):
            return bass.ds(c * CT, CT)

        with nc.Block() as block:
            @block.gpsimd
            def _(pool):
                for sm_ in (sub_ready, rot_used, pv_ready, h_done, pts_ready, ot_ready, pt_ready, p_ready, y_ready,
                            vx_ready):
                    pool.sem_inc(sm_, 1)

                def jobs(c):
                    for j, (which, t) in enumerate(JOBS):
                        dst = kr if which == "k" else qr
                        pool.wait_ge(rot_ready, c * 8 + 2 * j + 2)
                        nc.gpsimd.tensor_tensor(dst[:, t, 0], cos_t[:, j % 2, 0], sin_t[:, j % 2, 1],
                                                ALU.subtract).then_inc(rot_used, 1)
                        nc.gpsimd.tensor_tensor(dst[:, t, 1], cos_t[:, j % 2, 1], sin_t[:, j % 2, 0],
                                                ALU.add).then_inc(rot_used, 1)

                def units(c):
                    for u in range(NU):
                        e = ex[0:PW, u % 4]
                        pool.wait_ge(rc_ready, c * NU + u + 1)
                        nc.gpsimd.tensor_tensor(e, e, bc(rc[0:PW, u % 4].unsqueeze(2), [PW, 2 * HT, TOK]),
                                                ALU.mult).then_inc(norm_ready, 1)
                        pool.wait_ge(norm_ready, c * NU + u + 1)
                        if u >= 3:
                            pool.wait_ge(pt_ready, c * NU + u - 3 + 1)
                        else:
                            pool.wait_ge(pt_ready, c * NU + 1)
                        nc.gpsimd.tensor_tensor(pr[0:PW, u % 4, :, 0:TOK], e[:, 0:HT], e[:, HT:2 * HT],
                                                ALU.add).then_inc(p_ready, 1)

                jobs(0)
                with pool.Fori(0, CH - 1) as i:
                    units(i)
                    jobs(i + 1)
                units(CH - 1)

            @block.sync
            def _(sp):
                def jobs(c):
                    for p in range(PAIRS):
                        sp.wait_ge(vt_ready, c * PAIRS + p + 1)
                        for m in range(2):
                            for par in range(2):
                                sp.dma_start(vx[GAP * par:GAP * par + TOK, 2 * p + m, par, :],
                                             vt[GAP * m:GAP * m + TOK, p, par * 256:(par + 1) * 256]).then_inc(vx_ready, 16)

                jobs(0)
                with sp.Fori(1, CH) as i:
                    jobs(i)

            @block.tensor
            def _(pe):
                def job(c, j):
                    which, t = JOBS[j]
                    if j < 2:
                        pe.wait_ge(sub_ready, c * NU + 1)
                    else:
                        pe.wait_ge(rot_ready, c * 8 + 2 * (j - 2) + 2)
                    for half in range(2):
                        o = (2 * ED if which == "k" else 0) + half * ED + t * P
                        for k in range(ET):
                            last = nc.tensor.matmul(p_s[:, j % 2, half, 0:CT], K["wqk"][:, k, o:o + P],
                                                    xn[:, k, span(c)], start=(k == 0), stop=(k == ET - 1))
                    last.then_inc(qk_ready, 1)

                def values(c, loop):
                    pe.wait_ge(xg_ready, c + 1)
                    if loop:
                        pe.wait_ge(h_done, c)
                    for p in range(PAIRS):
                        if p >= 2:
                            pe.wait_ge(vt_ready, c * PAIRS + p - 1)
                        for k in range(ET):
                            both = xg[:, k, 2 * p:2 * p + 2, :].rearrange("p a b -> p (a b)")
                            last = nc.tensor.matmul(p_v[0:PW, p % 2, :], both[:, 0:PW], K["wv"][:, k, :],
                                                    start=(k == 0), stop=(k == ET - 1))
                        last.then_inc(v_ready, 1)

                def scores(c, u):
                    t, p = u // PAIRS, u % PAIRS
                    if u < 2:
                        pe.wait_ge(rot_ready, c * 8 + 2 * (u + 2) + 2)
                    else:
                        pe.wait_ge(sub_ready, c * NU + u - 1 + 1)
                    if p == 0:
                        pe.wait_ge(kx_dve, c * ET + t + 1)
                        pe.wait_ge(kx_act, c * ET + t + 1)
                        pe.wait_ge(rot_used, c * 8 + 4 * t + 4 + 1)
                    for m in range(2):
                        img = 2 * p + m
                        for half in range(2):
                            last = nc.tensor.matmul(
                                p_s[GAP * m:GAP * m + TOK, u % 2, half, 0:BW],
                                qr[:, t, half, img * TOK:(img + 1) * TOK],
                                kx[:, t, half, img].rearrange("p a b -> p (a b)"), start=True, stop=True)
                    last.then_inc(s_ready, 1)

                def turn(c, u):
                    pe.wait_ge(p_ready, c * NU + u + 1 + 1)
                    pe.wait_ge(pts_ready, c * NU + u + 1)
                    for hp in range(4):
                        src = pr[0:PW, u % 4, 2 * hp:2 * hp + 2, :].rearrange("p a b -> p (a b)")
                        last = nc.tensor.transpose(p_t[0:PW, hp * PW:(hp + 1) * PW], src[:, 0:PW], ident[0:PW, 0:PW])
                    last.then_inc(pt_ready, 1)

                def attend(c, u):
                    t, p = u // PAIRS, u % PAIRS
                    if u == 0:
                        pe.wait_ge(vx_ready, (c + 1) * (PAIRS * 4 * 16) + 1)
                    pe.wait_ge(pts_ready, c * NU + u + 1 + 1)
                    pe.wait_ge(ot_ready, c * NU + u + 1)
                    for m in range(2):
                        for hl in range(HT):
                            hg = t * HT + hl
                            last = nc.tensor.matmul(
                                p_o[32 * (hl % 4):32 * (hl % 4) + 32,
                                    (hl // 4) * 2 * TOK + m * TOK:(hl // 4) * 2 * TOK + (m + 1) * TOK],
                                vx[0:PW, 2 * p + m, hl % 2, (hg // 2) * 32:(hg // 2 + 1) * 32],
                                pts[0:PW, u % 2, (hl // 2) * PW + GAP * m:(hl // 2) * PW + GAP * m + TOK],
                                start=True, stop=True)
                    last.then_inc(pv_ready, 1)

                def project(c, more):
                    pe.wait_ge(ot_ready, c * NU + NU + 1)
                    if more:
                        pe.wait_ge(vt_ready, (c + 2) * PAIRS)
                    for t in range(ET):
                        for k in range(4):
                            last = nc.tensor.matmul(p_v[:, t, 0:CT], K["wp"][:, k, t * P:(t + 1) * P],
                                                    ot[:, k, :], start=(k == 0), stop=(k == 3))
                    last.then_inc(y_ready, 1)

                def units(c, more):
                    for s in range(NU + 3):
                        if s < NU:
                            scores(c, s)
                        elif more:
                            job(c + 1, s - NU)
                        if 2 <= s < NU + 2:
                            turn(c, s - 2)
                        if s >= 3:
                            attend(c, s - 3)
                    if more:
                        job(c + 1, 3)
                        values(c + 1, True)
                    project(c, more)

                pe.wait_ge(K["loaded"], 80)
                for j in range(4):
                    job(0, j)
                values(0, False)
                with pe.Fori(0, CH - 1) as i:
                    units(i, True)
                units(CH - 1, False)

            @block.scalar
            def _(act):
                def gather(c):
                    nc.scalar.copy(xg[:, :, :, 0:TOK],
                                   xn[:, :, span(c)].rearrange("p t (a b) -> p t a b", b=TOK)).then_inc(xg_ready, 1)

                def expand(c, t):
                    act.wait_ge(rot_used, c * 8 + 4 * t + 2 + 1)
                    for half in range(2):
                        for hh in range(4, HT):
                            last = nc.scalar.activation(
                                kx[:, t, half, :, hh, :], kr[:, t, half].rearrange("p (a b) -> p a b", b=TOK),
                                ACT.Copy, scale=K["mask0"][:, hh:hh + 1])
                    last.then_inc(kx_act, 1)

                def values(c):
                    act.wait_ge(vx_ready, c * (PAIRS * 4 * 16) + 1)
                    for p in range(PAIRS):
                        act.wait_ge(v_ready, c * PAIRS + p + 1)
                        nc.scalar.copy(vt[0:PW, p, :], p_v[0:PW, p % 2, :]).then_inc(vt_ready, 1)

                def units(c, more):
                    for s in range(NU + 3):
                        if s < NU:
                            act.wait_ge(sub_ready, c * NU + s + 1 + 1)
                            nc.scalar.activation(ex[0:PW, s % 4], ex[0:PW, s % 4], ACT.Exp).then_inc(exp_ready, 1)
                        if more and s == 1:
                            act.wait_ge(v_ready, (c + 1) * PAIRS)
                            gather(c + 1)
                        if 2 <= s < NU + 2:
                            u = s - 2
                            act.wait_ge(pt_ready, c * NU + u + 1 + 1)
                            nc.scalar.copy(pts[0:PW, u % 2], p_t[0:PW, 0:4 * PW]).then_inc(pts_ready, 1)
                        if s >= 3:
                            u = s - 3
                            t, p = u // PAIRS, u % PAIRS
                            act.wait_ge(pv_ready, c * NU + u + 1 + 1)
                            act.wait_ge(y_ready, c + 1)
                            nc.scalar.copy(ot[:, 2 * t:2 * t + 2, p * 2 * TOK:(p + 1) * 2 * TOK],
                                           p_o[:, 0:4 * TOK].rearrange("p (a b) -> p a b", a=2)).then_inc(ot_ready, 1)
                    if more:
                        expand(c + 1, 0)
                        values(c + 1)
                        expand(c + 1, 1)

                nc.scalar.preload_act_table_set("natural_log_exp_and_others")
                gather(0)
                expand(0, 0)
                values(0)
                expand(0, 1)
                with act.Fori(0, CH - 1) as i:
                    units(i, True)
                units(CH - 1, False)

            @block.vector
            def _(dve):
                def rotate(c, j):
                    dve.wait_ge(qk_ready, c * 4 + j + 1)
                    dve.wait_ge(rot_used, c * 8 + (2 * j - 2 if j >= 2 else 0) + 1)
                    for dst, col in ((cos_t, C_COS), (sin_t, C_SIN)):
                        table = cs[:, col:col + TOK].unsqueeze(1)
                        for half in range(2):
                            last = nc.vector.tensor_tensor(
                                dst[:, j % 2, half].rearrange("p (a b) -> p a b", b=TOK),
                                p_s[:, j % 2, half, 0:CT].rearrange("p (a b) -> p a b", b=TOK),
                                bc(table, [P, CI, TOK]), ALU.mult)
                        last.then_inc(rot_ready, 1)

                def expand(c, t):
                    dve.wait_ge(rot_used, c * 8 + 4 * t + 2 + 1)
                    for half in range(2):
                        for hh in range(4):
                            last = nc.vector.tensor_scalar(
                                kx[:, t, half, :, hh, :], kr[:, t, half].rearrange("p (a b) -> p a b", b=TOK),
                                K["mask0"][:, hh:hh + 1], None, ALU.mult)
                    last.then_inc(kx_dve, 1)

                def jobs(c):
                    rotate(c, 0)
                    rotate(c, 1)
                    expand(c, 0)
                    rotate(c, 2)
                    rotate(c, 3)
                    expand(c, 1)

                def units(c, more):
                    for s in range(NU + 1):
                        if s < NU:
                            dve.wait_ge(s_ready, c * NU + s + 1)
                            sc = p_s[0:PW, s % 2, :, 0:BW].rearrange("p a (b c) -> p a b c", c=TOK)
                            nc.vector.tensor_reduce(mx[0:PW, s % 2].rearrange("p (a b) -> p a b", a=2), sc,
                                                    AX.X, ALU.max).then_inc(max_ready, 1)
                            dve.wait_ge(max_ready, c * NU + s + 1)
                            dve.wait_ge(p_ready, c * NU + max(s - 3, 0) + 1)
                            nc.vector.tensor_tensor(
                                ex[0:PW, s % 4].rearrange("p (a b) c -> p a b c", a=2), sc,
                                bc(mx[0:PW, s % 2].rearrange("p (a b) -> p a b", a=2).unsqueeze(3), [PW, 2, HT, TOK]),
                                ALU.subtract).then_inc(sub_ready, 1)
                        if s >= 1:
                            u = s - 1
                            dve.wait_ge(exp_ready, c * NU + u + 1)
                            nc.vector.tensor_reduce(sm[0:PW, u % 2], ex[0:PW, u % 4], AX.X, ALU.add).then_inc(sum_ready, 1)
                            dve.wait_ge(sum_ready, c * NU + u + 1)
                            nc.vector.reciprocal(rc[0:PW, u % 4], sm[0:PW, u % 2]).then_inc(inv_ready, 1)
                            dve.wait_ge(inv_ready, c * NU + u + 1)
                            nc.vector.tensor_scalar(rc[0:PW, u % 4, HT:2 * HT], rc[0:PW, u % 4, HT:2 * HT],
                                                    K["neglam"][0:PW, 0:1], None, ALU.mult).then_inc(rc_ready, 1)
                    if more:
                        jobs(c + 1)
                    dve.wait_ge(y_ready, c + 1 + 1)
                    nc.vector.tensor_tensor(h[:, :, span(c)], h[:, :, span(c)], p_v[:, :, 0:CT], ALU.add).then_inc(h_done, 1)

                jobs(0)
                with dve.Fori(0, CH - 1) as i:
                    units(i, True)
                units(CH - 1, False)


def quantised_ffn(nc, K):
    h, xn, ident = K["h"], K["xn"], K["ident"]
    with ExitStack() as st:
        def sb(n, shape, dt=F32):
            return st.enter_context(nc.sbuf_tensor(f"ff_{n}", shape, dt))

        def sem(n):
            return st.enter_context(nc.semaphore(f"ff_{n}"))

        gate = sb("gate", [P, IT, NT])
        up = sb("up", [P, IT, NT])
        gq = sb("gq", [P, IT, NT], I16)
        uq = sb("uq", [P, IT, NT], I16)
        sg = sb("sg", [P, 2, NT])
        sq = sb("sq", [P, 2, NT], U16)
        xq = sb("xq", [P, ET, NT], I16)
        oq = sb("oq", [P, 2, IT, CT], I16)
        of = gate[:].rearrange("p a b -> p (a b)")[:, 0:2 * IT * CT].rearrange("p (s a b) -> p s a b", s=2, b=CT)
        part = sb("part", [P, 2, IT * CH])
        pmax = sb("pmax", [P, 8])
        grow = sb("grow", [1, 8])
        gmax = sb("gmax", [P, 8])
        sc = sb("sc", [P, 32])
        onesr = sb("onesr", [1, P])

        p_t = st.enter_context(nc.psum_tensor("ff_t", [P, 512], F32))
        p_b = st.enter_context(nc.psum_tensor("ff_b", [P, 512], F32))
        p_g = st.enter_context(nc.psum_tensor("ff_g", [P, 2, 2, 512], F32))

        ones_ready = sem("ones_ready")
        xmax = sem("xmax")
        pm_ready = sem("pm_ready")
        turned = sem("turned")
        row_ready = sem("row_ready")
        spread = sem("spread")
        scale = sem("scale")
        xq_int = sem("xq_int")
        x_ready = sem("x_ready")
        gu_ready = sem("gu_ready")
        gu_copied = sem("gu_copied")
        gu_max = sem("gu_max")
        gq_ready = sem("gq_ready")
        uq_ready = sem("uq_ready")
        sg_ready = sem("sg_ready")
        sq_ready = sem("sq_ready")
        act_ready = sem("act_ready")
        act_max = sem("act_max")
        aq_ready = sem("aq_ready")
        o_ready = sem("o_ready")
        o_max = sem("o_max")
        oq_ready = sem("oq_ready")
        of_ready = sem("of_ready")
        y_ready = sem("y_ready")
        h_done = sem("h_done")

        QM = 1.0 / 32767.0

        def spread_max(pe, n):
            pe.wait_ge(pm_ready, n + 1)
            w = 2 if n == 1 else 1
            c = PMC[n]
            for j in range(w):
                last = nc.tensor.transpose(p_t[0:1, j * P:(j + 1) * P], pmax[:, c + j:c + j + 1], ident)
            last.then_inc(turned, 1)
            pe.wait_ge(row_ready, n + 1)
            nc.tensor.matmul(p_b[:, c:c + w], onesr[0:1, :], grow[0:1, c:c + w], start=True, stop=True).then_inc(spread, 1)

        PMC = [0, 1, 3, 4]

        def cols(c):
            return slice(c * CT, (c + 1) * CT)

        with nc.Block() as block:
            @block.tensor
            def _(pe):
                pe.wait_ge(ones_ready, 1)
                spread_max(pe, 0)
                for c in range(CH):
                    pe.wait_ge(x_ready, c + 1)
                    for o in range(IT):
                        n = c * IT + o
                        if n >= 2:
                            pe.wait_ge(gu_copied, n - 1)
                            pe.wait_ge(gu_max, n - 1)
                        for m, wt in enumerate((K["wgate"], K["wup"])):
                            for k in range(ET):
                                last = nc.tensor.matmul(p_g[:, n % 2, m, 0:CT], wt[:, k, o * P:(o + 1) * P],
                                                        xn[:, k, cols(c)], start=(k == 0), stop=(k == ET - 1))
                        last.then_inc(gu_ready, 1)
                spread_max(pe, 1)
                spread_max(pe, 2)
                spread_max(pe, 3)
                for c in range(CH):
                    pe.wait_ge(of_ready, c + 1)
                    if c >= 2:
                        pe.wait_ge(h_done, c - 1)
                    for t in range(ET):
                        for k in range(IT):
                            last = nc.tensor.matmul(p_g[:, c % 2, t, 0:CT], K["wdown"][:, k, t * P:(t + 1) * P],
                                                    of[:, c % 2, k], start=(k == 0), stop=(k == IT - 1))
                    last.then_inc(y_ready, 1)

            @block.scalar
            def _(act):
                nc.scalar.preload_act_table_set("sigmoid_and_others")
                for n in range(CH * IT):
                    c, o = n // IT, n % IT
                    act.wait_ge(gu_ready, n + 1)
                    act.wait_ge(gu_max, n + 1)
                    nc.scalar.copy(gate[:, o, cols(c)], p_g[:, n % 2, 0, 0:CT])
                    nc.scalar.copy(up[:, o, cols(c)], p_g[:, n % 2, 1, 0:CT]).then_inc(gu_copied, 1)
                act.wait_ge(scale, 10)
                for o in range(IT):
                    act.wait_ge(gq_ready, o + 1)
                    if o >= 2:
                        act.wait_ge(sq_ready, o - 1)
                    nc.scalar.activation(sg[:, o % 2], gq[:, o], ACT.Sigmoid, scale=sc[:, 6:7]).then_inc(sg_ready, 1)
                nc.scalar.preload_act_table_set("natural_log_exp_and_others")
                act.wait_ge(gu_copied, CH * IT)
                for o in range(IT):
                    nc.scalar.activation(uq[:, o], up[:, o], ACT.Copy, scale=sc[:, 9:10]).then_inc(uq_ready, 1)

            @block.vector
            def _(dve):
                nc.vector.memset(onesr[:], 1.0).then_inc(ones_ready, 1)
                steps = [0]

                def link(ins):
                    steps[0] += 1
                    ins.then_inc(scale, 1)
                    dve.wait_ge(scale, steps[0])

                def global_max(n):
                    w, c = (2 if n == 1 else 1), PMC[n]
                    dve.wait_ge(turned, n + 1)
                    nc.vector.tensor_reduce(grow[0:1, c:c + w], p_t[0:1, 0:w * P].rearrange("p (a b) -> p a b", a=w),
                                            AX.X, ALU.max).then_inc(row_ready, 1)
                    dve.wait_ge(spread, n + 1)
                    return p_b[:, c:c + w]

                nc.vector.tensor_reduce(pmax[:, 0:1], xn[:].rearrange("p t n -> p (t n)"), AX.X, ALU.max,
                                        apply_absolute_value=True).then_inc(pm_ready, 1)
                g = global_max(0)
                link(nc.vector.tensor_scalar(sc[:, 0:1], g, QM, 1e-12, ALU.mult, ALU.max))
                link(nc.vector.reciprocal(sc[:, 1:2], sc[:, 0:1]))
                for c in range(CH):
                    nc.vector.tensor_scalar(xq[:, :, cols(c)], xn[:, :, cols(c)], sc[:, 1:2], None,
                                            ALU.mult).then_inc(xq_int, 1)
                    dve.wait_ge(xq_int, c + 1)
                    nc.vector.tensor_copy(xn[:, :, cols(c)], xq[:, :, cols(c)]).then_inc(x_ready, 1)
                for n in range(CH * IT):
                    dve.wait_ge(gu_ready, n + 1)
                    nc.vector.tensor_reduce(part[:, :, n], p_g[:, n % 2, :, 0:CT], AX.X, ALU.max,
                                            apply_absolute_value=True).then_inc(gu_max, 1)
                dve.wait_ge(gu_max, CH * IT)
                nc.vector.tensor_reduce(pmax[:, 1:3], part[:], AX.X, ALU.max).then_inc(pm_ready, 1)
                g = global_max(1)
                link(nc.vector.tensor_scalar(sc[:, 2:4], g, sc[:, 0:1], None, ALU.mult))
                link(nc.vector.tensor_scalar(sc[:, 6:8], sc[:, 2:4], QM, 1e-12, ALU.mult, ALU.max))
                link(nc.vector.reciprocal(sc[:, 4:6], sc[:, 6:8]))
                link(nc.vector.tensor_scalar(sc[:, 8:10], sc[:, 4:6], sc[:, 0:1], None, ALU.mult))
                dve.wait_ge(gu_copied, CH * IT)
                link(nc.vector.tensor_scalar(sc[:, 10:11], sc[:, 6:7], 1.0 / 65536.0, None, ALU.mult))
                link(nc.vector.memset(sc[:, 11:12], 0.0))
                link(nc.vector.memset(sc[:, 12:13], 0.0))
                link(nc.vector.memset(sc[:, 13:14], 0.0))
                for o in range(IT + 2):
                    if o < IT:
                        nc.vector.tensor_scalar(gq[:, o], gate[:, o], sc[:, 8:9], None, ALU.mult).then_inc(gq_ready, 1)
                    if 1 <= o <= IT:
                        dve.wait_ge(sg_ready, o)
                        if o >= 3:
                            dve.wait_ge(act_ready, o - 2)
                        nc.vector.tensor_scalar(sq[:, (o - 1) % 2], sg[:, (o - 1) % 2], 65536.0, None,
                                                ALU.mult).then_inc(sq_ready, 1)
                    if o >= 2:
                        dve.wait_ge(sq_ready, o - 1)
                        dve.wait_ge(gq_ready, o - 1)
                        nc.vector.tensor_tensor(gate[:, o - 2], gq[:, o - 2], sq[:, (o - 2) % 2],
                                                ALU.mult).then_inc(act_ready, 1)
                        dve.wait_ge(act_ready, o - 1)
                        nc.vector.tensor_reduce(part[:, 0, o - 2:o - 1], gate[:, o - 2], AX.X, ALU.max,
                                                apply_absolute_value=True).then_inc(act_max, 1)
                dve.wait_ge(act_max, IT)
                nc.vector.tensor_reduce(pmax[:, 3:4], part[:, 0, 0:IT], AX.X, ALU.max).then_inc(pm_ready, 1)
                g = global_max(2)
                link(nc.vector.tensor_scalar(sc[:, 14:15], g, sc[:, 10:11], None, ALU.mult))
                link(nc.vector.tensor_scalar(sc[:, 15:16], sc[:, 14:15], QM, 1e-12, ALU.mult, ALU.max))
                link(nc.vector.reciprocal(sc[:, 16:17], sc[:, 15:16]))
                link(nc.vector.tensor_scalar(sc[:, 17:18], sc[:, 16:17], sc[:, 10:11], None, ALU.mult))
                link(nc.vector.tensor_tensor(sc[:, 18:19], sc[:, 15:16], sc[:, 7:8], ALU.mult))
                for o in range(IT):
                    dve.wait_ge(sg_ready, IT)
                    nc.vector.tensor_scalar(gq[:, o], gate[:, o], sc[:, 17:18], None, ALU.mult).then_inc(aq_ready, 1)
                    dve.wait_ge(aq_ready, o + 1)
                    dve.wait_ge(uq_ready, o + 1)
                    nc.vector.tensor_tensor(up[:, o], gq[:, o], uq[:, o], ALU.mult).then_inc(o_ready, 1)
                    dve.wait_ge(o_ready, o + 1)
                    nc.vector.tensor_reduce(part[:, 1, o:o + 1], up[:, o], AX.X, ALU.max,
                                            apply_absolute_value=True).then_inc(o_max, 1)
                dve.wait_ge(o_max, IT)
                nc.vector.tensor_reduce(pmax[:, 4:5], part[:, 1, 0:IT], AX.X, ALU.max).then_inc(pm_ready, 1)
                g = global_max(3)
                link(nc.vector.tensor_scalar(sc[:, 19:20], g, sc[:, 18:19], None, ALU.mult))
                link(nc.vector.tensor_scalar(sc[:, 20:21], sc[:, 19:20], QM, 1e-12, ALU.mult, ALU.max))
                link(nc.vector.reciprocal(sc[:, 21:22], sc[:, 20:21]))
                link(nc.vector.tensor_scalar(sc[:, 22:23], sc[:, 21:22], sc[:, 18:19], None, ALU.mult))
                for c in range(CH + 1):
                    if c < CH:
                        nc.vector.tensor_scalar(oq[:, c % 2], up[:, :, cols(c)], sc[:, 22:23], None,
                                                ALU.mult).then_inc(oq_ready, 1)
                        dve.wait_ge(oq_ready, c + 1)
                        if c >= 2:
                            dve.wait_ge(y_ready, c - 1)
                        nc.vector.tensor_copy(of[:, c % 2], oq[:, c % 2]).then_inc(of_ready, 1)
                    if c >= 1:
                        dve.wait_ge(y_ready, c)
                        if c < CH:
                            dve.wait_ge(of_ready, c + 1)
                        nc.vector.scalar_tensor_tensor(out=h[:, :, cols(c - 1)], in0=p_g[:, (c - 1) % 2, :, 0:CT],
                                                       scalar=sc[:, 20:21], in1=h[:, :, cols(c - 1)],
                                                       op0=ALU.mult, op1=ALU.add).then_inc(h_done, 1)


def cosine_attention(nc, K):
    h, xn, cs, ident = K["h"], K["xn"], K["cst"], K["ident"]
    NU = PAIRS
    BW = HT * TOK
    with ExitStack() as st:
        def sb(n, shape, dt=F32):
            return st.enter_context(nc.sbuf_tensor(f"ca_{n}", shape, dt))

        def ps(n, shape):
            return st.enter_context(nc.psum_tensor(f"ca_{n}", shape, F32))

        def sem(n):
            return st.enter_context(nc.semaphore(f"ca_{n}"))

        xg = K["xg"]
        pr = K["pr"][:].rearrange("p (s a b) -> p s a b", s=2, b=GAP)
        sq = sb("sq", [P, 2, ET, CT])
        ss = sb("ss", [P, 2, ET, CT])
        ls = sb("ls", [P, 2, ET, CT])
        inv = sb("inv", [P, 2, ET, CT])
        qn = sb("qn", [P, ET, CT])
        kn = sb("kn", [P, ET, CT])
        kx = sb("kx", [P, ET, CI, HT, TOK])
        vx = sb("vx", [P, CI, HT, 2, HD])
        vs = sb("vs", [P, PAIRS, HT, 2, HD])
        ex = sb("ex", [P, 4, HEADS, TOK])
        pts = sb("pts", [P, 2, 2, 4 * PW])
        mx = sb("mx", [P, 2, HEADS])
        sm = sb("sm", [P, 2, HEADS])
        rc = sb("rc", [P, 4, HEADS])

        p_s = ps("p_s", [P, 2, 2, 512])
        p_t = ps("p_t", [P, 512])
        p_o = ps("p_o", [P, 512])
        p_x = ps("p_x", [P, 2, 512])

        init = sem("init")
        xg_ready = sem("xg_ready")
        qk_ready = sem("qk_ready")
        sq_ready = sem("sq_ready")
        ss_ready = sem("ss_ready")
        ss_kept = sem("ss_kept")
        log_ready = sem("log_ready")
        inv_ready = sem("inv_ready")
        qk_normed = sem("qk_normed")
        kx_dve = sem("kx_dve")
        kx_act = sem("kx_act")
        v_ready = sem("v_ready")
        vs_ready = sem("vs_ready")
        vx_ready = sem("vx_ready")
        s_ready = sem("s_ready")
        max_ready = sem("max_ready")
        sub_ready = sem("sub_ready")
        exp_ready = sem("exp_ready")
        sum_ready = sem("sum_ready")
        rc_ready = sem("rc_ready")
        p_ready = sem("p_ready")
        pt_ready = sem("pt_ready")
        pts_ready = sem("pts_ready")
        pv_ready = sem("pv_ready")
        h_done = sem("h_done")


        def span(c):
            return bass.ds(c * CT, CT)

        with nc.Block() as block:
            @block.gpsimd
            def _(pool):
                nc.gpsimd.memset(vx[:], 0.0).then_inc(init, 1)
                nc.gpsimd.memset(vs[:], 0.0).then_inc(init, 1)
                for counter in (sub_ready, pv_ready, h_done, pts_ready, pt_ready, p_ready, vx_ready):
                    pool.sem_inc(counter, 1)

                def units(c):
                    for u in range(NU):
                        pool.wait_ge(rc_ready, c * NU + u + 1)
                        pool.wait_ge(pt_ready, (c * NU + max(u - 1, 0)) * 2 + 1)
                        nc.gpsimd.tensor_tensor(pr[0:PW, u % 2, :, 0:TOK], ex[0:PW, u % 4],
                                                bc(rc[0:PW, u % 4].unsqueeze(2), [PW, HEADS, TOK]),
                                                ALU.mult).then_inc(p_ready, 1)

                units(0)
                with pool.Fori(1, CH) as i:
                    units(i)

            @block.sync
            def _(sp):
                def send(c):
                    for b in range(2):
                        sp.wait_ge(vs_ready, c * 2 + b + 1)
                        sp.dma_start(vx[GAP:GAP + TOK, 4 * b:4 * b + 4:2], vs[0:TOK, 2 * b:2 * b + 2]).then_inc(vx_ready, 16)
                        sp.dma_start(vx[0:TOK, 4 * b + 1:4 * b + 4:2], vs[GAP:GAP + TOK, 2 * b:2 * b + 2]).then_inc(vx_ready, 16)

                sp.wait_ge(init, 2)
                send(0)
                with sp.Fori(1, CH) as i:
                    send(i)

            @block.tensor
            def _(pe):
                def job(c, j):
                    pe.wait_ge(sub_ready, c * NU + 1)
                    for t in range(ET):
                        o = (1 - j) * ED + t * P
                        for k in range(ET):
                            last = nc.tensor.matmul(p_s[:, j, t, 0:CT], K["w1qk"][:, k, o:o + P],
                                                    xn[:, k, span(c)], start=(k == 0), stop=(k == ET - 1))
                    last.then_inc(qk_ready, 1)

                def squares(c, j, first=False):
                    pe.wait_ge(sq_ready, c * 2 + j + 1)
                    if j:
                        pe.wait_ge(ss_kept, c * 2 + 1)
                    elif not first:
                        pe.wait_ge(vs_ready, c * 2)
                    for t in range(ET):
                        last = nc.tensor.matmul(p_x[:, t, 0:CT], cs[:, C_BD:C_BD + P], sq[:, j, t],
                                                start=True, stop=True)
                    last.then_inc(ss_ready, 1)

                def values(c):
                    pe.wait_ge(xg_ready, c + 1)
                    pe.wait_ge(ss_kept, c * 2 + 2)
                    for p in range(PAIRS):
                        for k in range(ET):
                            both = xg[:, k, 2 * p:2 * p + 2, :].rearrange("p a b -> p (a b)")
                            last = nc.tensor.matmul(p_x[0:PW, p // 2, (p % 2) * ED:(p % 2 + 1) * ED], both[:, 0:PW],
                                                    K["w1v"][:, k, :], start=(k == 0), stop=(k == ET - 1))
                    last.then_inc(v_ready, 1)

                def scores(c, u):
                    if u < 2:
                        pe.wait_ge(qk_normed, c * 2 + 2)
                    else:
                        pe.wait_ge(sub_ready, c * NU + u - 1 + 1)
                    if u == 0:
                        pe.wait_ge(kx_dve, c + 1)
                        pe.wait_ge(kx_act, c + 1)
                    for m in range(2):
                        img = 2 * u + m
                        for t in range(ET):
                            last = nc.tensor.matmul(p_s[GAP * m:GAP * m + TOK, u % 2, t, 0:BW],
                                                    qn[:, t, img * TOK:(img + 1) * TOK],
                                                    kx[:, t, img].rearrange("p a b -> p (a b)"), start=True, stop=True)
                    last.then_inc(s_ready, 1)

                def turn(c, u, b):
                    if b == 0:
                        pe.wait_ge(p_ready, c * NU + u + 1 + 1)
                    pe.wait_ge(pts_ready, (c * NU + u) * 2 + b + 1)
                    for hq in range(4):
                        src = pr[0:PW, u % 2, 8 * b + 2 * hq:8 * b + 2 * hq + 2, :].rearrange("p a b -> p (a b)")
                        last = nc.tensor.transpose(p_t[0:PW, hq * PW:(hq + 1) * PW], src[:, 0:PW], ident[0:PW, 0:PW])
                    last.then_inc(pt_ready, 1)

                def attend(c, u):
                    if u == 0:
                        pe.wait_ge(vx_ready, (c + 1) * 64 + 1)
                    pe.wait_ge(pts_ready, (c * NU + u) * 2 + 2 + 1)
                    pe.wait_ge(h_done, c * NU + u + 1)
                    for m in range(2):
                        for hp in range(HT):
                            col = (hp // 4) * 2 * TOK + m * TOK
                            last = nc.tensor.matmul(
                                p_o[32 * (hp % 4):32 * (hp % 4) + 32, col:col + TOK],
                                vx[0:PW, 2 * u + m, hp].rearrange("p a b -> p (a b)"),
                                pts[0:PW, u % 2, hp // 4, (hp % 4) * PW + GAP * m:(hp % 4) * PW + GAP * m + TOK],
                                start=True, stop=True)
                    last.then_inc(pv_ready, 1)

                def units(c, more):
                    for s in range(NU + 3):
                        if s < NU:
                            scores(c, s)
                        elif more and s < NU + 2:
                            job(c + 1, s - NU)
                        if 2 <= s < NU + 2:
                            turn(c, s - 2, 0)
                        if more and s > NU:
                            squares(c + 1, s - NU - 1)
                        if s >= 3:
                            attend(c, s - 3)
                        if 2 <= s < NU + 2:
                            turn(c, s - 2, 1)
                    if more:
                        values(c + 1)

                pe.wait_ge(init, 2)
                for j in range(2):
                    job(0, j)
                for j in range(2):
                    squares(0, j, first=True)
                values(0)
                with pe.Fori(0, CH - 1) as i:
                    units(i, True)
                units(CH - 1, False)

            @block.scalar
            def _(act):
                def gather(c):
                    nc.scalar.copy(xg[:, :, :, 0:TOK],
                                   xn[:, :, span(c)].rearrange("p t (a b) -> p t a b", b=TOK)).then_inc(xg_ready, 1)

                def square(c, j):
                    act.wait_ge(qk_ready, c * 2 + j + 1)
                    nc.scalar.activation(sq[:, j], p_s[:, j, :, 0:CT], ACT.Square).then_inc(sq_ready, 1)

                def inverse(c, j):
                    act.wait_ge(ss_kept, c * 2 + j + 1)
                    nc.scalar.activation(ls[:, j], ss[:, j], ACT.Ln, scale=L2_SCALE).then_inc(log_ready, 1)
                    act.wait_ge(log_ready, c * 2 + j + 1)
                    nc.scalar.activation(inv[:, j], ls[:, j], ACT.Exp, scale=-0.5,
                                         bias=K["eps"][:, 1:2]).then_inc(inv_ready, 1)

                def expand(c):
                    act.wait_ge(qk_normed, c * 2 + 1)
                    for t in range(ET):
                        for hh in range(5, HT):
                            last = nc.scalar.activation(kx[:, t, :, hh, :], kn[:, t].rearrange("p (a b) -> p a b", b=TOK),
                                                        ACT.Copy, scale=K["mask1"][:, hh:hh + 1])
                    last.then_inc(kx_act, 1)

                def values(c, b):
                    v = p_x[:, b].rearrange("p (q a b c) -> p q a b c", q=2, a=2, c=HD)
                    im = slice(4 * b, 4 * b + 4, 2)
                    im1 = slice(4 * b + 1, 4 * b + 4, 2)
                    pp = slice(2 * b, 2 * b + 2)
                    nc.scalar.copy(vx[0:TOK, im, :, 0, :], v[0:TOK, :, 0])
                    nc.scalar.copy(vs[0:TOK, pp, :, 1, :], v[0:TOK, :, 1])
                    nc.scalar.copy(vx[GAP:PW, im1, :, 1, :], v[GAP:PW, :, 1])
                    nc.scalar.copy(vs[GAP:PW, pp, :, 0, :], v[GAP:PW, :, 0]).then_inc(vs_ready, 1)

                def units(c, more):
                    for s in range(NU + 2):
                        if s < NU:
                            act.wait_ge(sub_ready, c * NU + s + 1 + 1)
                            nc.scalar.activation(ex[0:PW, s % 4], ex[0:PW, s % 4], ACT.Exp).then_inc(exp_ready, 1)
                        elif more:
                            square(c + 1, s - NU)
                        if s == 0:
                            act.wait_ge(v_ready, c + 1)
                            act.wait_ge(vx_ready, c * 64 + 1)
                            act.wait_ge(pv_ready, c * NU + 1)
                        if s < 2:
                            values(c, s)
                        if more and s == 1:
                            gather(c + 1)
                        if s >= 2:
                            u = s - 2
                            for b in range(2):
                                act.wait_ge(pt_ready, (c * NU + u) * 2 + b + 1 + 1)
                                nc.scalar.copy(pts[0:PW, u % 2, b], p_t[0:PW, 0:4 * PW]).then_inc(pts_ready, 1)
                    if more:
                        for j in range(2):
                            inverse(c + 1, j)
                        expand(c + 1)

                act.wait_ge(init, 2)
                gather(0)
                for j in range(2):
                    square(0, j)
                for j in range(2):
                    inverse(0, j)
                expand(0)
                with act.Fori(0, CH - 1) as i:
                    units(i, True)
                units(CH - 1, False)

            @block.vector
            def _(dve):
                def keep(c, j):
                    dve.wait_ge(ss_ready, c * 2 + j + 1)
                    nc.vector.tensor_scalar(ss[:, j], p_x[:, :, 0:CT], 1e-24, None, ALU.max).then_inc(ss_kept, 1)

                def normalise(c, j):
                    dve.wait_ge(inv_ready, c * 2 + j + 1)
                    nc.vector.tensor_tensor((kn, qn)[j][:], p_s[:, j, :, 0:CT], inv[:, j], ALU.mult).then_inc(qk_normed, 1)

                def expand(c):
                    dve.wait_ge(qk_normed, c * 2 + 1)
                    for t in range(ET):
                        for hh in range(5):
                            last = nc.vector.tensor_scalar(
                                kx[:, t, :, hh, :], kn[:, t].rearrange("p (a b) -> p a b", b=TOK),
                                K["mask1"][:, hh:hh + 1], None, ALU.mult)
                    last.then_inc(kx_dve, 1)

                def add(c, u):
                    dve.wait_ge(pv_ready, c * NU + u + 1 + 1)
                    pair = bass.ds(c * CT + u * 2 * TOK, 2 * TOK)
                    nc.vector.tensor_tensor(h[:, :, pair], h[:, :, pair],
                                            p_o[:, 0:4 * TOK].rearrange("p (a b) -> p a b", a=2),
                                            ALU.add).then_inc(h_done, 1)

                def units(c, more):
                    for s in range(NU + 1):
                        if s >= 4:
                            add(c, s - 4)
                        if s < NU:
                            dve.wait_ge(s_ready, c * NU + s + 1)
                            sc = p_s[0:PW, s % 2, :, 0:BW].rearrange("p a (b c) -> p a b c", c=TOK)
                            nc.vector.tensor_reduce(mx[0:PW, s % 2].rearrange("p (a b) -> p a b", a=2), sc,
                                                    AX.X, ALU.max).then_inc(max_ready, 1)
                            dve.wait_ge(max_ready, c * NU + s + 1)
                            dve.wait_ge(p_ready, c * NU + 1)
                            nc.vector.tensor_tensor(
                                ex[0:PW, s % 4].rearrange("p (a b) c -> p a b c", a=2), sc,
                                bc(mx[0:PW, s % 2].rearrange("p (a b) -> p a b", a=2).unsqueeze(3), [PW, 2, HT, TOK]),
                                ALU.subtract).then_inc(sub_ready, 1)
                        if s >= 1:
                            u = s - 1
                            dve.wait_ge(exp_ready, c * NU + u + 1)
                            nc.vector.tensor_reduce(sm[0:PW, u % 2], ex[0:PW, u % 4], AX.X, ALU.add).then_inc(sum_ready, 1)
                            dve.wait_ge(sum_ready, c * NU + u + 1)
                            nc.vector.reciprocal(rc[0:PW, u % 4], sm[0:PW, u % 2]).then_inc(rc_ready, 1)
                    add(c, 1)
                    if more:
                        keep(c + 1, 0)
                        add(c, 2)
                        keep(c + 1, 1)
                        normalise(c + 1, 0)
                        add(c, 3)
                        expand(c + 1)
                        normalise(c + 1, 1)
                    else:
                        add(c, 2)
                        add(c, 3)

                for j in range(2):
                    keep(0, j)
                normalise(0, 0)
                expand(0)
                normalise(0, 1)
                with dve.Fori(0, CH - 1) as i:
                    units(i, True)
                units(CH - 1, False)


def tree_ffn(nc, K, wq1, routT, leafT, woutT, outT):
    h, xn, vec, ident = K["h"], K["xn"], K["vec"], K["ident"]
    NTT = (NT + P - 1) // P
    NN = LEAVES - 1
    with ExitStack() as st:
        def sb(n, shape, dt=F32):
            return st.enter_context(nc.sbuf_tensor(f"tr_{n}", shape, dt))

        def ps(n, shape):
            return st.enter_context(nc.psum_tensor(f"tr_{n}", shape, F32))

        def sem(n):
            return st.enter_context(nc.semaphore(f"tr_{n}"))

        wq = sb("wq", [P, ET, ED])
        wr = sb("wr", [P, ET, NN])
        lf = sb("lf", [P, ET, LEAVES])
        wo = sb("wo", [P, ET, ED])
        route = sb("route", [P, ET, NN])
        leafo = sb("leafo", [P, ET, ED])
        sig = sb("sig", [P, NTT, LEAVES])
        lpa = sb("lpa", [P, NTT, LEAVES])
        lpb = sb("lpb", [P, NTT, LEAVES])
        lpT = sb("lpT", [P, ET, NT])
        y = sb("y", [P, ET, NT])

        p_w = ps("p_w", [P, 2, 512])
        p_l = ps("p_l", [P, 2, 512])
        p_t = ps("p_t", [P, 2, 512])
        p_y = ps("p_y", [P, 2, 512])

        w_in = sem("w_in")
        fold_ready = sem("fold_ready")
        fold_kept = sem("fold_kept")
        logit_ready = sem("logit_ready")
        sig_ready = sem("sig_ready")
        sig_zero = sem("sig_zero")
        level = sem("level")
        lpT_psum = sem("lpT_psum")
        lpT_ready = sem("lpT_ready")
        y_psum = sem("y_psum")
        y_ready = sem("y_ready")
        stored = sem("stored")

        def rows(n):
            return min(P, NT - n * P)

        HALF = [(0, NTT // 2), (NTT // 2, NTT)]

        with nc.Block() as block:
            @block.sync
            def _(sp):
                sp.dma_start(wq[:], wq1).then_inc(w_in, 16)
                sp.dma_start(wr[:], routT).then_inc(w_in, 16)
                sp.dma_start(lf[:], leafT).then_inc(w_in, 16)
                sp.dma_start(wo[:], woutT).then_inc(w_in, 16)
                for c in range(CH):
                    sp.wait_ge(y_ready, c + 1)
                    sp.dma_start(outT[:, :, c * CT:(c + 1) * CT], y[:, :, c * CT:(c + 1) * CT]).then_inc(stored, 16)
                sp.wait_ge(stored, CH * 16)

            @block.gpsimd
            def _(pool):
                nc.gpsimd.memset(sig[:], 0.5).then_inc(sig_zero, 1)

            @block.tensor
            def _(pe):
                pe.wait_ge(w_in, 64)
                for t in range(ET):
                    for k in range(ET):
                        last = nc.tensor.matmul(p_w[:, 0, t * 256:t * 256 + NN], wq[:, k, t * P:(t + 1) * P], wr[:, k, :],
                                                start=(k == 0), stop=(k == ET - 1))
                last.then_inc(fold_ready, 1)
                for t in range(ET):
                    for k in range(ET):
                        last = nc.tensor.matmul(p_w[:, 1, t * 256:t * 256 + ED], lf[:, k, t * P:(t + 1) * P], wo[:, k, :],
                                                start=(k == 0), stop=(k == ET - 1))
                last.then_inc(fold_ready, 1)
                pe.wait_ge(fold_kept, 1)
                for n in range(NTT):
                    if n >= 2:
                        pe.wait_ge(sig_ready, n - 1)
                    r = rows(n)
                    for k in range(ET):
                        last = nc.tensor.matmul(p_l[0:r, n % 2, 0:NN], xn[:, k, n * P:n * P + r], route[:, k, :],
                                                start=(k == 0), stop=(k == ET - 1))
                    last.then_inc(logit_ready, 1)
                for n in range(NTT):
                    if n in (0, NTT // 2):
                        pe.wait_ge(level, 16 if n == 0 else 32)
                    if n >= 2:
                        pe.wait_ge(lpT_ready, n - 1)
                    r = rows(n)
                    for t in range(ET):
                        last = nc.tensor.transpose(p_t[:, n % 2, t * P:t * P + r], lpa[0:r, n, t * P:(t + 1) * P],
                                                   ident[0:r, 0:r])
                    last.then_inc(lpT_psum, 1)
                pe.wait_ge(fold_kept, 2)
                for c in range(CH):
                    pe.wait_ge(lpT_ready, min(NTT, -(-(c + 1) * CT // P)))
                    if c >= 1:
                        pe.wait_ge(y_ready, c)
                    for t in range(ET):
                        for k in range(ET):
                            last = nc.tensor.matmul(p_y[:, t, 0:CT], leafo[:, k, t * P:(t + 1) * P],
                                                    lpT[:, k, c * CT:(c + 1) * CT], start=(k == 0), stop=(k == ET - 1))
                    last.then_inc(y_psum, 1)

            @block.scalar
            def _(act):
                act.wait_ge(sig_zero, 1)
                act.wait_ge(fold_ready, 2)
                nc.scalar.copy(route[:], p_w[:, 0].rearrange("p (a b) -> p a b", a=2)[:, :, 0:NN]).then_inc(fold_kept, 1)
                nc.scalar.copy(leafo[:], p_w[:, 1].rearrange("p (a b) -> p a b", a=2)).then_inc(fold_kept, 1)
                for n in range(NTT):
                    r = rows(n)
                    act.wait_ge(logit_ready, n + 1)
                    nc.scalar.activation(sig[0:r, n, 0:NN], p_l[0:r, n % 2, 0:NN], ACT.Sigmoid).then_inc(sig_ready, 1)
                for n in range(NTT):
                    r = rows(n)
                    act.wait_ge(lpT_psum, n + 1)
                    nc.scalar.copy(lpT[:, :, n * P:n * P + r],
                                   p_t[:, n % 2, 0:2 * P].rearrange("p (a b) -> p a b", a=2)[:, :, 0:r]).then_inc(lpT_ready, 1)

            @block.vector
            def _(dve):
                done = 0
                for a, b in HALF:
                    dve.wait_ge(sig_ready, b)
                    n = b - a
                    for lv in range(DEPTH):
                        w = 2 ** lv
                        src, dst = (lpb, lpa) if lv % 2 else (lpa, lpb)
                        pair = dst[:, a:b, 0:2 * w].rearrange("p n (c s) -> p n c s", s=2)
                        g = sig[:, a:b, w - 1:2 * w - 1]
                        if lv == 0:
                            nc.vector.tensor_copy(pair[:, :, :, 1], g).then_inc(level, 1)
                            nc.vector.tensor_scalar(pair[:, :, :, 0], g, -1.0, 1.0, ALU.mult, ALU.add).then_inc(level, 1)
                        else:
                            nc.vector.tensor_tensor(pair[:, :, :, 1], src[:, a:b, 0:w], g, ALU.mult).then_inc(level, 1)
                            dve.wait_ge(level, done + 1)
                            nc.vector.tensor_tensor(pair[:, :, :, 0], src[:, a:b, 0:w], pair[:, :, :, 1],
                                                    ALU.subtract).then_inc(level, 1)
                        done += 2
                        dve.wait_ge(level, done)
                for c in range(CH):
                    dve.wait_ge(y_psum, c + 1)
                    cols = slice(c * CT, (c + 1) * CT)
                    for t in range(ET):
                        last = nc.vector.scalar_tensor_tensor(out=y[:, t, cols], in0=p_y[:, t, 0:CT],
                                                              scalar=vec[:, V_WB + t:V_WB + t + 1], in1=h[:, t, cols],
                                                              op0=ALU.add, op1=ALU.add)
                    last.then_inc(y_ready, 1)


def tiles(a, k):
    return np.ascontiguousarray(a.reshape(k, P, -1).transpose(1, 0, 2))


def constants():
    c = np.zeros((P, C_END), np.float32)
    c[:, C_ID:C_ID + P] = np.eye(P)
    row = np.arange(P)
    c[:, C_BD:C_BD + P] = (row[:, None] // HD) == (row[None, :] // HD)
    c[:, C_MASK:C_MASK + HT] = (row[:, None] // HD) == np.arange(HT)[None, :]
    inv = (np.float32(1.0) / np.float32(10000.0) ** (np.arange(0, 2 * HD, 2, dtype=np.float32) / np.float32(2 * HD)))
    ang = np.arange(TOK, dtype=np.float32)[None, :] * inv.astype(np.float32)[row % HD][:, None]
    c[:, C_COS:C_COS + TOK] = np.cos(ang)
    c[:, C_SIN:C_SIN + TOK] = np.sin(ang)
    return c


def kernel(**inp):
    import concourse.bacc as bacc
    from concourse.bass_utils import run_bass_kernel_spmd

    a = {k: np.asarray(v) for k, v in inp.items()}
    x = a["x"].reshape(IMGS, 3, 6, 16, 6, 16).transpose(0, 2, 4, 3, 5, 1).reshape(IMGS * PATCH, PD)
    xT = x.T.reshape(PT6, P, CH, CP).transpose(2, 1, 0, 3)

    def vec(v):
        return v.reshape(-1, P).T

    pos = a["L0_tok_pos_emb"][0].T.reshape(ET, P, TOK).transpose(1, 0, 2).reshape(P, ET * TOK)
    vecs = np.concatenate([vec(a["L0_tok_ln1_g"]), vec(a["L0_tok_ln1_b"]), vec(a["L0_tok_b_proj"]),
                           vec(a["L0_tok_ln2_g"]), vec(a["L0_tok_ln2_b"]), vec(a["L0_tok_cls_token"].reshape(-1)),
                           vec(a["L1_ffn_Wout_b"]), pos], axis=1)
    lams = np.concatenate([a["L0_attn_lambda_q1"], a["L0_attn_lambda_q2"],
                           a["L0_attn_lambda_k1"], a["L0_attn_lambda_k2"]]).reshape(1, 64)
    wqkv = a["L0_attn_W_qkv"]
    wv = wqkv[4 * ED:].reshape(2, HT, 2, HD, ED).transpose(2, 1, 0, 3, 4).reshape(2 * ED, ED)
    w1v = a["L1_attn_Wv"].reshape(HT, 2, HD, ED).transpose(1, 0, 2, 3).reshape(ED, ED)
    arrays = {
        "xT": xT, "wtok": tiles(a["L0_tok_W_proj"], PT6), "vecs": vecs, "lams": lams,
        "gsc": a["L1_attn_g_scale"].reshape(1, 1), "cst": constants(),
        "wqkT": tiles(wqkv[:4 * ED].T, ET), "wvT": tiles(wv.T, ET),
        "wprojT": tiles(a["L0_attn_W_proj"].T, 4),
        "w_up": tiles(a["L0_ffn_w_up"], IT).reshape(P, -1), "w_gate": tiles(a["L0_ffn_w_gate"], IT).reshape(P, -1),
        "w_down": tiles(a["L0_ffn_w_down"], ET).reshape(P, -1),
        "w1qkT": tiles(np.concatenate([a["L1_attn_Wq"], a["L1_attn_Wk"]]).T, ET),
        "w1vT": tiles(w1v.T, ET),
        "wq1": tiles(a["L1_ffn_Wq"], ET), "routT": tiles(a["L1_ffn_routers"].T, ET),
        "leafT": tiles(a["L1_ffn_leaf_values"].T, ET), "woutT": tiles(a["L1_ffn_Wout_w"].T, ET),
    }
    arrays = {k: np.ascontiguousarray(v) for k, v in arrays.items()}
    nc = bacc.Bacc("TRN2", target_bir_lowering=False, num_devices=1)
    args = [nc.dram_tensor(k, v.shape, mybir.dt.from_np(v.dtype), kind="ExternalInput").ap() for k, v in arrays.items()]
    out = nc.dram_tensor("outT", (P, ET, NT), F32, kind="ExternalOutput").ap()
    program(nc, *args, out)
    got = run_bass_kernel_spmd(nc, [arrays], core_ids=[0]).results[0]["outT"]
    return np.ascontiguousarray(got.transpose(2, 1, 0).reshape(IMGS, TOK, ED))
```

```python
from contextlib import ExitStack
import math

import numpy as np

import concourse.bass as bass
from concourse import mybir

F32 = mybir.dt.float32
I16 = mybir.dt.int16
U16 = mybir.dt.uint16
ALU = mybir.AluOpType
ACT = mybir.ActivationFunctionType
AX = mybir.AxisListType

P = 128
IMGS = 32
PATCH = 36
TOK = PATCH + 1
NT = IMGS * TOK
CH = 4
CI = IMGS // CH
CT = CI * TOK
CP = CI * PATCH
PAIRS = CI // 2
ED = 256
ET = ED // P
PD = 768
PT6 = PD // P
HEADS = 16
HD = 16
HT = 8
IF = 768
IT = IF // P
GAP = 64
PW = GAP + TOK
BLK = 32
LEAVES = 256
DEPTH = 8
EPS = 1e-5
L2_SCALE = 2.0 ** 16

C_ID, C_BD, C_MASK, C_COS, C_SIN, C_END = 0, 128, 256, 264, 301, 338
V_G1, V_B1, V_BP, V_G2, V_B2, V_CLS, V_WB, V_POS, V_END = 0, 6, 12, 14, 16, 18, 20, 22, 22 + 2 * TOK


def bc(ap, shape):
    return ap.to_broadcast(shape)


def program(nc, xT, wtok, vecs, lams, gsc, cst, wqkT, wvT, wprojT, w_up, w_gate, w_down,
            w1qkT, w1vT, wq1, routT, leafT, woutT, outT):
    with ExitStack() as top:
        def sb(name, shape, dt=F32):
            return top.enter_context(nc.sbuf_tensor(name, shape, dt))

        K = {}
        K["h"] = sb("h", [P, ET, NT])
        K["xn"] = sb("xn", [P, ET, NT])
        K["cst"] = sb("cst_sb", [P, C_END])
        K["vec"] = sb("vec_sb", [P, V_END])
        K["wqk"] = sb("wqk_sb", [P, ET, 4 * ED])
        K["wv"] = sb("wv_sb", [P, ET, 2 * ED])
        K["wp"] = sb("wp_sb", [P, 4, ED])
        K["w1qk"] = sb("w1qk_sb", [P, ET, 2 * ED])
        K["w1v"] = sb("w1v_sb", [P, ET, ED])
        K["wup"] = sb("wup_sb", [P, ET, IF])
        K["wgate"] = sb("wgate_sb", [P, ET, IF])
        K["wdown"] = sb("wdown_sb", [P, IT, ED])
        K["xmax"] = sb("xmax", [P, CH])
        K["mask0"] = sb("mask0", [P, HT])
        K["mask1"] = sb("mask1", [P, HT])
        K["neglam"] = sb("neglam", [P, 2])
        K["eps"] = sb("eps", [P, 2])
        K["mean256"] = sb("mean256", [P, P])
        K["xg"] = sb("xg", [P, ET, CI, GAP])
        K["pr"] = sb("pr", [P, 4 * HT * GAP])
        K["vx"] = sb("vx", [P, CI, 2, HT * 32])
        K["loaded"] = top.enter_context(nc.semaphore("weights_loaded"))
        K["ln_sems"] = [top.enter_context(nc.semaphore(f"ln_{n}")) for n in
                        ("h_added", "sq_added", "mean_ready", "centred", "squared", "var_ready", "logged", "rstd_ready", "xn_ready")]
        K["ident"] = K["cst"][:, C_ID:C_ID + P]

        tokenizer(nc, K, xT, wtok, vecs, lams, gsc, cst, wqkT, wvT, wprojT, w_up, w_gate, w_down, w1qkT, w1vT)
        layernorm(nc, K, "ln_a", 0)
        diff_attention(nc, K)
        layernorm(nc, K, "ln_f", 1, maxima=True)
        quantised_ffn(nc, K)
        layernorm(nc, K, "ln_b", 2)
        for name, cols in (("wq1", ED), ("rout", LEAVES - 1), ("leaf", LEAVES), ("wout", ED), ("route", LEAVES - 1),
                           ("leafo", ED)):
            K[name] = sb(name + "_sb", [P, ET, cols])
        cosine_attention(nc, K, wq1, routT, leafT, woutT)
        layernorm(nc, K, "ln_g", 3)
        tree_ffn(nc, K, outT)


def tokenizer(nc, K, xT, wtok, vecs, lams, gsc, cst, wqkT, wvT, wprojT, w_up, w_gate, w_down, w1qkT, w1vT):
    h, cs, vec, ident = K["h"], K["cst"], K["vec"], K["ident"]
    with ExitStack() as st:
        def sb(name, shape, dt=F32):
            return st.enter_context(nc.sbuf_tensor(name, shape, dt))

        def ps(name, shape):
            return st.enter_context(nc.psum_tensor(name, shape, F32))

        def sem(name):
            return st.enter_context(nc.semaphore(name))

        x = sb("x_sb", [P, CH, PT6, CP])
        w = sb("wtok_sb", [P, PT6, ED])
        wg = sb("wtok_g", [P, PT6, ED])
        mean768 = sb("mean768", [P, P])
        xs = sb("t_xs", [P, 2, 3, CP])
        xc = sb("t_xc", [P, 2, PT6, CP])
        sq = sb("t_sq", [P, PT6, CP])
        qs = sb("t_qs", [P, 3, CP])
        ln1 = sb("t_ln1", [P, CP])
        rstd1 = sb("t_rstd1", [P, CP])
        zr = sb("t_zr", [P, ET, CP])
        zs = sb("t_zs", [P, ET, CP])
        xc2 = sb("t_xc2", [P, ET, CP])
        sq2 = sb("t_sq2", [P, ET, CP])
        ln2 = sb("t_ln2", [P, CP])
        rstd2 = sb("t_rstd2", [P, CP])
        z3 = sb("t_z3", [P, ET, CP])
        c0 = sb("t_c0", [P, ET])
        posb = sb("t_posb", [P, ET, TOK])
        raw = sb("raw_w", [P, 3, IT * ED])
        wint = sb("int_w", [P, IT * ED], I16)
        wmax = sb("wmax", [P, 3, 48])
        wsc = sb("wsc", [P, 3, 48])
        wrs = sb("wrs", [P, 3, 48])
        row = sb("row", [1, 80])
        onesr = sb("onesr", [1, P])

        p_mean = ps("p_mean", [P, 512])
        p_var = ps("p_var", [P, 512])
        p_z = ps("p_z", [P, 2, 2, 512])
        p_mu2 = ps("p_mu2", [P, 512])
        p_var2 = ps("p_var2", [P, 512])

        small_in = sem("small_in")
        wtok_in = sem("wtok_in")
        x_in = [sem(f"x_in{c}") for c in range(CH)]
        ffw_in = [sem(f"ffw_in{m}") for m in range(3)]
        consts = sem("consts")
        wg_ready = sem("wg_ready")
        c0_psum = sem("c0_psum")
        c0_ready = sem("c0_ready")
        lam_step = sem("lam_step")
        lam_exp = sem("lam_exp")
        lam_spread = sem("lam_spread")
        xs_half = sem("xs_half")
        xs_ready = sem("xs_ready")
        mean_ready = sem("mean_ready")
        xc_ready = sem("xc_ready")
        sq_ready = sem("sq_ready")
        qs_half = sem("qs_half")
        qs_ready = sem("qs_ready")
        var_ready = sem("var_ready")
        ln1_done = sem("ln1_done")
        rstd1_ready = sem("rstd1_ready")
        z_ready = sem("z_ready")
        zr_ready = sem("zr_ready")
        zs_ready = sem("zs_ready")
        mu2_ready = sem("mu2_ready")
        xc2_ready = sem("xc2_ready")
        sq2_ready = sem("sq2_ready")
        var2_ready = sem("var2_ready")
        ln2_done = sem("ln2_done")
        rstd2_ready = sem("rstd2_ready")
        z3_ready = sem("z3_ready")
        h_ready = sem("h_ready")
        wmax_ready = sem("wmax_ready")
        wsc_ready = sem("wsc_ready")
        wint_ready = sem("wint_ready")
        wdq_ready = sem("wdq_ready")
        wt_psum = sem("wt_psum")
        wt_out = sem("wt_out")

        with nc.Block() as block:
            @block.sync
            def _(sp):
                sp.dma_start(x[:, 0], xT[0]).then_inc(x_in[0], 16)
                sp.dma_start(cs[:], cst).then_inc(small_in, 16)
                sp.dma_start(vec[:], vecs).then_inc(small_in, 16)
                sp.dma_start(row[0:1, 0:64], lams).then_inc(small_in, 16)
                sp.dma_start(row[0:1, 79:80], gsc).then_inc(small_in, 16)
                sp.dma_start(w[:], wtok).then_inc(wtok_in, 16)
                for c in range(1, CH):
                    sp.dma_start(x[:, c], xT[c]).then_inc(x_in[c], 16)
                for n, src in enumerate((w_up, w_gate, w_down)):
                    sp.dma_start(raw[:, n, :], src).then_inc(ffw_in[n], 16)
                sp.dma_start(K["wqk"][:], wqkT).then_inc(K["loaded"], 16)
                sp.dma_start(K["wv"][:], wvT).then_inc(K["loaded"], 16)
                sp.dma_start(K["wp"][:], wprojT).then_inc(K["loaded"], 16)
                sp.dma_start(K["w1qk"][:], w1qkT).then_inc(K["loaded"], 16)
                sp.dma_start(K["w1v"][:], w1vT).then_inc(K["loaded"], 16)

            @block.gpsimd
            def _(pool):
                nc.gpsimd.memset(mean768[:], 1.0 / PD).then_inc(consts, 1)
                nc.gpsimd.memset(K["mean256"][:], 1.0 / ED).then_inc(consts, 1)
                nc.gpsimd.memset(onesr[:], 1.0).then_inc(consts, 1)
                nc.gpsimd.memset(K["eps"][:, 0:1], EPS).then_inc(consts, 1)
                nc.gpsimd.memset(K["eps"][:, 1:2], 0.5 * math.log(L2_SCALE)).then_inc(consts, 1)
                nc.gpsimd.memset(K["xg"][:], 0.0)
                nc.gpsimd.memset(K["pr"][:], 0.0)

                def add_patches(c):
                    pool.wait_ge(x_in[c], 16)
                    if c >= 2:
                        pool.wait_ge(mean_ready, c - 1)
                    s_ = xs[:, c % 2]
                    nc.gpsimd.tensor_tensor(s_, x[:, c, 0:3], x[:, c, 3:6], ALU.add).then_inc(xs_half, 1)
                    pool.wait_ge(xs_half, c + 1)
                    nc.gpsimd.tensor_tensor(s_[:, 0], s_[:, 0], s_[:, 1], ALU.add).then_inc(xs_ready, 1)

                def add_squares(c):
                    pool.wait_ge(sq_ready, c + 1)
                    if c >= 1:
                        pool.wait_ge(var_ready, c)
                    nc.gpsimd.tensor_tensor(qs[:], sq[:, 0:3], sq[:, 3:6], ALU.add).then_inc(qs_half, 1)
                    pool.wait_ge(qs_half, c + 1)
                    nc.gpsimd.tensor_tensor(qs[:, 0], qs[:, 0], qs[:, 1], ALU.add).then_inc(qs_ready, 1)

                add_patches(0)
                add_patches(1)
                for c in range(CH):
                    add_squares(c)
                    if c + 2 < CH:
                        add_patches(c + 2)
                nc.gpsimd.memset(K["vx"][:], 0.0)

            @block.tensor
            def _(pe):
                def mean(c):
                    pe.wait_ge(xs_ready, c + 1)
                    if c >= 1:
                        pe.wait_ge(xc_ready, c)
                    for k in (0, 2):
                        last = nc.tensor.matmul(p_mean[:, 0:CP], mean768[:], xs[:, c % 2, k], start=(k == 0), stop=(k == 2))
                    last.then_inc(mean_ready, 1)

                def project(c):
                    pe.wait_ge(xc_ready, c + 1)
                    if c >= 2:
                        pe.wait_ge(zr_ready, c - 1)
                    for t in range(ET):
                        for k in range(PT6):
                            last = nc.tensor.matmul(p_z[:, c % 2, t, 0:CP], wg[:, k, t * P:(t + 1) * P],
                                                    xc[:, c % 2, k, :], start=(k == 0), stop=(k == PT6 - 1))
                    last.then_inc(z_ready, 1)

                def variance(c):
                    pe.wait_ge(qs_ready, c + 1)
                    if c >= 1:
                        pe.wait_ge(ln1_done, c)
                    for k in (0, 2):
                        last = nc.tensor.matmul(p_var[:, 0:CP], mean768[:], qs[:, k], start=(k == 0), stop=(k == 2))
                    last.then_inc(var_ready, 1)

                def mean2(c):
                    pe.wait_ge(zs_ready, 2 * c + 2)
                    if c >= 1:
                        pe.wait_ge(xc2_ready, c)
                    for k in range(ET):
                        last = nc.tensor.matmul(p_mu2[:, 0:CP], K["mean256"][:], zs[:, k, :],
                                                start=(k == 0), stop=(k == ET - 1))
                    last.then_inc(mu2_ready, 1)

                def variance2(c):
                    pe.wait_ge(sq2_ready, c + 1)
                    if c >= 1:
                        pe.wait_ge(ln2_done, c)
                    for k in range(ET):
                        last = nc.tensor.matmul(p_var2[:, 0:CP], K["mean256"][:], sq2[:, k, :],
                                                start=(k == 0), stop=(k == ET - 1))
                    last.then_inc(var2_ready, 1)

                def turn_weights(m):
                    pe.wait_ge(wdq_ready, m + 1)
                    for q in range(3):
                        n = 3 * m + q
                        pe.wait_ge(zr_ready, CH if n % 4 >= 2 else CH - 1)
                        if n >= 4:
                            pe.wait_ge(wt_out, n - 3)
                        for a in range(2):
                            for b in range(2):
                                piece = (2 * q + b) * ET + a if m < 2 else b * IT + 2 * q + a
                                last = nc.tensor.transpose(p_z[:, n % 4 // 2, n % 2, (2 * a + b) * P:(2 * a + b + 1) * P],
                                                           raw[:, m, piece * P:(piece + 1) * P], ident)
                        last.then_inc(wt_psum, 1)

                pe.wait_ge(consts, 5)
                pe.wait_ge(small_in, 64)
                mean(0)
                pe.wait_ge(wtok_in, 16)
                for t in range(ET):
                    for k in range(PT6):
                        last = nc.tensor.matmul(p_var[:, t:t + 1], w[:, k, t * P:(t + 1) * P],
                                                vec[:, V_B1 + k:V_B1 + k + 1], start=(k == 0), stop=(k == PT6 - 1))
                last.then_inc(c0_psum, 1)
                pe.wait_ge(lam_step, 4)
                nc.tensor.matmul(p_mu2[:, 0:2], onesr[0:1, :], row[0:1, 78:80], start=True, stop=True).then_inc(lam_spread, 1)
                mean(1)
                pe.wait_ge(wg_ready, PT6)
                for s in range(CH + 1):
                    if s < CH:
                        project(s)
                    if s == CH:
                        turn_weights(0)
                    if s == 1:
                        pe.wait_ge(lam_step, 5)
                    if s >= 1:
                        mean2(s - 1)
                    if s < CH:
                        if s == 0:
                            pe.wait_ge(c0_ready, 1)
                        variance(s)
                    if s + 2 < CH:
                        mean(s + 2)
                    if s == CH:
                        turn_weights(1)
                    if s >= 1:
                        variance2(s - 1)
                turn_weights(2)

            @block.scalar
            def _(act):
                def square(c):
                    act.wait_ge(xc_ready, c + 1)
                    if c >= 1:
                        act.wait_ge(qs_half, c)
                    nc.scalar.activation(sq[:], xc[:, c % 2], ACT.Square).then_inc(sq_ready, 1)

                def shift(c):
                    act.wait_ge(zr_ready, c + 1)
                    if c >= 1:
                        act.wait_ge(xc2_ready, c)
                    for t in range(ET):
                        nc.scalar.activation(zs[:, t], zr[:, t], ACT.Identity, bias=c0[:, t:t + 1]).then_inc(zs_ready, 1)

                def square2(c):
                    act.wait_ge(xc2_ready, c + 1)
                    nc.scalar.activation(sq2[:], xc2[:], ACT.Square).then_inc(sq2_ready, 1)

                def invert(c):
                    act.wait_ge(var_ready, c + 1)
                    nc.scalar.activation(ln1[:], p_var[:, 0:CP], ACT.Ln, bias=K["eps"][:, 0:1]).then_inc(ln1_done, 1)
                    act.wait_ge(ln1_done, c + 1)
                    if c >= 1:
                        act.wait_ge(zr_ready, c)
                    nc.scalar.activation(rstd1[:], ln1[:], ACT.Exp, scale=-0.5).then_inc(rstd1_ready, 1)

                def invert2(c):
                    act.wait_ge(var2_ready, c + 1)
                    nc.scalar.activation(ln2[:], p_var2[:, 0:CP], ACT.Ln, bias=K["eps"][:, 0:1]).then_inc(ln2_done, 1)
                    act.wait_ge(ln2_done, c + 1)
                    if c >= 1:
                        act.wait_ge(z3_ready, c)
                    nc.scalar.activation(rstd2[:], ln2[:], ACT.Exp, scale=-0.5).then_inc(rstd2_ready, 1)

                def keep_weights(m):
                    for q in range(3):
                        n = 3 * m + q
                        act.wait_ge(wt_psum, n + 1)
                        if m < 2:
                            dst = K[("wup", "wgate")[m]][:, :, 2 * q * P:(2 * q + 2) * P]
                        else:
                            dst = K["wdown"][:, 2 * q:2 * q + 2, :]
                        nc.scalar.copy(dst, p_z[:, n % 4 // 2, n % 2, :].rearrange("p (a b) -> p a b", a=2)).then_inc(wt_out, 1)

                nc.scalar.preload_act_table_set("natural_log_exp_and_others")
                act.wait_ge(consts, 5)
                act.wait_ge(lam_step, 2)
                nc.scalar.activation(row[0:1, 70:72], row[0:1, 68:70], ACT.Exp).then_inc(lam_exp, 1)
                act.wait_ge(c0_ready, 1)
                for s in range(CH + 1):
                    if s < CH:
                        square(s)
                    if s >= 1:
                        shift(s - 1)
                        if s == CH:
                            keep_weights(0)
                        square2(s - 1)
                    if s < CH:
                        invert(s)
                    if s == CH:
                        keep_weights(1)
                    if s >= 1:
                        invert2(s - 1)
                keep_weights(2)

            @block.vector
            def _(dve):
                hv = h[:].rearrange("p t (i n) -> p t i n", n=TOK)

                def centre(c):
                    dve.wait_ge(mean_ready, c + 1)
                    if c >= 2:
                        dve.wait_ge(sq_ready, c - 1)
                        dve.wait_ge(z_ready, c - 1)
                    nc.vector.tensor_tensor(xc[:, c % 2], x[:, c], bc(p_mean[:, 0:CP].unsqueeze(1), [P, PT6, CP]),
                                            ALU.subtract).then_inc(xc_ready, 1)

                def scale(c):
                    dve.wait_ge(z_ready, c + 1)
                    dve.wait_ge(rstd1_ready, c + 1)
                    if c >= 1:
                        dve.wait_ge(zs_ready, 2 * c)
                    nc.vector.tensor_tensor(zr[:], p_z[:, c % 2, :, 0:CP], bc(rstd1[:].unsqueeze(1), [P, ET, CP]),
                                            ALU.mult).then_inc(zr_ready, 1)

                def centre2(c):
                    dve.wait_ge(mu2_ready, c + 1)
                    if c >= 1:
                        dve.wait_ge(sq2_ready, c)
                        dve.wait_ge(z3_ready, c)
                    nc.vector.tensor_tensor(xc2[:], zs[:], bc(p_mu2[:, 0:CP].unsqueeze(1), [P, ET, CP]),
                                            ALU.subtract).then_inc(xc2_ready, 1)

                def tokens(c):
                    dve.wait_ge(rstd2_ready, c + 1)
                    if c >= 1:
                        dve.wait_ge(h_ready, 2 * c + 1)
                    nc.vector.tensor_tensor(z3[:], xc2[:], bc(rstd2[:].unsqueeze(1), [P, ET, CP]),
                                            ALU.mult).then_inc(z3_ready, 1)
                    dve.wait_ge(z3_ready, c + 1)
                    for t in range(ET):
                        nc.vector.scalar_tensor_tensor(
                            out=hv[:, t, c * CI:(c + 1) * CI, 1:TOK],
                            in0=z3[:, t].rearrange("p (i n) -> p i n", n=PATCH),
                            scalar=vec[:, V_G2 + t:V_G2 + t + 1],
                            in1=bc(posb[:, t, 1:TOK].unsqueeze(1), [P, CI, PATCH]),
                            op0=ALU.mult, op1=ALU.add).then_inc(h_ready, 1)

                ints = wint[:].rearrange("p (b n) -> p b n", n=BLK)

                def weight_scales(m):
                    dve.wait_ge(ffw_in[m], 16)
                    nc.vector.tensor_reduce(wmax[:, m], raw[:, m].rearrange("p (b n) -> p b n", n=BLK), AX.X, ALU.max,
                                            apply_absolute_value=True).then_inc(wmax_ready, 1)
                    dve.wait_ge(wmax_ready, m + 1)
                    nc.vector.tensor_scalar(wsc[:, m], wmax[:, m], 1.0 / 7.0, 1e-12, ALU.mult, ALU.max).then_inc(wsc_ready, 1)
                    dve.wait_ge(wsc_ready, 2 * m + 1)
                    nc.vector.reciprocal(wrs[:, m], wsc[:, m]).then_inc(wsc_ready, 1)

                def weight_integers(m):
                    dve.wait_ge(wsc_ready, 2 * m + 2)
                    if m:
                        dve.wait_ge(wdq_ready, m)
                    nc.vector.tensor_tensor(ints, raw[:, m].rearrange("p (b n) -> p b n", n=BLK),
                                            bc(wrs[:, m].unsqueeze(2), [P, 48, BLK]), ALU.mult).then_inc(wint_ready, 1)

                def weight_values(m):
                    dve.wait_ge(wint_ready, m + 1)
                    nc.vector.tensor_tensor(raw[:, m].rearrange("p (b n) -> p b n", n=BLK), ints,
                                            bc(wsc[:, m].unsqueeze(2), [P, 48, BLK]), ALU.mult).then_inc(wdq_ready, 1)

                dve.wait_ge(small_in, 64)
                nc.vector.tensor_tensor(row[0:1, 0:32], row[0:1, 0:32], row[0:1, 32:64], ALU.mult).then_inc(lam_step, 1)
                dve.wait_ge(lam_step, 1)
                nc.vector.tensor_reduce(row[0:1, 68:70], row[0:1, 0:32].rearrange("p (a b) -> p a b", a=2),
                                        AX.X, ALU.add).then_inc(lam_step, 1)
                centre(0)
                dve.wait_ge(wtok_in, 16)
                for k in range(PT6):
                    nc.vector.tensor_scalar(wg[:, k], w[:, k], vec[:, V_G1 + k:V_G1 + k + 1], None, ALU.mult).then_inc(wg_ready, 1)
                dve.wait_ge(lam_exp, 1)
                nc.vector.tensor_tensor(row[0:1, 72:73], row[0:1, 71:72], row[0:1, 70:71], ALU.subtract).then_inc(lam_step, 1)
                dve.wait_ge(lam_step, 3)
                nc.vector.tensor_scalar(row[0:1, 78:79], row[0:1, 72:73], -(0.8 - 0.6 * math.exp(0.0)), None,
                                        ALU.add).then_inc(lam_step, 1)
                centre(1)
                dve.wait_ge(c0_psum, 1)
                nc.vector.tensor_tensor(c0[:], p_var[:, 0:ET], vec[:, V_BP:V_BP + ET], ALU.add).then_inc(c0_ready, 1)
                dve.wait_ge(lam_spread, 1)
                nc.vector.tensor_copy(K["neglam"][:], p_mu2[:, 0:2]).then_inc(lam_step, 1)
                dve.wait_ge(lam_step, 5)
                nc.vector.tensor_scalar(K["mask0"][:], cs[:, C_MASK:C_MASK + HT], float(HD) ** -0.5, None, ALU.mult)
                nc.vector.tensor_scalar(K["mask1"][:], cs[:, C_MASK:C_MASK + HT], K["neglam"][:, 1:2], None, ALU.mult)
                nc.vector.tensor_tensor(posb[:], vec[:, V_POS:V_END].rearrange("p (t n) -> p t n", t=ET),
                                        bc(vec[:, V_B2:V_B2 + ET].unsqueeze(2), [P, ET, TOK]), ALU.add).then_inc(c0_ready, 1)
                nc.vector.tensor_tensor(hv[:, :, :, 0],
                                        bc(vec[:, V_CLS:V_CLS + ET].unsqueeze(2), [P, ET, IMGS]),
                                        bc(vec[:, V_POS:V_END].rearrange("p (t n) -> p t n", t=ET)[:, :, 0:1],
                                           [P, ET, IMGS]), ALU.add).then_inc(h_ready, 1)
                dve.wait_ge(c0_ready, 2)
                for s in range(1, CH + 1):
                    scale(s - 1)
                    if s >= 2:
                        tokens(s - 2)
                    if s + 1 < CH:
                        centre(s + 1)
                    if 2 <= s:
                        weight_values(s - 2)
                    if s <= 3:
                        weight_scales(s - 1)
                    centre2(s - 1)
                    if s <= 3:
                        weight_integers(s - 1)
                tokens(CH - 1)


def layernorm(nc, K, name, nth, maxima=False):
    h, xn = K["h"], K["xn"]
    with ExitStack() as st:
        def sb(n, shape, dt=F32):
            return st.enter_context(nc.sbuf_tensor(f"{name}_{n}", shape, dt))

        xc = sb("xc", [P, CH, ET, CT])
        sq = sb("sq", [P, CH, ET, CT])
        lnv = sb("lnv", [P, CH, CT])
        rstd = sb("rstd", [P, CH, CT])
        hs = sb("hs", [P, CH, CT])
        ss = sb("ss", [P, CH, CT])
        p_mu = st.enter_context(nc.psum_tensor(f"{name}_mu", [P, CH, 512], F32))
        p_var = st.enter_context(nc.psum_tensor(f"{name}_var", [P, CH, 512], F32))
        h_added, sq_added, mean_ready, centred, squared, var_ready, logged, rstd_ready, xn_ready = K["ln_sems"]
        b = CH * nth

        def cols(c):
            return slice(c * CT, (c + 1) * CT)

        with nc.Block() as block:
            @block.gpsimd
            def _(pool):
                for c in range(CH):
                    nc.gpsimd.tensor_tensor(hs[:, c], h[:, 0, cols(c)], h[:, 1, cols(c)], ALU.add).then_inc(h_added, 1)
                for c in range(CH):
                    pool.wait_ge(squared, b + c + 1)
                    nc.gpsimd.tensor_tensor(ss[:, c], sq[:, c, 0], sq[:, c, 1], ALU.add).then_inc(sq_added, 1)

            @block.tensor
            def _(pe):
                for c in range(CH):
                    pe.wait_ge(h_added, b + c + 1)
                    nc.tensor.matmul(p_mu[:, c, 0:CT], K["mean256"][:], hs[:, c], start=True, stop=True).then_inc(mean_ready, 1)
                for c in range(CH):
                    pe.wait_ge(sq_added, b + c + 1)
                    nc.tensor.matmul(p_var[:, c, 0:CT], K["mean256"][:], ss[:, c], start=True, stop=True).then_inc(var_ready, 1)

            @block.vector
            def _(dve):
                for c in range(CH):
                    dve.wait_ge(mean_ready, b + c + 1)
                    nc.vector.tensor_tensor(xc[:, c], h[:, :, cols(c)], bc(p_mu[:, c, 0:CT].unsqueeze(1), [P, ET, CT]),
                                            ALU.subtract).then_inc(centred, 1)
                for c in range(CH):
                    dve.wait_ge(rstd_ready, b + c + 1)
                    nc.vector.tensor_tensor(xn[:, :, cols(c)], xc[:, c], bc(rstd[:, c].unsqueeze(1), [P, ET, CT]),
                                            ALU.mult).then_inc(xn_ready, 1)
                    if maxima:
                        dve.wait_ge(xn_ready, b + c + 1)
                        nc.vector.tensor_reduce(K["xmax"][:, c:c + 1], xn[:, :, cols(c)], AX.XY, ALU.max,
                                                apply_absolute_value=True)

            @block.scalar
            def _(act):
                for c in range(CH):
                    act.wait_ge(centred, b + c + 1)
                    nc.scalar.activation(sq[:, c], xc[:, c], ACT.Square).then_inc(squared, 1)
                for c in range(CH):
                    act.wait_ge(var_ready, b + c + 1)
                    nc.scalar.activation(lnv[:, c], p_var[:, c, 0:CT], ACT.Ln, bias=K["eps"][:, 0:1]).then_inc(logged, 1)
                    act.wait_ge(logged, b + c + 1)
                    nc.scalar.activation(rstd[:, c], lnv[:, c], ACT.Exp, scale=-0.5).then_inc(rstd_ready, 1)


def diff_attention(nc, K):
    h, xn, cs, ident = K["h"], K["xn"], K["cst"], K["ident"]
    NU = ET * PAIRS
    VX_IN = 2 * 4 * 16
    BW = HT * TOK
    with ExitStack() as st:
        def sb(n, shape, dt=F32):
            return st.enter_context(nc.sbuf_tensor(f"da_{n}", shape, dt))

        def ps(n, shape):
            return st.enter_context(nc.psum_tensor(f"da_{n}", shape, F32))

        def sem(n):
            return st.enter_context(nc.semaphore(f"da_{n}"))

        xg, vx = K["xg"], K["vx"]
        pr = K["pr"][:].rearrange("p (s a b) -> p s a b", s=4, b=GAP)
        cos_t = sb("cost", [P, 2, 2, CT])
        sin_t = sb("sint", [P, 2, 2, CT])
        qr = sb("qr", [P, ET, 2, CT])
        kr = sb("kr", [P, ET, 2, CT])
        kx = sb("kx", [P, ET, 2, CI, HT, TOK])
        vt = sb("vt", [P, PAIRS, 512])
        ex = sb("ex", [P, 4, 2 * HT, TOK])
        pts = sb("pts", [P, 2, 4 * PW])
        ot = sb("ot", [P, 4, CT])
        mx = sb("mx", [P, 2, 2 * HT])
        sm = sb("sm", [P, 2, 2 * HT])
        rc = sb("rc", [P, 4, 2 * HT])

        p_s = ps("p_s", [P, 2, 2, 512])
        p_t = ps("p_t", [P, 512])
        p_o = ps("p_o", [P, 512])
        p_v = ps("p_v", [P, 2, 512])

        xg_ready = sem("xg_ready")
        qk_ready = sem("qk_ready")
        rot_ready = sem("rot_ready")
        rot_used = sem("rot_used")
        kx_dve = sem("kx_dve")
        kx_act = sem("kx_act")
        v_ready = sem("v_ready")
        vt_ready = sem("vt_ready")
        vx_ready = sem("vx_ready")
        s_ready = sem("s_ready")
        max_ready = sem("max_ready")
        sub_ready = sem("sub_ready")
        exp_ready = sem("exp_ready")
        sum_ready = sem("sum_ready")
        inv_ready = sem("inv_ready")
        rc_ready = sem("rc_ready")
        norm_ready = sem("norm_ready")
        p_ready = sem("p_ready")
        pt_ready = sem("pt_ready")
        pts_ready = sem("pts_ready")
        pv_ready = sem("pv_ready")
        ot_ready = sem("ot_ready")
        y_ready = sem("y_ready")
        h_done = sem("h_done")

        JOBS = [("k", 0), ("q", 0), ("k", 1), ("q", 1)]

        def span(c):
            return bass.ds(c * CT, CT)

        with nc.Block() as block:
            @block.gpsimd
            def _(pool):
                for sm_ in (sub_ready, rot_used, pv_ready, h_done, pts_ready, ot_ready, pt_ready, p_ready, y_ready,
                            vx_ready):
                    pool.sem_inc(sm_, 1)

                def jobs(c):
                    for j, (which, t) in enumerate(JOBS):
                        dst = kr if which == "k" else qr
                        pool.wait_ge(rot_ready, c * 8 + 2 * j + 2)
                        nc.gpsimd.tensor_tensor(dst[:, t, 0], cos_t[:, j % 2, 0], sin_t[:, j % 2, 1],
                                                ALU.subtract).then_inc(rot_used, 1)
                        nc.gpsimd.tensor_tensor(dst[:, t, 1], cos_t[:, j % 2, 1], sin_t[:, j % 2, 0],
                                                ALU.add).then_inc(rot_used, 1)

                def units(c, first=False):
                    for u in range(NU):
                        e = ex[0:PW, u % 4]
                        pool.wait_ge(rc_ready, c * NU + u + 1)
                        nc.gpsimd.tensor_tensor(e, e, bc(rc[0:PW, u % 4].unsqueeze(2), [PW, 2 * HT, TOK]),
                                                ALU.mult).then_inc(norm_ready, 1)
                        pool.wait_ge(norm_ready, c * NU + u + 1)
                        if not first or u >= 4:
                            pool.wait_ge(pt_ready, c * NU + u - 4 + 1 + 1)
                        nc.gpsimd.tensor_tensor(pr[0:PW, u % 4, :, 0:TOK], e[:, 0:HT], e[:, HT:2 * HT],
                                                ALU.add).then_inc(p_ready, 1)

                jobs(0)
                units(0, first=True)
                with pool.Fori(1, CH) as i:
                    jobs(i)
                    units(i)

            @block.sync
            def _(sp):
                def jobs(c):
                    for b in range(2):
                        sp.wait_ge(vt_ready, c * PAIRS + 2 * b + 2)
                        for m in range(2):
                            for par in range(2):
                                sp.dma_start(vx[GAP * par:GAP * par + TOK, 4 * b + m:4 * b + 4:2, par, :],
                                             vt[GAP * m:GAP * m + TOK, 2 * b:2 * b + 2,
                                                par * 256:(par + 1) * 256]).then_inc(vx_ready, 16)

                jobs(0)
                with sp.Fori(1, CH) as i:
                    jobs(i)

            @block.tensor
            def _(pe):
                def job(c, j, first=False):
                    which, t = JOBS[j]
                    if j < 2:
                        if not first:
                            pe.wait_ge(sub_ready, c * NU - 1 + j + 1)
                    else:
                        pe.wait_ge(rot_ready, c * 8 + 2 * (j - 2) + 2)
                    for half in range(2):
                        o = (2 * ED if which == "k" else 0) + half * ED + t * P
                        for k in range(ET):
                            last = nc.tensor.matmul(p_s[:, j % 2, half, 0:CT], K["wqk"][:, k, o:o + P],
                                                    xn[:, k, span(c)], start=(k == 0), stop=(k == ET - 1))
                    last.then_inc(qk_ready, 1)

                def values(c, p, first=False):
                    if p == 0:
                        pe.wait_ge(xg_ready, c + 1)
                        if not first:
                            pe.wait_ge(h_done, c)
                    if p >= 2:
                        pe.wait_ge(vt_ready, c * PAIRS + p - 1)
                    for k in range(ET):
                        both = xg[:, k, 2 * p:2 * p + 2, :].rearrange("p a b -> p (a b)")
                        last = nc.tensor.matmul(p_v[0:PW, p % 2, :], both[:, 0:PW], K["wv"][:, k, :],
                                                start=(k == 0), stop=(k == ET - 1))
                    last.then_inc(v_ready, 1)

                def scores(c, u):
                    t, p = u // PAIRS, u % PAIRS
                    if u < 2:
                        pe.wait_ge(rot_ready, c * 8 + 2 * (u + 2) + 2)
                    else:
                        pe.wait_ge(sub_ready, c * NU + u - 1 + 1)
                    if p == 0:
                        pe.wait_ge(kx_dve, (c * ET + t + 1) * 4)
                        pe.wait_ge(kx_act, (c * ET + t + 1) * 4)
                        pe.wait_ge(rot_used, c * 8 + 4 * t + 4 + 1)
                    for m in range(2):
                        img = 2 * p + m
                        for half in range(2):
                            last = nc.tensor.matmul(
                                p_s[GAP * m:GAP * m + TOK, u % 2, half, 0:BW],
                                qr[:, t, half, img * TOK:(img + 1) * TOK],
                                kx[:, t, half, img].rearrange("p a b -> p (a b)"), start=True, stop=True)
                    last.then_inc(s_ready, 1)

                def turn(c, u):
                    pe.wait_ge(p_ready, c * NU + u + 1 + 1)
                    pe.wait_ge(pts_ready, c * NU + u + 1)
                    for hp in range(4):
                        src = pr[0:PW, u % 4, 2 * hp:2 * hp + 2, :].rearrange("p a b -> p (a b)")
                        last = nc.tensor.transpose(p_t[0:PW, hp * PW:(hp + 1) * PW], src[:, 0:PW], ident[0:PW, 0:PW])
                    last.then_inc(pt_ready, 1)

                def attend(c, u):
                    t, p = u // PAIRS, u % PAIRS
                    if u == 0:
                        pe.wait_ge(vx_ready, (c + 1) * VX_IN + 1)
                    pe.wait_ge(pts_ready, c * NU + u + 1 + 1)
                    pe.wait_ge(ot_ready, c * NU + u + 1)
                    for m in range(2):
                        for hl in range(HT):
                            hg = t * HT + hl
                            last = nc.tensor.matmul(
                                p_o[32 * (hl % 4):32 * (hl % 4) + 32,
                                    (hl // 4) * 2 * TOK + m * TOK:(hl // 4) * 2 * TOK + (m + 1) * TOK],
                                vx[0:PW, 2 * p + m, hl % 2, (hg // 2) * 32:(hg // 2 + 1) * 32],
                                pts[0:PW, u % 2, (hl // 2) * PW + GAP * m:(hl // 2) * PW + GAP * m + TOK],
                                start=True, stop=True)
                    last.then_inc(pv_ready, 1)

                def project(c, t, more=True):
                    if t == 0:
                        pe.wait_ge(ot_ready, c * NU + NU + 1)
                        if more:
                            pe.wait_ge(vt_ready, (c + 2) * PAIRS)
                    for k in range(4):
                        last = nc.tensor.matmul(p_v[:, t, 0:CT], K["wp"][:, k, t * P:(t + 1) * P],
                                                ot[:, k, :], start=(k == 0), stop=(k == 3))
                    if t == ET - 1:
                        last.then_inc(y_ready, 1)

                def steps(c, lo, hi, first=False, more=True):
                    for s in range(lo, hi):
                        if s < NU:
                            scores(c, s)
                        elif more:
                            job(c + 1, s - NU)
                        if s < 2:
                            values(c, 2 * s, first)
                            values(c, 2 * s + 1, first)
                        elif s < 4 and not first:
                            project(c - 1, s - 2)
                        if 3 <= s < NU + 3:
                            turn(c, s - 3)
                        if s >= 4:
                            attend(c, s - 4)

                pe.wait_ge(K["loaded"], 80)
                for j in range(4):
                    job(0, j, first=True)
                steps(0, 0, 4, first=True)
                with pe.Fori(0, CH - 1) as i:
                    steps(i, 4, NU + 4)
                    steps(i + 1, 0, 4)
                steps(CH - 1, 4, NU + 4, more=False)
                for t in range(ET):
                    project(CH - 1, t, more=False)

            @block.scalar
            def _(act):
                def gather(c):
                    nc.scalar.copy(xg[:, :, :, 0:TOK],
                                   xn[:, :, span(c)].rearrange("p t (a b) -> p t a b", b=TOK)).then_inc(xg_ready, 1)

                def expand(c, t, heads):
                    act.wait_ge(rot_used, c * 8 + 4 * t + 2 + 1)
                    for hh in heads:
                        for half in range(2):
                            last = nc.scalar.activation(
                                kx[:, t, half, :, hh, :], kr[:, t, half].rearrange("p (a b) -> p a b", b=TOK),
                                ACT.Copy, scale=K["mask0"][:, hh:hh + 1])
                        last.then_inc(kx_act, 1)

                def values(c, p):
                    if p == 0:
                        act.wait_ge(vx_ready, c * VX_IN + 1)
                    act.wait_ge(v_ready, c * PAIRS + p + 1)
                    nc.scalar.copy(vt[0:PW, p, :], p_v[0:PW, p % 2, :]).then_inc(vt_ready, 1)

                def steps(c, lo, hi, more=True):
                    for s in range(lo, hi):
                        if 3 <= s < NU + 3:
                            u = s - 3
                            act.wait_ge(pt_ready, c * NU + u + 1 + 1)
                            nc.scalar.copy(pts[0:PW, u % 2], p_t[0:PW, 0:4 * PW]).then_inc(pts_ready, 1)
                        if s < NU:
                            act.wait_ge(sub_ready, c * NU + s + 1 + 1)
                            nc.scalar.activation(ex[0:PW, s % 4], ex[0:PW, s % 4], ACT.Exp).then_inc(exp_ready, 1)
                        if s < 2:
                            values(c, 2 * s)
                            values(c, 2 * s + 1)
                        if s < 2:
                            expand(c, 1, range(4 + 2 * s, 6 + 2 * s))
                        if s >= 4:
                            u = s - 4
                            t, p = u // PAIRS, u % PAIRS
                            act.wait_ge(pv_ready, c * NU + u + 1 + 1)
                            act.wait_ge(y_ready, c + 1)
                            nc.scalar.copy(ot[:, 2 * t:2 * t + 2, p * 2 * TOK:(p + 1) * 2 * TOK],
                                           p_o[:, 0:4 * TOK].rearrange("p (a b) -> p a b", a=2)).then_inc(ot_ready, 1)
                        if more and s == 5:
                            act.wait_ge(v_ready, (c + 1) * PAIRS)
                            gather(c + 1)
                        if more and s in (NU + 1, NU + 2):
                            expand(c + 1, 0, range(4, 6) if s == NU + 1 else range(6, HT))

                nc.scalar.preload_act_table_set("natural_log_exp_and_others")
                gather(0)
                expand(0, 0, range(4, HT))
                steps(0, 0, 4)
                with act.Fori(0, CH - 1) as i:
                    steps(i, 4, NU + 4)
                    steps(i + 1, 0, 4)
                steps(CH - 1, 4, NU + 4, more=False)

            @block.vector
            def _(dve):
                def rotate(c, j):
                    dve.wait_ge(qk_ready, c * 4 + j + 1)
                    dve.wait_ge(rot_used, c * 8 + (2 * j - 2 if j >= 2 else 0) + 1)
                    for dst, col in ((cos_t, C_COS), (sin_t, C_SIN)):
                        table = cs[:, col:col + TOK].unsqueeze(1)
                        for half in range(2):
                            last = nc.vector.tensor_tensor(
                                dst[:, j % 2, half].rearrange("p (a b) -> p a b", b=TOK),
                                p_s[:, j % 2, half, 0:CT].rearrange("p (a b) -> p a b", b=TOK),
                                bc(table, [P, CI, TOK]), ALU.mult)
                        last.then_inc(rot_ready, 1)

                def expand(c, t, heads):
                    dve.wait_ge(rot_used, c * 8 + 4 * t + 2 + 1)
                    for hh in heads:
                        for half in range(2):
                            last = nc.vector.tensor_scalar(
                                kx[:, t, half, :, hh, :], kr[:, t, half].rearrange("p (a b) -> p a b", b=TOK),
                                K["mask0"][:, hh:hh + 1], None, ALU.mult)
                        last.then_inc(kx_dve, 1)

                def steps(c, lo, hi, first=False, more=True):
                    for s in range(lo, hi):
                        u = s - 1
                        if s < NU:
                            dve.wait_ge(s_ready, c * NU + s + 1)
                            sc = p_s[0:PW, s % 2, :, 0:BW].rearrange("p a (b c) -> p a b c", c=TOK)
                            nc.vector.tensor_reduce(mx[0:PW, s % 2].rearrange("p (a b) -> p a b", a=2), sc,
                                                    AX.X, ALU.max).then_inc(max_ready, 1)
                        if 0 <= u < NU:
                            dve.wait_ge(exp_ready, c * NU + u + 1)
                            nc.vector.tensor_reduce(sm[0:PW, u % 2], ex[0:PW, u % 4], AX.X, ALU.add).then_inc(sum_ready, 1)
                        if s < NU:
                            dve.wait_ge(max_ready, c * NU + s + 1)
                            if not first:
                                dve.wait_ge(p_ready, c * NU + s - 4 + 1 + 1)
                            nc.vector.tensor_tensor(
                                ex[0:PW, s % 4].rearrange("p (a b) c -> p a b c", a=2), sc,
                                bc(mx[0:PW, s % 2].rearrange("p (a b) -> p a b", a=2).unsqueeze(3), [PW, 2, HT, TOK]),
                                ALU.subtract).then_inc(sub_ready, 1)
                        if 0 <= u < NU:
                            dve.wait_ge(sum_ready, c * NU + u + 1)
                            nc.vector.reciprocal(rc[0:PW, u % 4], sm[0:PW, u % 2]).then_inc(inv_ready, 1)
                            dve.wait_ge(inv_ready, c * NU + u + 1)
                            nc.vector.tensor_scalar(rc[0:PW, u % 4, HT:2 * HT], rc[0:PW, u % 4, HT:2 * HT],
                                                    K["neglam"][0:PW, 0:1], None, ALU.mult).then_inc(rc_ready, 1)
                        if s < 2:
                            expand(c, 1, range(2 * s, 2 * s + 2))
                        if s >= NU and more:
                            rotate(c + 1, s - NU)
                        if s == NU + 1 and more:
                            expand(c + 1, 0, range(4))

                def add(c):
                    dve.wait_ge(y_ready, c + 1 + 1)
                    nc.vector.tensor_tensor(h[:, :, span(c)], h[:, :, span(c)], p_v[:, :, 0:CT], ALU.add).then_inc(h_done, 1)

                rotate(0, 0)
                rotate(0, 1)
                expand(0, 0, range(4))
                rotate(0, 2)
                rotate(0, 3)
                steps(0, 0, 4, first=True)
                with dve.Fori(0, CH - 1) as i:
                    steps(i, 4, NU + 4)
                    steps(i + 1, 0, 4)
                    add(i)
                steps(CH - 1, 4, NU + 4, more=False)
                add(CH - 1)



def quantised_ffn(nc, K):
    h, xn, ident = K["h"], K["xn"], K["ident"]
    with ExitStack() as st:
        def sb(n, shape, dt=F32):
            return st.enter_context(nc.sbuf_tensor(f"ff_{n}", shape, dt))

        def sem(n):
            return st.enter_context(nc.semaphore(f"ff_{n}"))

        gate = sb("gate", [P, IT, NT])
        up = sb("up", [P, IT, NT])
        gq = sb("gq", [P, IT, NT], I16)
        uq = sb("uq", [P, IT, NT], I16)
        sg = sb("sg", [P, 2, NT])
        sq = sb("sq", [P, 2, NT], U16)
        xq = sb("xq", [P, ET, NT], I16)
        oq = sb("oq", [P, 2, IT, CT], I16)
        of = gate[:].rearrange("p a b -> p (a b)")[:, 0:2 * IT * CT].rearrange("p (s a b) -> p s a b", s=2, b=CT)
        part = sb("part", [P, 4, IT * CH])
        pmax = sb("pmax", [P, 8])
        grow = sb("grow", [1, 8])
        sc = sb("sc", [P, 24])
        onesr = sb("onesr", [1, P])

        p_t = st.enter_context(nc.psum_tensor("ff_t", [P, 512], F32))
        p_b = st.enter_context(nc.psum_tensor("ff_b", [P, 512], F32))
        p_g = st.enter_context(nc.psum_tensor("ff_g", [P, 2, 2, 512], F32))

        ones_ready = sem("ones_ready")
        pm_ready = sem("pm_ready")
        turned = sem("turned")
        row_ready = sem("row_ready")
        spread = sem("spread")
        scale = sem("scale")
        xq_int = sem("xq_int")
        x_ready = sem("x_ready")
        gu_ready = sem("gu_ready")
        gu_copied = sem("gu_copied")
        gu_max = sem("gu_max")
        gq_ready = sem("gq_ready")
        uq_ready = sem("uq_ready")
        sg_ready = sem("sg_ready")
        sq_ready = sem("sq_ready")
        act_ready = sem("act_ready")
        act_max = sem("act_max")
        aq_first = sem("aq_first")
        aq_ready = sem("aq_ready")
        o_ready = sem("o_ready")
        o_max = sem("o_max")
        oq_ready = sem("oq_ready")
        of_ready = sem("of_ready")
        y_ready = sem("y_ready")
        h_done = sem("h_done")

        QM = 1.0 / 32767.0
        GS = CH * IT // 2
        ROUND = [(0, 1), (1, 1), (2, 2), (4, 1)]
        X, INV_X = 0, 1
        GMAX, GATE, INV_G, TO_GATE = 2, 3, 4, 5
        UNIT = 6
        AUMAX, ACTS, UPS, INV_AU, TO_ACT, TO_UP = 8, 10, 11, 12, 14, 15
        PROD, PMAX, OUT, INV_O, TO_OUT = 16, 17, 18, 19, 20

        def cols(c):
            return slice(c * CT, (c + 1) * CT)

        with nc.Block() as block:
            @block.tensor
            def _(pe):
                def turn_max(n):
                    c, w = ROUND[n]
                    pe.wait_ge(pm_ready, n + 1)
                    for j in range(w):
                        last = nc.tensor.transpose(p_t[0:1, j * P:(j + 1) * P], pmax[:, c + j:c + j + 1], ident)
                    last.then_inc(turned, 1)

                def spread_max(n):
                    c, w = ROUND[n]
                    pe.wait_ge(row_ready, n + 1)
                    nc.tensor.matmul(p_b[:, c:c + w], onesr[0:1, :], grow[0:1, c:c + w],
                                     start=True, stop=True).then_inc(spread, 1)

                def product(m, n):
                    c, o = n // (IT // 2), n % (IT // 2) * 2
                    if m == 0:
                        pe.wait_ge(x_ready, c + 1)
                    step = m * GS + n
                    if step >= 2:
                        pe.wait_ge(gu_copied, step - 1)
                        pe.wait_ge(gu_max, step - 1)
                    for j in range(2):
                        for k in range(ET):
                            last = nc.tensor.matmul(p_g[:, n % 2, j, 0:CT],
                                                    K[("wgate", "wup")[m]][:, k, (o + j) * P:(o + j + 1) * P],
                                                    xn[:, k, cols(c)], start=(k == 0), stop=(k == ET - 1))
                    last.then_inc(gu_ready, 1)

                pe.wait_ge(ones_ready, 1)
                turn_max(0)
                spread_max(0)
                for n in range(GS):
                    product(0, n)
                product(1, 0)
                turn_max(1)
                product(1, 1)
                spread_max(1)
                for n in range(2, GS):
                    product(1, n)
                for n in (2, 3):
                    turn_max(n)
                    spread_max(n)
                for c in range(CH):
                    pe.wait_ge(of_ready, c + 1)
                    if c >= 2:
                        pe.wait_ge(h_done, c - 1)
                    for t in range(ET):
                        for k in range(IT):
                            last = nc.tensor.matmul(p_g[:, c % 2, t, 0:CT], K["wdown"][:, k, t * P:(t + 1) * P],
                                                    of[:, c % 2, k], start=(k == 0), stop=(k == IT - 1))
                    last.then_inc(y_ready, 1)

            @block.scalar
            def _(act):
                def keep(m, n):
                    c, o = n // (IT // 2), n % (IT // 2) * 2
                    step = m * GS + n
                    act.wait_ge(gu_ready, step + 1)
                    act.wait_ge(gu_max, step + 1)
                    nc.scalar.copy((gate, up)[m][:, o:o + 2, cols(c)], p_g[:, n % 2, :, 0:CT]).then_inc(gu_copied, 1)

                def sigmoid(o):
                    nc.scalar.activation(gq[:, o], gate[:, o], ACT.Copy, scale=sc[:, TO_GATE:TO_GATE + 1]).then_inc(gq_ready, 1)
                    act.wait_ge(gq_ready, o + 1)
                    if o >= 2:
                        act.wait_ge(sq_ready, o - 1)
                    nc.scalar.activation(sg[:, o % 2], gq[:, o], ACT.Sigmoid,
                                         scale=sc[:, GATE:GATE + 1]).then_inc(sg_ready, 1)

                nc.scalar.preload_act_table_set("sigmoid_and_others")
                for n in range(GS):
                    keep(0, n)
                keep(1, 0)
                keep(1, 1)
                act.wait_ge(scale, 6)
                act.wait_ge(gu_copied, GS)
                for n in range(2, GS):
                    if n - 2 < IT:
                        sigmoid(n - 2)
                    keep(1, n)
                nc.scalar.preload_act_table_set("natural_log_exp_and_others")
                act.wait_ge(scale, 12)
                act.wait_ge(gu_copied, 2 * GS)
                for o in range(IT):
                    if o:
                        nc.scalar.activation(gq[:, o], gate[:, o], ACT.Copy, scale=sc[:, TO_ACT:TO_ACT + 1]).then_inc(aq_ready, 1)
                    nc.scalar.activation(uq[:, o], up[:, o], ACT.Copy, scale=sc[:, TO_UP:TO_UP + 1]).then_inc(uq_ready, 1)

            @block.vector
            def _(dve):
                nc.vector.memset(onesr[:], 1.0).then_inc(ones_ready, 1)
                steps = [0]

                def link(ins):
                    steps[0] += 1
                    ins.then_inc(scale, 1)
                    dve.wait_ge(scale, steps[0])

                def one(c, w=1):
                    return sc[:, c:c + w]

                def row_max(n):
                    c, w = ROUND[n]
                    dve.wait_ge(turned, n + 1)
                    nc.vector.tensor_reduce(grow[0:1, c:c + w], p_t[0:1, 0:w * P].rearrange("p (a b) -> p a b", a=w),
                                            AX.X, ALU.max).then_inc(row_ready, 1)

                def global_max(n):
                    c, w = ROUND[n]
                    dve.wait_ge(spread, n + 1)
                    return p_b[:, c:c + w]

                def step_max(m, n):
                    step = m * GS + n
                    dve.wait_ge(gu_ready, step + 1)
                    nc.vector.tensor_reduce(part[:, m, 2 * n:2 * n + 2], p_g[:, n % 2, :, 0:CT], AX.X, ALU.max,
                                            apply_absolute_value=True).then_inc(gu_max, 1)

                nc.vector.tensor_reduce(pmax[:, 0:1], K["xmax"][:], AX.X, ALU.max).then_inc(pm_ready, 1)
                row_max(0)
                link(nc.vector.tensor_scalar(one(X), global_max(0), QM, 1e-12, ALU.mult, ALU.max))
                link(nc.vector.reciprocal(one(INV_X), one(X)))
                for c in range(CH):
                    nc.vector.tensor_scalar(xq[:, :, cols(c)], xn[:, :, cols(c)], one(INV_X), None,
                                            ALU.mult).then_inc(xq_int, 1)
                    dve.wait_ge(xq_int, c + 1)
                    nc.vector.tensor_copy(xn[:, :, cols(c)], xq[:, :, cols(c)]).then_inc(x_ready, 1)
                for n in range(GS):
                    step_max(0, n)
                dve.wait_ge(gu_max, GS)
                nc.vector.tensor_reduce(pmax[:, 1:2], part[:, 0], AX.X, ALU.max).then_inc(pm_ready, 1)
                step_max(1, 0)
                row_max(1)
                step_max(1, 1)
                link(nc.vector.tensor_scalar(one(GMAX), global_max(1), one(X), None, ALU.mult))
                link(nc.vector.tensor_scalar(one(GATE), one(GMAX), QM, 1e-12, ALU.mult, ALU.max))
                link(nc.vector.reciprocal(one(INV_G), one(GATE)))
                link(nc.vector.tensor_scalar(one(TO_GATE), one(INV_G), one(X), None, ALU.mult))
                link(nc.vector.tensor_scalar(one(UNIT), one(GATE), 1.0 / 65536.0, None, ALU.mult))
                link(nc.vector.tensor_copy(one(UNIT + 1), one(X)))

                def round_sigmoid(o):
                    dve.wait_ge(sg_ready, o + 1)
                    nc.vector.tensor_scalar(sq[:, o % 2], sg[:, o % 2], 65536.0, None, ALU.mult).then_inc(sq_ready, 1)

                def gate_sigmoid(o):
                    dve.wait_ge(sq_ready, o + 1)
                    nc.vector.tensor_tensor(gate[:, o], gq[:, o], sq[:, o % 2], ALU.mult).then_inc(act_ready, 1)

                def gate_max(o):
                    dve.wait_ge(act_ready, o + 1)
                    nc.vector.tensor_reduce(part[:, 2, o:o + 1], gate[:, o], AX.X, ALU.max,
                                            apply_absolute_value=True).then_inc(act_max, 1)

                pieces = [(round_sigmoid, 0)]
                for o in range(IT):
                    if o + 1 < IT:
                        pieces.append((round_sigmoid, o + 1))
                    pieces += [(gate_sigmoid, o), (gate_max, o)]
                for n in range(2, GS):
                    step_max(1, n)
                    for piece, o in pieces[2 * (n - 2):2 * (n - 1)]:
                        piece(o)
                dve.wait_ge(act_max, IT)
                nc.vector.tensor_reduce(pmax[:, 2:3], part[:, 2, 0:IT], AX.X, ALU.max)
                dve.wait_ge(gu_max, 2 * GS)
                nc.vector.tensor_reduce(pmax[:, 3:4], part[:, 1], AX.X, ALU.max).then_inc(pm_ready, 1)
                row_max(2)
                link(nc.vector.tensor_tensor(one(AUMAX, 2), global_max(2), one(UNIT, 2), ALU.mult))
                link(nc.vector.tensor_scalar(one(ACTS, 2), one(AUMAX, 2), QM, 1e-12, ALU.mult, ALU.max))
                link(nc.vector.reciprocal(one(INV_AU, 2), one(ACTS, 2)))
                link(nc.vector.tensor_tensor(one(TO_ACT, 2), one(INV_AU, 2), one(UNIT, 2), ALU.mult))
                nc.vector.tensor_scalar(gq[:, 0], gate[:, 0], one(TO_ACT), None, ALU.mult).then_inc(aq_first, 1)
                link(nc.vector.tensor_tensor(one(PROD), one(ACTS), one(UPS), ALU.mult))
                for o in range(IT):
                    if o == 0:
                        dve.wait_ge(aq_first, 1)
                    else:
                        dve.wait_ge(aq_ready, o)
                    dve.wait_ge(uq_ready, o + 1)
                    nc.vector.tensor_tensor(up[:, o], gq[:, o], uq[:, o], ALU.mult).then_inc(o_ready, 1)
                    dve.wait_ge(o_ready, o + 1)
                    nc.vector.tensor_reduce(part[:, 3, o:o + 1], up[:, o], AX.X, ALU.max,
                                            apply_absolute_value=True).then_inc(o_max, 1)
                dve.wait_ge(o_max, IT)
                nc.vector.tensor_reduce(pmax[:, 4:5], part[:, 3, 0:IT], AX.X, ALU.max).then_inc(pm_ready, 1)
                row_max(3)
                link(nc.vector.tensor_scalar(one(PMAX), global_max(3), one(PROD), None, ALU.mult))
                link(nc.vector.tensor_scalar(one(OUT), one(PMAX), QM, 1e-12, ALU.mult, ALU.max))
                link(nc.vector.reciprocal(one(INV_O), one(OUT)))
                link(nc.vector.tensor_scalar(one(TO_OUT), one(INV_O), one(PROD), None, ALU.mult))
                for c in range(CH + 1):
                    if c < CH:
                        nc.vector.tensor_scalar(oq[:, c % 2], up[:, :, cols(c)], one(TO_OUT), None,
                                                ALU.mult).then_inc(oq_ready, 1)
                        dve.wait_ge(oq_ready, c + 1)
                        if c >= 2:
                            dve.wait_ge(y_ready, c - 1)
                        nc.vector.tensor_copy(of[:, c % 2], oq[:, c % 2]).then_inc(of_ready, 1)
                    if c >= 1:
                        dve.wait_ge(y_ready, c)
                        if c < CH:
                            dve.wait_ge(of_ready, c + 1)
                        nc.vector.scalar_tensor_tensor(out=h[:, :, cols(c - 1)], in0=p_g[:, (c - 1) % 2, :, 0:CT],
                                                       scalar=one(OUT), in1=h[:, :, cols(c - 1)],
                                                       op0=ALU.mult, op1=ALU.add).then_inc(h_done, 1)


def cosine_attention(nc, K, wq1, routT, leafT, woutT):
    h, xn, cs, ident = K["h"], K["xn"], K["cst"], K["ident"]
    NU = PAIRS
    BW = HT * TOK
    HI = CI // 2
    HC = HI * TOK
    with ExitStack() as st:
        def sb(n, shape, dt=F32):
            return st.enter_context(nc.sbuf_tensor(f"ca_{n}", shape, dt))

        def ps(n, shape):
            return st.enter_context(nc.psum_tensor(f"ca_{n}", shape, F32))

        def sem(n):
            return st.enter_context(nc.semaphore(f"ca_{n}"))

        xg = K["xg"]
        pr = K["pr"][:].rearrange("p (s a b) -> p s a b", s=2, b=GAP)
        raw = sb("raw", [P, 2, ET, CT])
        sq = sb("sq", [P, 2, ET, CT])
        ss = sb("ss", [P, 2, ET, CT])
        ls = sb("ls", [P, 2, ET, CT])
        inv = sb("inv", [P, 2, ET, CT])
        qn = sb("qn", [P, ET, CT])
        kn = sb("kn", [P, ET, CT])
        kx = sb("kx", [P, ET, CI, HT, TOK])
        vx = sb("vx", [P, CI, HT, 2, HD])
        vs = sb("vs", [P, PAIRS, HT, 2, HD])
        ex = sb("ex", [P, 4, HEADS, TOK])
        pts = sb("pts", [P, 2, 2, 4 * PW])
        mx = sb("mx", [P, 2, HEADS])
        sm = sb("sm", [P, 2, HEADS])
        rc = sb("rc", [P, 4, HEADS])

        p_s = ps("p_s", [P, 2, 2, 512])
        p_t = ps("p_t", [P, 512])
        p_o = ps("p_o", [P, 512])
        p_x = ps("p_x", [P, 2, 512])

        init = sem("init")
        gap_zero = sem("gap_zero")
        tree_in = sem("tree_in")
        fold_ready = sem("fold_ready")
        fold_kept = sem("fold_kept")
        xg_ready = sem("xg_ready")
        qk_ready = sem("qk_ready")
        raw_kept = sem("raw_kept")
        sq_ready = sem("sq_ready")
        ss_ready = sem("ss_ready")
        ss_kept = sem("ss_kept")
        log_ready = sem("log_ready")
        inv_ready = sem("inv_ready")
        kn_ready = sem("kn_ready")
        qn_ready = sem("qn_ready")
        kx_dve = sem("kx_dve")
        kx_act = sem("kx_act")
        v_ready = sem("v_ready")
        vs_ready = sem("vs_ready")
        vx_ready = sem("vx_ready")
        s_ready = sem("s_ready")
        max_ready = sem("max_ready")
        sub_ready = sem("sub_ready")
        exp_ready = sem("exp_ready")
        sum_ready = sem("sum_ready")
        rc_ready = sem("rc_ready")
        p_ready = sem("p_ready")
        pt_ready = sem("pt_ready")
        pts_ready = sem("pts_ready")
        pv_ready = sem("pv_ready")
        h_done = sem("h_done")

        def span(c):
            return bass.ds(c * CT, CT)

        with nc.Block() as block:
            @block.gpsimd
            def _(pool):
                nc.gpsimd.memset(vx[:], 0.0).then_inc(init, 1)
                nc.gpsimd.memset(vs[:], 0.0).then_inc(init, 1)

                def units(c, first=False):
                    for s in range(NU):
                        u = c * NU + s
                        pool.wait_ge(rc_ready, u + 1)
                        if not first or s >= 2:
                            pool.wait_ge(pt_ready, (u - 2) * 2 + 2)
                        nc.gpsimd.tensor_tensor(pr[0:PW, s % 2, :, 0:TOK], ex[0:PW, s % 4],
                                                bc(rc[0:PW, s % 4].unsqueeze(2), [PW, HEADS, TOK]),
                                                ALU.mult).then_inc(p_ready, 1)

                units(0, first=True)
                with pool.Fori(1, CH) as i:
                    units(i)

            @block.sync
            def _(sp):
                for name, src in (("wq1", wq1), ("rout", routT), ("leaf", leafT), ("wout", woutT)):
                    sp.dma_start(K[name][:], src).then_inc(tree_in, 16)

                def send(c):
                    for b in range(2):
                        sp.wait_ge(vs_ready, c * 2 + b + 1)
                        sp.dma_start(vx[GAP:GAP + TOK, 4 * b:4 * b + 4:2], vs[0:TOK, 2 * b:2 * b + 2]).then_inc(vx_ready, 16)
                        sp.dma_start(vx[0:TOK, 4 * b + 1:4 * b + 4:2], vs[GAP:GAP + TOK, 2 * b:2 * b + 2]).then_inc(vx_ready, 16)

                send(0)
                with sp.Fori(1, CH) as i:
                    send(i)

            @block.tensor
            def _(pe):
                def project(n, j, t, first=False):
                    bank = t if j == 0 else 1 - t
                    if j == 1:
                        pe.wait_ge(ss_kept, n * 4 + t + 1)
                    elif t == 0:
                        if not first:
                            pe.wait_ge(ss_kept, n * 4)
                    elif not first:
                        pe.wait_ge(vs_ready, (n - 1) * 2)
                    o = (1 - j) * ED + t * P
                    for k in range(ET):
                        last = nc.tensor.matmul(p_x[:, bank, 0:CT], K["w1qk"][:, k, o:o + P],
                                                xn[:, k, span(n)], start=(k == 0), stop=(k == ET - 1))
                    last.then_inc(qk_ready, 1)

                def squares(n, j, t, first=False):
                    pe.wait_ge(sq_ready, n * 4 + 2 * j + t + 1)
                    if j == 0 and t == 0:
                        pe.wait_ge(raw_kept, n * 4 + 2)
                    if j == 0 and t == 1 and not first:
                        pe.wait_ge(vs_ready, (n - 1) * 2 + 1)
                    nc.tensor.matmul(p_x[:, 1 - t, 0:CT], cs[:, C_BD:C_BD + P], sq[:, j, t],
                                     start=True, stop=True).then_inc(ss_ready, 1)

                def values(c, b, more):
                    if b == 0:
                        pe.wait_ge(xg_ready, c + 1)
                        if more:
                            pe.wait_ge(raw_kept, (c + 1) * 4 + 1)
                    elif more:
                        pe.wait_ge(ss_kept, (c + 1) * 4 + 3)
                    if not more:
                        pe.wait_ge(ss_kept, (c + 1) * 4)
                    for q in range(2):
                        p = 2 * b + q
                        for k in range(ET):
                            both = xg[:, k, 2 * p:2 * p + 2, :].rearrange("p a b -> p (a b)")
                            last = nc.tensor.matmul(p_x[0:PW, b, q * ED:(q + 1) * ED], both[:, 0:PW],
                                                    K["w1v"][:, k, :], start=(k == 0), stop=(k == ET - 1))
                    last.then_inc(v_ready, 1)

                def scores(c, s, first):
                    if not first or s >= 2:
                        pe.wait_ge(sub_ready, c * NU + s - 1)
                    if s % 2 == 0:
                        for ready in (kx_dve, kx_act, qn_ready):
                            pe.wait_ge(ready, c * 2 + s // 2 + 1)
                    for m in range(2):
                        img = 2 * s + m
                        for t in range(ET):
                            last = nc.tensor.matmul(p_s[GAP * m:GAP * m + TOK, s % 2, t, 0:BW],
                                                    qn[:, t, img * TOK:(img + 1) * TOK],
                                                    kx[:, t, img].rearrange("p a b -> p (a b)"), start=True, stop=True)
                    last.then_inc(s_ready, 1)

                def turn(c, s, b, first):
                    u = c * NU + s
                    if b == 0:
                        pe.wait_ge(p_ready, u + 1)
                    if first and s == b == 0:
                        pe.wait_ge(fold_kept, 1)
                    if not first or s or b:
                        pe.wait_ge(pts_ready, u * 2 + b)
                    for hq in range(4):
                        src = pr[0:PW, s % 2, 8 * b + 2 * hq:8 * b + 2 * hq + 2, :].rearrange("p a b -> p (a b)")
                        last = nc.tensor.transpose(p_t[0:PW, hq * PW:(hq + 1) * PW], src[:, 0:PW], ident[0:PW, 0:PW])
                    last.then_inc(pt_ready, 1)

                def attend(c, s, first):
                    pair = s % NU
                    u = c * NU + s
                    if pair % 2 == 0:
                        pe.wait_ge(vx_ready, (c if s >= 0 else c - 1) * 64 + 32 * (pair // 2) + 32)
                    pe.wait_ge(pts_ready, u * 2 + 2)
                    if not first or s:
                        pe.wait_ge(h_done, u)
                    for m in range(2):
                        for hp in range(HT):
                            col = (hp // 4) * 2 * TOK + m * TOK
                            last = nc.tensor.matmul(
                                p_o[32 * (hp % 4):32 * (hp % 4) + 32, col:col + TOK],
                                vx[0:PW, 2 * pair + m, hp].rearrange("p a b -> p (a b)"),
                                pts[0:PW, pair % 2, hp // 4, (hp % 4) * PW + GAP * m:(hp % 4) * PW + GAP * m + TOK],
                                start=True, stop=True)
                    last.then_inc(pv_ready, 1)

                def steps(c, first=False, more=True):
                    for s in range(NU if more else NU + 3):
                        if s < NU:
                            scores(c, s, first)
                        turns = (not first or s >= 2) and s - 2 < NU
                        if more and s == 0:
                            project(c + 1, 0, 0)
                        if turns:
                            turn(c, s - 2, 0, first)
                        if more:
                            if s == 0:
                                if first:
                                    pe.wait_ge(ss_kept, 4)
                                    project(c + 1, 0, 1, first=True)
                                else:
                                    project(c + 1, 0, 1)
                            if s == 1:
                                squares(c + 1, 0, 0)
                                squares(c + 1, 0, 1)
                        if not first or s >= 3:
                            attend(c, s - 3, first)
                        if turns:
                            turn(c, s - 2, 1, first)
                        if s == 0:
                            values(c, 0, more)
                        if more and s == 1:
                            project(c + 1, 1, 0)
                            project(c + 1, 1, 1)
                        if more and s == 2:
                            squares(c + 1, 1, 0)
                            squares(c + 1, 1, 1)
                        if s == 3:
                            values(c, 1, more)

                for j in range(2):
                    for t in range(ET):
                        project(0, j, t, first=True)
                    for t in range(ET):
                        squares(0, j, t, first=True)
                pe.wait_ge(tree_in, 64)
                for bank, a, b, cols in ((p_o, "wq1", "rout", LEAVES - 1), (p_t, "leaf", "wout", ED)):
                    for t in range(ET):
                        for k in range(ET):
                            last = nc.tensor.matmul(bank[:, t * 256:t * 256 + cols], K[a][:, k, t * P:(t + 1) * P],
                                                    K[b][:, k, :], start=(k == 0), stop=(k == ET - 1))
                    last.then_inc(fold_ready, 1)
                pe.wait_ge(gap_zero, 1)
                steps(0, first=True)
                with pe.Fori(1, CH - 1) as i:
                    steps(i)
                steps(CH - 1, more=False)

            @block.scalar
            def _(act):
                def gather(c, first=False):
                    if not first:
                        act.wait_ge(v_ready, c * 2)
                    nc.scalar.copy(xg[:, :, :, 0:TOK],
                                   xn[:, :, span(c)].rearrange("p t (a b) -> p t a b", b=TOK)).then_inc(xg_ready, 1)

                def square(n, j, t):
                    act.wait_ge(raw_kept, n * 4 + 2 * j + t + 1)
                    nc.scalar.activation(sq[:, j, t], raw[:, j, t], ACT.Square).then_inc(sq_ready, 1)

                def inverse(n, j):
                    act.wait_ge(ss_kept, n * 4 + 2 * j + 2)
                    nc.scalar.activation(ls[:, j], ss[:, j], ACT.Ln, scale=L2_SCALE).then_inc(log_ready, 1)
                    act.wait_ge(log_ready, n * 2 + j + 1)
                    nc.scalar.activation(inv[:, j], ls[:, j], ACT.Exp, scale=-0.5,
                                         bias=K["eps"][:, 1:2]).then_inc(inv_ready, 1)

                def expand(n, half, first=False):
                    act.wait_ge(kn_ready, n + 1)
                    if not first:
                        act.wait_ge(s_ready, n * NU + 2 * half - 2)
                    for t in range(ET):
                        for hh in range(6, HT):
                            last = nc.scalar.activation(
                                kx[:, t, half * HI:(half + 1) * HI, hh, :],
                                kn[:, t, half * HC:(half + 1) * HC].rearrange("p (a b) -> p a b", b=TOK),
                                ACT.Copy, scale=K["mask1"][:, hh:hh + 1])
                    last.then_inc(kx_act, 1)

                def values(c, b, first=False):
                    act.wait_ge(v_ready, c * 2 + b + 1)
                    if not first:
                        act.wait_ge(pv_ready, (c - 1) * NU + 2 * b + 2)
                    if not first or b:
                        act.wait_ge(vx_ready, c * 64 + b * 32)
                    v = p_x[:, b].rearrange("p (q a b c) -> p q a b c", q=2, a=2, c=HD)
                    im = slice(4 * b, 4 * b + 4, 2)
                    im1 = slice(4 * b + 1, 4 * b + 4, 2)
                    pp = slice(2 * b, 2 * b + 2)
                    nc.scalar.copy(vs[0:TOK, pp, :, 1, :], v[0:TOK, :, 1])
                    nc.scalar.copy(vs[GAP:PW, pp, :, 0, :], v[GAP:PW, :, 0])
                    nc.scalar.copy(vx[0:TOK, im, :, 0, :], v[0:TOK, :, 0])
                    nc.scalar.copy(vx[GAP:PW, im1, :, 1, :], v[GAP:PW, :, 1]).then_inc(vs_ready, 1)

                def steps(c, first=False, more=True):
                    for s in range(NU if more else NU + 2):
                        u = c * NU + s
                        for b in range(2):
                            if not first or s >= 2:
                                act.wait_ge(pt_ready, (u - 2) * 2 + b + 1)
                                nc.scalar.copy(pts[0:PW, s % 2, b], p_t[0:PW, 0:4 * PW]).then_inc(pts_ready, 1)
                            if b == 0 and s < NU:
                                act.wait_ge(sub_ready, u + 1)
                                nc.scalar.activation(ex[0:PW, s], ex[0:PW, s], ACT.Exp).then_inc(exp_ready, 1)
                            if b == 0 and s == 0 and not first:
                                gather(c)
                        if s == 0:
                            if more:
                                square(c + 1, 0, 0)
                                square(c + 1, 0, 1)
                            values(c, 0, first)
                            expand(c, 1, first)
                        if more and s == 1:
                            inverse(c + 1, 0)
                            square(c + 1, 1, 0)
                            square(c + 1, 1, 1)
                        if more and s == 2:
                            inverse(c + 1, 1)
                        if s == 3:
                            if more:
                                expand(c + 1, 0)
                            values(c, 1, first)

                gather(0, first=True)
                act.wait_ge(init, 2)
                for j in range(2):
                    for t in range(ET):
                        square(0, j, t)
                    inverse(0, j)
                expand(0, 0, first=True)
                act.wait_ge(fold_ready, 2)
                nc.scalar.copy(K["route"][:], p_o[:].rearrange("p (a b) -> p a b", a=2)[:, :, 0:LEAVES - 1])
                nc.scalar.copy(K["leafo"][:], p_t[:].rearrange("p (a b) -> p a b", a=2)).then_inc(fold_kept, 1)
                steps(0, first=True)
                with act.Fori(1, CH - 1) as i:
                    steps(i)
                steps(CH - 1, more=False)

            @block.vector
            def _(dve):
                def keep_raw(n, j, first=False):
                    for t in range(ET):
                        dve.wait_ge(qk_ready, n * 4 + 2 * j + t + 1)
                        if t == 0 and not first:
                            dve.wait_ge(qn_ready if j else kn_ready, n * 2 if j else n)
                        nc.vector.tensor_copy(raw[:, j, t], p_x[:, 1 - t if j else t, 0:CT]).then_inc(raw_kept, 1)

                def keep_sums(n, j):
                    for t in range(ET):
                        dve.wait_ge(ss_ready, n * 4 + 2 * j + t + 1)
                        nc.vector.tensor_scalar(ss[:, j, t], p_x[:, 1 - t, 0:CT], 1e-24, None, ALU.max).then_inc(ss_kept, 1)

                def normalise_keys(n, first=False):
                    dve.wait_ge(inv_ready, n * 2 + 1)
                    if not first:
                        dve.wait_ge(kx_dve, n * 2)
                        dve.wait_ge(kx_act, n * 2)
                    nc.vector.tensor_tensor(kn[:], raw[:, 0], inv[:, 0], ALU.mult).then_inc(kn_ready, 1)

                def normalise_queries(n, half, first=False):
                    if half == 0:
                        dve.wait_ge(inv_ready, n * 2 + 2)
                    if not first:
                        dve.wait_ge(s_ready, n * NU + 2 * half - 2)
                    part = slice(half * HC, (half + 1) * HC)
                    nc.vector.tensor_tensor(qn[:, :, part], raw[:, 1, :, part], inv[:, 1, :, part],
                                            ALU.mult).then_inc(qn_ready, 1)

                def expand(n, half, first=False):
                    dve.wait_ge(kn_ready, n + 1)
                    if not first:
                        dve.wait_ge(s_ready, n * NU + 2 * half - 2)
                    for t in range(ET):
                        for hh in range(6):
                            last = nc.vector.tensor_scalar(
                                kx[:, t, half * HI:(half + 1) * HI, hh, :],
                                kn[:, t, half * HC:(half + 1) * HC].rearrange("p (a b) -> p a b", b=TOK),
                                K["mask1"][:, hh:hh + 1], None, ALU.mult)
                    last.then_inc(kx_dve, 1)

                def add(c, s):
                    dve.wait_ge(pv_ready, c * NU + s + 1)
                    pair = bass.ds(c * CT + s * 2 * TOK, 2 * TOK)
                    nc.vector.tensor_tensor(h[:, :, pair], h[:, :, pair],
                                            p_o[:, 0:4 * TOK].rearrange("p (a b) -> p a b", a=2),
                                            ALU.add).then_inc(h_done, 1)

                def steps(c, first=False, more=True):
                    for s in range(NU if more else NU + 4):
                        u = c * NU + s
                        if not first:
                            add(c, s - 4)
                        summed = (not first or s >= 1) and s <= NU
                        if summed:
                            dve.wait_ge(exp_ready, u)
                            nc.vector.tensor_reduce(sm[0:PW, (s - 1) % 2], ex[0:PW, (s - 1) % 4], AX.X,
                                                    ALU.add).then_inc(sum_ready, 1)
                        if s < NU:
                            dve.wait_ge(s_ready, u + 1)
                            sc = p_s[0:PW, s % 2, :, 0:BW].rearrange("p a (b c) -> p a b c", c=TOK)
                            nc.vector.tensor_reduce(mx[0:PW, s % 2].rearrange("p (a b) -> p a b", a=2), sc,
                                                    AX.X, ALU.max).then_inc(max_ready, 1)
                        if summed:
                            dve.wait_ge(sum_ready, u)
                            nc.vector.reciprocal(rc[0:PW, (s - 1) % 4], sm[0:PW, (s - 1) % 2]).then_inc(rc_ready, 1)
                        if s < NU:
                            dve.wait_ge(max_ready, u + 1)
                            if not first:
                                dve.wait_ge(p_ready, u - 3)
                            nc.vector.tensor_tensor(
                                ex[0:PW, s].rearrange("p (a b) c -> p a b c", a=2), sc,
                                bc(mx[0:PW, s % 2].rearrange("p (a b) -> p a b", a=2).unsqueeze(3), [PW, 2, HT, TOK]),
                                ALU.subtract).then_inc(sub_ready, 1)
                        if more and s == 0:
                            keep_raw(c + 1, 0)
                        if s == 0:
                            normalise_queries(c, 1, first)
                            expand(c, 1, first)
                        if more and s == 1:
                            keep_sums(c + 1, 0)
                            keep_raw(c + 1, 1)
                        if more and s == 2:
                            normalise_keys(c + 1)
                            keep_sums(c + 1, 1)
                        if more and s == 3:
                            normalise_queries(c + 1, 0)
                            expand(c + 1, 0)

                nc.vector.memset(p_s[32:64], 0.0).then_inc(gap_zero, 1)
                keep_raw(0, 0, first=True)
                keep_sums(0, 0)
                keep_raw(0, 1, first=True)
                normalise_keys(0, first=True)
                keep_sums(0, 1)
                expand(0, 0, first=True)
                normalise_queries(0, 0, first=True)
                steps(0, first=True)
                with dve.Fori(1, CH - 1) as i:
                    steps(i)
                steps(CH - 1, more=False)


def tree_ffn(nc, K, outT):
    h, xn, vec, ident, route, leafo = K["h"], K["xn"], K["vec"], K["ident"], K["route"], K["leafo"]
    NTT = (NT + P - 1) // P
    NN = LEAVES - 1
    with ExitStack() as st:
        def sb(n, shape, dt=F32):
            return st.enter_context(nc.sbuf_tensor(f"tr_{n}", shape, dt))

        def ps(n, shape):
            return st.enter_context(nc.psum_tensor(f"tr_{n}", shape, F32))

        def sem(n):
            return st.enter_context(nc.semaphore(f"tr_{n}"))

        sig = sb("sig", [P, NTT, LEAVES])
        lpa = sb("lpa", [P, NTT, LEAVES])
        lpb = sb("lpb", [P, NTT, LEAVES])
        lpT = sb("lpT", [P, ET, NT])
        y = sb("y", [P, ET, NT])

        p_l = ps("p_l", [P, 2, 512])
        p_t = ps("p_t", [P, 2, 512])
        p_y = ps("p_y", [P, 2, 2, 512])

        logit_ready = sem("logit_ready")
        sig_ready = sem("sig_ready")
        sig_zero = sem("sig_zero")
        level = sem("level")
        lpT_psum = sem("lpT_psum")
        lpT_ready = sem("lpT_ready")
        y_psum = sem("y_psum")
        y_ready = sem("y_ready")
        stored = sem("stored")

        def rows(n):
            return min(P, NT - n * P)

        HALF = [(0, NTT // 2), (NTT // 2, NTT)]

        with nc.Block() as block:
            @block.sync
            def _(sp):
                for c in range(CH):
                    sp.wait_ge(y_ready, c + 1)
                    sp.dma_start(outT[:, :, c * CT:(c + 1) * CT], y[:, :, c * CT:(c + 1) * CT]).then_inc(stored, 16)
                sp.wait_ge(stored, CH * 16)

            @block.gpsimd
            def _(pool):
                nc.gpsimd.memset(sig[:], 0.5).then_inc(sig_zero, 1)

            @block.tensor
            def _(pe):
                for n in range(NTT):
                    if n >= 2:
                        pe.wait_ge(sig_ready, n - 1)
                    r = rows(n)
                    for k in range(ET):
                        last = nc.tensor.matmul(p_l[0:r, n % 2, 0:NN], xn[:, k, n * P:n * P + r], route[:, k, :],
                                                start=(k == 0), stop=(k == ET - 1))
                    last.then_inc(logit_ready, 1)
                c = 0
                for n in range(NTT):
                    if n in (0, NTT // 2):
                        pe.wait_ge(level, 16 if n == 0 else 32)
                    if n >= 2:
                        pe.wait_ge(lpT_ready, n - 1)
                    r = rows(n)
                    for t in range(ET):
                        last = nc.tensor.transpose(p_t[:, n % 2, t * P:t * P + r], lpa[0:r, n, t * P:(t + 1) * P],
                                                   ident[0:r, 0:r])
                    last.then_inc(lpT_psum, 1)
                    while c < CH and (n == NTT // 2 - 1 or n == NTT - 1) and (c + 1) * CT <= n * P + r:
                        pe.wait_ge(lpT_ready, -(-(c + 1) * CT // P))
                        if c >= 2:
                            pe.wait_ge(y_ready, c - 1)
                        for t in range(ET):
                            for k in range(ET):
                                last = nc.tensor.matmul(p_y[:, c % 2, t, 0:CT], leafo[:, k, t * P:(t + 1) * P],
                                                        lpT[:, k, c * CT:(c + 1) * CT], start=(k == 0), stop=(k == ET - 1))
                        last.then_inc(y_psum, 1)
                        c += 1

            @block.scalar
            def _(act):
                nc.scalar.preload_act_table_set("sigmoid_and_others")
                act.wait_ge(sig_zero, 1)
                for n in range(NTT):
                    r = rows(n)
                    act.wait_ge(logit_ready, n + 1)
                    nc.scalar.activation(sig[0:r, n, 0:NN], p_l[0:r, n % 2, 0:NN], ACT.Sigmoid).then_inc(sig_ready, 1)
                for n in range(NTT):
                    r = rows(n)
                    act.wait_ge(lpT_psum, n + 1)
                    nc.scalar.copy(lpT[:, :, n * P:n * P + r],
                                   p_t[:, n % 2, 0:2 * P].rearrange("p (a b) -> p a b", a=2)[:, :, 0:r]).then_inc(lpT_ready, 1)

            @block.vector
            def _(dve):
                done = 0
                for a, b in HALF:
                    dve.wait_ge(sig_ready, b)
                    n = b - a
                    for lv in range(DEPTH):
                        w = 2 ** lv
                        src, dst = (lpb, lpa) if lv % 2 else (lpa, lpb)
                        pair = dst[:, a:b, 0:2 * w].rearrange("p n (c s) -> p n c s", s=2)
                        g = sig[:, a:b, w - 1:2 * w - 1]
                        if lv == 0:
                            nc.vector.tensor_copy(pair[:, :, :, 1], g).then_inc(level, 1)
                            nc.vector.tensor_scalar(pair[:, :, :, 0], g, -1.0, 1.0, ALU.mult, ALU.add).then_inc(level, 1)
                        else:
                            nc.vector.tensor_tensor(pair[:, :, :, 1], src[:, a:b, 0:w], g, ALU.mult).then_inc(level, 1)
                            dve.wait_ge(level, done + 1)
                            nc.vector.tensor_tensor(pair[:, :, :, 0], src[:, a:b, 0:w], pair[:, :, :, 1],
                                                    ALU.subtract).then_inc(level, 1)
                        done += 2
                        dve.wait_ge(level, done)
                for c in range(CH):
                    dve.wait_ge(y_psum, c + 1)
                    cols = slice(c * CT, (c + 1) * CT)
                    for t in range(ET):
                        last = nc.vector.scalar_tensor_tensor(out=y[:, t, cols], in0=p_y[:, c % 2, t, 0:CT],
                                                              scalar=vec[:, V_WB + t:V_WB + t + 1], in1=h[:, t, cols],
                                                              op0=ALU.add, op1=ALU.add)
                    last.then_inc(y_ready, 1)


def tiles(a, k):
    return np.ascontiguousarray(a.reshape(k, P, -1).transpose(1, 0, 2))


def constants():
    c = np.zeros((P, C_END), np.float32)
    c[:, C_ID:C_ID + P] = np.eye(P)
    row = np.arange(P)
    c[:, C_BD:C_BD + P] = (row[:, None] // HD) == (row[None, :] // HD)
    c[:, C_MASK:C_MASK + HT] = (row[:, None] // HD) == np.arange(HT)[None, :]
    inv = (np.float32(1.0) / np.float32(10000.0) ** (np.arange(0, 2 * HD, 2, dtype=np.float32) / np.float32(2 * HD)))
    ang = np.arange(TOK, dtype=np.float32)[None, :] * inv.astype(np.float32)[row % HD][:, None]
    c[:, C_COS:C_COS + TOK] = np.cos(ang)
    c[:, C_SIN:C_SIN + TOK] = np.sin(ang)
    return c


def kernel(**inp):
    import concourse.bacc as bacc
    from concourse.bass_utils import run_bass_kernel_spmd

    a = {k: np.asarray(v) for k, v in inp.items()}
    x = a["x"].reshape(IMGS, 3, 6, 16, 6, 16).transpose(0, 2, 4, 3, 5, 1).reshape(IMGS * PATCH, PD)
    xT = x.T.reshape(PT6, P, CH, CP).transpose(2, 1, 0, 3)

    def vec(v):
        return v.reshape(-1, P).T

    pos = a["L0_tok_pos_emb"][0].T.reshape(ET, P, TOK).transpose(1, 0, 2).reshape(P, ET * TOK)
    vecs = np.concatenate([vec(a["L0_tok_ln1_g"]), vec(a["L0_tok_ln1_b"]), vec(a["L0_tok_b_proj"]),
                           vec(a["L0_tok_ln2_g"]), vec(a["L0_tok_ln2_b"]), vec(a["L0_tok_cls_token"].reshape(-1)),
                           vec(a["L1_ffn_Wout_b"]), pos], axis=1)
    lams = np.concatenate([a["L0_attn_lambda_q1"], a["L0_attn_lambda_q2"],
                           a["L0_attn_lambda_k1"], a["L0_attn_lambda_k2"]]).reshape(1, 64)
    wqkv = a["L0_attn_W_qkv"]
    wv = wqkv[4 * ED:].reshape(2, HT, 2, HD, ED).transpose(2, 1, 0, 3, 4).reshape(2 * ED, ED)
    w1v = a["L1_attn_Wv"].reshape(HT, 2, HD, ED).transpose(1, 0, 2, 3).reshape(ED, ED)
    arrays = {
        "xT": xT, "wtok": tiles(a["L0_tok_W_proj"], PT6), "vecs": vecs, "lams": lams,
        "gsc": a["L1_attn_g_scale"].reshape(1, 1), "cst": constants(),
        "wqkT": tiles(wqkv[:4 * ED].T, ET), "wvT": tiles(wv.T, ET),
        "wprojT": tiles(a["L0_attn_W_proj"].T, 4),
        "w_up": tiles(a["L0_ffn_w_up"], IT).reshape(P, -1), "w_gate": tiles(a["L0_ffn_w_gate"], IT).reshape(P, -1),
        "w_down": tiles(a["L0_ffn_w_down"], ET).reshape(P, -1),
        "w1qkT": tiles(np.concatenate([a["L1_attn_Wq"], a["L1_attn_Wk"]]).T, ET),
        "w1vT": tiles(w1v.T, ET),
        "wq1": tiles(a["L1_ffn_Wq"], ET), "routT": tiles(a["L1_ffn_routers"].T, ET),
        "leafT": tiles(a["L1_ffn_leaf_values"].T, ET), "woutT": tiles(a["L1_ffn_Wout_w"].T, ET),
    }
    arrays = {k: np.ascontiguousarray(v) for k, v in arrays.items()}
    nc = bacc.Bacc("TRN2", target_bir_lowering=False, num_devices=1)
    args = [nc.dram_tensor(k, v.shape, mybir.dt.from_np(v.dtype), kind="ExternalInput").ap() for k, v in arrays.items()]
    out = nc.dram_tensor("outT", (P, ET, NT), F32, kind="ExternalOutput").ap()
    program(nc, *args, out)
    got = run_bass_kernel_spmd(nc, [arrays], core_ids=[0]).results[0]["outT"]
    return np.ascontiguousarray(got.transpose(2, 1, 0).reshape(IMGS, TOK, ED))
```
